# Optimizing a Trainium2 kernel written in Bass

```python
import numpy as np
import jax
import jax.numpy as jnp

def _softmax(x, axis=-1):
    return jax.nn.softmax(x, axis=axis)

def _gelu(x):
    return jax.nn.gelu(x, approximate=True)

def _silu(x):
    return jax.nn.silu(x)

def _sigmoid(x):
    return jax.nn.sigmoid(x)

def _layernorm(x, axis=-1, eps=1e-05):
    m = jnp.mean(x, axis=axis, keepdims=True)
    v = jnp.var(x, axis=axis, keepdims=True)
    return (x - m) / jnp.sqrt(v + eps)

def _scatter_add(tgt, idx, src, axis=0):
    return tgt.at[idx].add(src)

def _segment_sum(src, seg, n):
    return jax.ops.segment_sum(src, seg, n)
kernel_name = 'mk_adaln_d2_jaxref_r4_32494b'

def setup_inputs(seed: int=0):
    np.random.seed(seed)
    _w = jnp.asarray

    def _L0_attn_setup():
        import jax, jax.numpy as jnp
        import numpy as np
        B, T, C = (64, 64, 256)
        N_HEAD, HEAD_SIZE, KV_RANK = (16, 64, 128)
        BLOCK_SIZE = 64
        key = jax.random.key(seed)
        ks = jax.random.split(key, 5)
        HD = N_HEAD * HEAD_SIZE

        def init(k, shape):
            fan_in = shape[0]
            bound = 1.0 / np.sqrt(fan_in)
            return jax.random.uniform(k, shape, jnp.float32, -bound, bound)
        return {'x': jax.random.normal(ks[0], (B, T, C), jnp.float32), 'w_kv_down': init(ks[1], (C, KV_RANK)), 'w_kv_up': init(ks[2], (KV_RANK, 2 * HD)), 'w_q': init(ks[3], (C, HD)), 'w_out': init(ks[4], (HD, C))}
    _L0_attn_in = _L0_attn_setup()

    def _L0_ffn_setup():
        import jax, jax.numpy as jnp
        import numpy as np
        D_MODEL, D_FF, RANK = (256, 1024, 64)
        B, S = (4, 1024)
        key = jax.random.key(seed)
        ks = jax.random.split(key, 7)
        return {'x': jax.random.normal(ks[0], (B, S, D_MODEL), dtype=jnp.float32), 'U1': jax.random.normal(ks[1], (D_MODEL, RANK), dtype=jnp.float32) * 0.02, 'V1': jax.random.normal(ks[2], (RANK, D_FF), dtype=jnp.float32) * 0.02, 'b1': jnp.zeros((D_FF,), dtype=jnp.float32), 'U2': jax.random.normal(ks[3], (D_FF, RANK), dtype=jnp.float32) * 0.02, 'V2': jax.random.normal(ks[4], (RANK, D_MODEL), dtype=jnp.float32) * 0.02, 'b2': jnp.zeros((D_MODEL,), dtype=jnp.float32)}
    _L0_ffn_in = _L0_ffn_setup()
    _L0_c = _w((lambda *s: np.random.randn(*s).astype(np.float32) * 0.05)(4, 256))
    _L0_wmod = _w((lambda *s: np.random.randn(*s).astype(np.float32) * 0.05)(256, 6 * 256) * 256 ** (-0.5))

    def _L1_attn_setup():
        import jax, jax.numpy as jnp
        import numpy as np
        B, S, D, H, MLP = (2, 512, 256, 16, 1024)
        DH = D // H
        EPS_LN = 1e-06
        KERNEL_EPS = 0.001

        def layer_norm(x, scale, bias):
            m = jnp.mean(x, axis=-1, keepdims=True)
            v = jnp.mean(jnp.square(x - m), axis=-1, keepdims=True)
            return (x - m) * jax.lax.rsqrt(v + EPS_LN) * scale + bias

        def performer_causal_attention(q, k, v):
            phi_q = jax.nn.relu(q) + KERNEL_EPS
            phi_k = jax.nn.relu(k) + KERNEL_EPS
            kv = jnp.cumsum(jnp.einsum('bshm,bshd->bshmd', phi_k, v), axis=1)
            num = jnp.einsum('bshm,bshmd->bshd', phi_q, kv)
            den = jnp.einsum('bshm,bshm->bsh', phi_q, jnp.cumsum(phi_k, axis=1))
            return num / den[..., None]
        key = jax.random.key(seed)
        ks = jax.random.split(key, 7)

        def w(k, shape, scale):
            return jax.random.normal(k, shape, jnp.float32) * scale
        s_in = 1.0 / np.sqrt(D)
        return {'inputs': jax.random.normal(ks[0], (B, S, D), jnp.float32), 'ln1_scale': jnp.ones((D,), jnp.float32), 'ln1_bias': jnp.zeros((D,), jnp.float32), 'wq': w(ks[1], (D, H, DH), s_in), 'wk': w(ks[2], (D, H, DH), s_in), 'wv': w(ks[3], (D, H, DH), s_in), 'wo': w(ks[4], (H, DH, D), s_in), 'ln2_scale': jnp.ones((D,), jnp.float32), 'ln2_bias': jnp.zeros((D,), jnp.float32), 'w1': w(ks[5], (D, MLP), s_in), 'b1': jnp.zeros((MLP,), jnp.float32), 'w2': w(ks[6], (MLP, D), 1.0 / np.sqrt(MLP)), 'b2': jnp.zeros((D,), jnp.float32)}
    _L1_attn_in = _L1_attn_setup()

    def _L1_ffn_setup():
        import jax, jax.numpy as jnp
        import numpy as np
        DM, NE, ES, ESZ = (256, 16, 4, 64)
        BATCH, SEQ = (8, 512)
        key = jax.random.key(seed)
        k = jax.random.split(key, 5)
        scale = 0.02
        return {'x': jax.random.normal(k[0], (BATCH, SEQ, DM), dtype=jnp.float32), 'controller': jax.random.normal(k[1], (DM, NE, ES), dtype=jnp.float32) * scale, 'f1': jax.random.normal(k[2], (DM, NE, ES, ESZ), dtype=jnp.float32) * scale, 'f2': jax.random.normal(k[3], (NE, ES, ESZ, DM), dtype=jnp.float32) * scale, 'bias': jax.random.normal(k[4], (NE, ES, ESZ), dtype=jnp.float32) * scale}
    _L1_ffn_in = _L1_ffn_setup()
    _L1_c = _w((lambda *s: np.random.randn(*s).astype(np.float32) * 0.05)(4, 256))
    _L1_wmod = _w((lambda *s: np.random.randn(*s).astype(np.float32) * 0.05)(256, 6 * 256) * 256 ** (-0.5))
    _d = {'L0_attn_x': _L0_attn_in['x'], 'L0_attn_w_kv_down': _L0_attn_in['w_kv_down'], 'L0_attn_w_kv_up': _L0_attn_in['w_kv_up'], 'L0_attn_w_q': _L0_attn_in['w_q'], 'L0_attn_w_out': _L0_attn_in['w_out'], 'L0_ffn_U1': _L0_ffn_in['U1'], 'L0_ffn_V1': _L0_ffn_in['V1'], 'L0_ffn_b1': _L0_ffn_in['b1'], 'L0_ffn_U2': _L0_ffn_in['U2'], 'L0_ffn_V2': _L0_ffn_in['V2'], 'L0_ffn_b2': _L0_ffn_in['b2'], 'L0_c': _L0_c, 'L0_wmod': _L0_wmod, 'L1_attn_ln1_scale': _L1_attn_in['ln1_scale'], 'L1_attn_ln1_bias': _L1_attn_in['ln1_bias'], 'L1_attn_wq': _L1_attn_in['wq'], 'L1_attn_wk': _L1_attn_in['wk'], 'L1_attn_wv': _L1_attn_in['wv'], 'L1_attn_wo': _L1_attn_in['wo'], 'L1_attn_ln2_scale': _L1_attn_in['ln2_scale'], 'L1_attn_ln2_bias': _L1_attn_in['ln2_bias'], 'L1_attn_w1': _L1_attn_in['w1'], 'L1_attn_b1': _L1_attn_in['b1'], 'L1_attn_w2': _L1_attn_in['w2'], 'L1_attn_b2': _L1_attn_in['b2'], 'L1_ffn_controller': _L1_ffn_in['controller'], 'L1_ffn_f1': _L1_ffn_in['f1'], 'L1_ffn_f2': _L1_ffn_in['f2'], 'L1_ffn_bias': _L1_ffn_in['bias'], 'L1_c': _L1_c, 'L1_wmod': _L1_wmod}
    _x0 = _d['L0_attn_x']
    _d['L0_attn_x'] = jax.random.normal(jax.random.fold_in(jax.random.key(seed), 1), (4, 1024, 256), dtype=_x0.dtype)
    del _x0
    return _d

def reference(L0_attn_x, L0_attn_w_kv_down, L0_attn_w_kv_up, L0_attn_w_q, L0_attn_w_out, L0_ffn_U1, L0_ffn_V1, L0_ffn_b1, L0_ffn_U2, L0_ffn_V2, L0_ffn_b2, L0_c, L0_wmod, L1_attn_ln1_scale, L1_attn_ln1_bias, L1_attn_wq, L1_attn_wk, L1_attn_wv, L1_attn_wo, L1_attn_ln2_scale, L1_attn_ln2_bias, L1_attn_w1, L1_attn_b1, L1_attn_w2, L1_attn_b2, L1_ffn_controller, L1_ffn_f1, L1_ffn_f2, L1_ffn_bias, L1_c, L1_wmod):

    def _L0_attn_ref(x, w_kv_down, w_kv_up, w_q, w_out):
        import jax, jax.numpy as jnp
        import numpy as np
        B, T, C = (64, 64, 256)
        N_HEAD, HEAD_SIZE, KV_RANK = (16, 64, 128)
        BLOCK_SIZE = 64
        Bx, Tx, Cx = x.shape
        HD = N_HEAD * HEAD_SIZE
        latent_kv = x @ w_kv_down
        kv = latent_kv @ w_kv_up
        k, v = (kv[..., :HD], kv[..., HD:])
        k = k.reshape(Bx, Tx, N_HEAD, HEAD_SIZE)
        v = v.reshape(Bx, Tx, N_HEAD, HEAD_SIZE)
        q = (x @ w_q).reshape(Bx, Tx, N_HEAD, HEAD_SIZE)
        scale = HEAD_SIZE ** (-0.5)
        att = jnp.einsum('bqhd,bkhd->bhqk', q, k) * scale
        causal = jnp.tril(jnp.ones((Tx, Tx), dtype=bool))
        att = jnp.where(causal, att, -jnp.inf)
        att = jax.nn.softmax(att, axis=-1)
        y = jnp.einsum('bhqk,bkhd->bqhd', att, v)
        y = y.reshape(Bx, Tx, HD)
        return y @ w_out

    def _L0_ffn_ref(x, U1, V1, b1, U2, V2, b2):
        import jax, jax.numpy as jnp
        import numpy as np
        D_MODEL, D_FF, RANK = (256, 1024, 64)
        B, S = (4, 1024)
        P = jnp.einsum('bsd,dr->bsr', x, U1)
        H = jax.nn.gelu(jnp.einsum('bsr,rf->bsf', P, V1) + b1)
        Q = jnp.einsum('bsf,fr->bsr', H, U2)
        return jnp.einsum('bsr,rd->bsd', Q, V2) + b2

    def _L1_attn_ref(inputs, ln1_scale, ln1_bias, wq, wk, wv, wo, ln2_scale, ln2_bias, w1, b1, w2, b2):
        import jax, jax.numpy as jnp
        import numpy as np
        B, S, D, H, MLP = (2, 512, 256, 16, 1024)
        DH = D // H
        EPS_LN = 1e-06
        KERNEL_EPS = 0.001

        def layer_norm(x, scale, bias):
            m = jnp.mean(x, axis=-1, keepdims=True)
            v = jnp.mean(jnp.square(x - m), axis=-1, keepdims=True)
            return (x - m) * jax.lax.rsqrt(v + EPS_LN) * scale + bias

        def performer_causal_attention(q, k, v):
            phi_q = jax.nn.relu(q) + KERNEL_EPS
            phi_k = jax.nn.relu(k) + KERNEL_EPS
            kv = jnp.cumsum(jnp.einsum('bshm,bshd->bshmd', phi_k, v), axis=1)
            num = jnp.einsum('bshm,bshmd->bshd', phi_q, kv)
            den = jnp.einsum('bshm,bshm->bsh', phi_q, jnp.cumsum(phi_k, axis=1))
            return num / den[..., None]
        x = layer_norm(inputs, ln1_scale, ln1_bias)
        q = jnp.einsum('bsd,dhm->bshm', x, wq)
        k = jnp.einsum('bsd,dhm->bshm', x, wk)
        v = jnp.einsum('bsd,dhm->bshm', x, wv)
        attn = performer_causal_attention(q, k, v)
        attn_out = jnp.einsum('bshm,hmd->bsd', attn, wo)
        x = attn_out + inputs
        y = layer_norm(x, ln2_scale, ln2_bias)
        y = jax.nn.gelu(y @ w1 + b1) @ w2 + b2
        return x + y

    def _L1_ffn_ref(x, controller, f1, f2, bias):
        import jax, jax.numpy as jnp
        import numpy as np
        DM, NE, ES, ESZ = (256, 16, 4, 64)
        BATCH, SEQ = (8, 512)
        ne = controller.shape[1]
        d = x.shape[-1]
        grouped = x.reshape(x.shape[:-2] + (-1, ne, d))
        logits = jnp.einsum('...btd,des->...btes', grouped, controller)
        tie = jnp.linspace(0.0, 1e-06, ne, dtype=logits.dtype).reshape(ne, 1, 1)
        logits = logits + tie
        perm = (logits == jnp.max(logits, axis=-3, keepdims=True)).astype(x.dtype)
        sel = jnp.einsum('...btd,...btes->...besd', grouped, perm)
        inner = jax.nn.relu(jnp.einsum('...besd,desf->...besf', sel, f1) + bias)
        inter = jnp.einsum('...besf,esfd->...besd', inner, f2)
        out = jnp.einsum('...besd,...btes->...btd', inter, perm)
        return out.reshape(x.shape)
    x = L0_attn_x
    mod = (_silu(L0_c) @ L0_wmod).reshape(L0_c.shape[0], 6, 1, -1)
    sa, ca, ga, sb, cb, gb = (mod[:, 0], mod[:, 1], mod[:, 2], mod[:, 3], mod[:, 4], mod[:, 5])
    ga = (2 * (ga >= 0) - 1) * jnp.maximum(jnp.abs(ga), 0.25)
    gb = (2 * (gb >= 0) - 1) * jnp.maximum(jnp.abs(gb), 0.25)
    h = _layernorm(x, axis=-1) * (1 + ca) + sa
    x = x + ga * _L0_attn_ref(h, L0_attn_w_kv_down, L0_attn_w_kv_up, L0_attn_w_q, L0_attn_w_out)
    h = _layernorm(x, axis=-1) * (1 + cb) + sb
    x = x + gb * _L0_ffn_ref(h, L0_ffn_U1, L0_ffn_V1, L0_ffn_b1, L0_ffn_U2, L0_ffn_V2, L0_ffn_b2)
    mod = (_silu(L1_c) @ L1_wmod).reshape(L1_c.shape[0], 6, 1, -1)
    sa, ca, ga, sb, cb, gb = (mod[:, 0], mod[:, 1], mod[:, 2], mod[:, 3], mod[:, 4], mod[:, 5])
    ga = (2 * (ga >= 0) - 1) * jnp.maximum(jnp.abs(ga), 0.25)
    gb = (2 * (gb >= 0) - 1) * jnp.maximum(jnp.abs(gb), 0.25)
    h = _layernorm(x, axis=-1) * (1 + ca) + sa
    x = x + ga * _L1_attn_ref(h, L1_attn_ln1_scale, L1_attn_ln1_bias, L1_attn_wq, L1_attn_wk, L1_attn_wv, L1_attn_wo, L1_attn_ln2_scale, L1_attn_ln2_bias, L1_attn_w1, L1_attn_b1, L1_attn_w2, L1_attn_b2)
    h = _layernorm(x, axis=-1) * (1 + cb) + sb
    x = x + gb * _L1_ffn_ref(h, L1_ffn_controller, L1_ffn_f1, L1_ffn_f2, L1_ffn_bias)
    return x

_drawn_inputs = setup_inputs


def setup_inputs(seed=0):
    import zlib

    import numpy as np

    out = dict(_drawn_inputs(seed))
    spreads = {'L0_ffn_b1': (0.0, 0.8),
     'L0_ffn_b2': (0.0, 2.0),
     'L1_attn_ln1_scale': (1.0, 0.6),
     'L1_attn_ln1_bias': (0.0, 2.0),
     'L1_attn_ln2_scale': (1.0, 0.6),
     'L1_attn_ln2_bias': (0.0, 2.0),
     'L1_attn_b1': (0.0, 2.0),
     'L1_attn_b2': (0.0, 2.0)}
    factors = {'L0_attn_w_kv_down': 8.0,
     'L0_attn_w_kv_up': 8.0,
     'L0_attn_w_q': 8.0,
     'L0_attn_w_out': 8.0,
     'L0_ffn_U1': 8.0,
     'L0_ffn_V1': 8.0,
     'L0_ffn_U2': 8.0,
     'L0_ffn_V2': 8.0,
     'L1_attn_wq': 28.52,
     'L1_attn_wk': 23.368,
     'L1_ffn_controller': 21.145,
     'L1_ffn_f1': 29.36,
     'L1_ffn_f2': 19.972,
     'L1_ffn_bias': 64.0,
     'L1_attn_wv': 8.0,
     'L1_attn_wo': 8.0,
     'L1_attn_w1': 8.0,
     'L1_attn_w2': 7.04,
     'L1_c': 3.536,
     'L1_wmod': 3.32}
    for name, (base, spread) in spreads.items():
        noise = np.random.default_rng([zlib.crc32(name.encode()), seed]).standard_normal(out[name].shape)
        drawn = base * np.exp(spread * noise) if base else spread * noise
        out[name] = jnp.asarray(drawn.astype(out[name].dtype))
    for name, factor in factors.items():
        out[name] = (out[name] * factor).astype(out[name].dtype)
    return out
```

```python
import numpy as np
import concourse.bass as bass
from concourse import mybir
from contextlib import ExitStack

F32 = mybir.dt.float32
BF16 = mybir.dt.bfloat16
ACT = mybir.ActivationFunctionType
ALU = mybir.AluOpType
AX_X = mybir.AxisListType.X

P = 128
NB = 4
S = 1024
D = 256
C = D // P
T = S // P
NH = 2
HW = S // NH
TH = T // NH
HD0 = 64
HEADS0 = 16
PAIRS = HEADS0 // 2
RK = 128
FF = 1024
FM = FF // P
RF = 64
U = 2 * T
EPS = 1e-5
HEADS1 = 16
HD1 = 16
HC = HEADS1 // C
VW = HD1 + 1
EPS_LN = 1e-6
EPS_PHI = 1e-3
NE = 16
ES = 64
EF = 64
G = S // NE
GT = P // NE
EP = ES // 2
NEG = -1e30


class Lane:

    def __init__(self, sem):
        self.sem, self.steps = sem, []

    def do(self, emit, *after):
        step = Step(self, emit, [a for a in after if a is not None])
        self.steps.append(step)
        return step

    def number(self):
        n = 0
        for s in self.steps:
            if s.needed:
                n += 1
                s.value = n

    def emit(self, engine):
        seen = {}
        for s in self.steps:
            for a in s.after:
                sem, value = (a.lane.sem, a.value) if isinstance(a, Step) else a
                if seen.get(sem.name, 0) < value:
                    engine.wait_ge(sem, value)
                    seen[sem.name] = value
            last = s.emit(engine)
            if s.needed:
                last.then_inc(self.sem, 1)


class Step:
    def __init__(self, lane, emit, after):
        self.lane, self.emit, self.after = lane, emit, after
        self.needed, self.value = False, 0
        for a in after:
            if isinstance(a, Step):
                a.needed = True


class Banks:

    def __init__(self, tiles):
        self.tiles, self.readers, self.at = tiles, [None] * len(tiles), -1

    def take(self):
        self.at = (self.at + 1) % len(self.tiles)
        return self.at, self.tiles[self.at], self.readers[self.at]

    def read_by(self, index, step):
        self.readers[index] = step


def build(nc, I, out):
    ctx = ExitStack()
    ctx.enter_context(nc.allow_non_contiguous_dma(reason="bias columns and broadcast rows"))

    def sb(name, shape, dt=F32):
        return ctx.enter_context(nc.sbuf_tensor(name, shape, dt))

    def semaphore(name):
        return ctx.enter_context(nc.semaphore(name))

    bank = [ctx.enter_context(nc.psum_tensor(f"bank{i}", [P, 512], F32)) for i in range(4)]
    score_tiles = [ctx.enter_context(nc.psum_tensor(f"scores{i}", [P, 2, 512], F32)) for i in range(2)]
    all_banks = [b[:, :] for b in bank] + [s[:, i, :] for s in score_tiles for i in range(2)]

    wout = sb("wout", [P, PAIRS, D])
    u1, v1 = sb("u1", [P, C, RF]), sb("v1", [RF, FF])
    u2, v2 = sb("u2", [P, FM, RF]), sb("v2", [RF, D])
    wdown = sb("wdown", [P, C, RK])
    wq1, wkv1, wo1 = sb("wq1", [P, C, D]), sb("wkv1", [P, C, 2 * D]), sb("wo1", [P, C, D])
    w1, w2 = sb("w1", [P, C, FF]), sb("w2", [P, FM, D])
    ctrl = sb("ctrl", [P, C, 2 * ES])
    f1 = sb("f1", [P, C, ES, EF])
    b1_0, b1_1 = sb("b1_0", [P, FM]), sb("b1_1", [P, FM])
    b2_0, b2_1 = sb("b2_0", [P, D]), sb("b2_1", [P, D])
    ln_cols = sb("ln_cols", [P, 4, C])
    fbias = sb("fbias", [P, EP])
    tie = sb("tie", [P, NE])
    ident = sb("ident", [P, P])
    ident_b = sb("ident_b", [P, P], BF16)
    neg_b = sb("neg_b", [P, P], BF16)
    tril = sb("tril", [P, P])
    head_mask = sb("head_mask", [P, HC])
    kv_mask = sb("kv_mask", [P, HC, VW])
    half_mask = sb("half_mask", [P, 2])
    minus_half = sb("minus_half", [P, T])
    x = sb("x", [P, T, D])
    h = sb("h", [P, T, D])
    xn = sb("xn", [P, T, D])
    mod_rows = sb("mod_rows", [P, 8, D])
    mod_cols = sb("mod_cols", [P, 4, C])
    tmp = sb("tmp", [P, 4, D])
    stats = sb("stats", [P, T, 6])
    mv = sb("mv", [P, T, 2])
    rstd = sb("rstd", [P, T])
    neg_max = sb("neg_max", [P, 4])
    row_sum = sb("row_sum", [P, 8])
    rec = sb("rec", [P, HEADS1])
    logit_max = sb("logit_max", [P, G])
    kv_state = sb("kv_state", [P, C, HC * VW])

    used = [0]
    overlay = sb("overlay", [P, 8192])
    ROOM = 2 * S + S + 2 * S + 2 * S + 2 * S + 2 * S + 2 * S + S + 1024
    room = sb("room", [P, ROOM])

    def places():
        used[0] = 0

    def part(words, text=None, **kw):
        a = room[:, used[0]:used[0] + words]
        used[0] += words
        if used[0] > ROOM:
            raise ValueError("the work space is too small")
        return a.rearrange(text, **kw) if text else a

    lane = {k: Lane(semaphore(f"{k}_steps")) for k in ("pe", "act", "dve", "pool", "sp")}
    pe, act, dve, pool, sp = (lane[k] for k in ("pe", "act", "dve", "pool", "sp"))
    setup = {k: Lane(semaphore(f"{k}_setup")) for k in ("pe", "act", "dve", "pool", "sp")}
    loaded = {k: semaphore(f"loaded_{k}") for k in ("weights", "cond", "mod", "x", "rows", "f2", "w0", "w1")}
    stored_mod, stored = semaphore("stored_mod"), semaphore("stored")
    flow = {k: semaphore(k) for k in (
        "scores_done", "max_done", "exp_done", "turned_low", "turned_high", "copied_low", "copied_high",
        "values_done", "inverted", "normed", "job_done", "job_read")}
    names = ("pe", "act", "dve", "pool", "sp")

    mod_dram = nc.dram_tensor("mod_scratch", [NB, 2, 6, D], F32, kind="Internal").ap()

    places()
    cond = part(2 * C * NB, "p (l c b) -> p l c b", l=2, c=C)
    silu = part(2 * C * NB, "p (l c b) -> p l c b", l=2, c=C)
    wmod = [part(C * 6 * D, "p (c n) -> p c n", c=C) for _ in range(2)]
    mod_sb = part(2 * 6 * D, "p (l s n) -> p l s n", l=2, s=6)
    gate_a, gate_s = xn[:, 0:2, :], xn[:, 2:4, :]

    weight_loads = []

    def load(dst, src):
        weight_loads.append((dst, src))

    def rows(w, p=P):
        return w.rearrange("(c p) n -> p c n", p=p)

    load(wdown[:, :, :], rows(I["L0_attn_w_kv_down"]))
    load(wout[:, :, :], rows(I["L0_attn_w_out"]))
    load(u1[:, :, :], rows(I["L0_ffn_U1"]))
    load(v1[:, :], I["L0_ffn_V1"])
    load(u2[:, :, :], rows(I["L0_ffn_U2"]))
    load(v2[:, :], I["L0_ffn_V2"])
    load(wq1[:, :, :], rows(I["L1_attn_wq"].rearrange("d h m -> d (h m)")))
    load(wkv1[:, :, 0:D], rows(I["L1_attn_wk"].rearrange("d h m -> d (h m)")))
    load(wkv1[:, :, D:2 * D], rows(I["L1_attn_wv"].rearrange("d h m -> d (h m)")))
    load(wo1[:, :, :], rows(I["L1_attn_wo"].rearrange("h m d -> (h m) d")))
    load(w1[:, :, :], rows(I["L1_attn_w1"]))
    load(w2[:, :, :], rows(I["L1_attn_w2"]))
    for k in range(2):
        load(ctrl[:, :, k * ES:(k + 1) * ES], rows(I["L1_ffn_controller"].rearrange("d e s -> d (e s)")))
    load(b1_0[:, :], I["L0_ffn_b1"].rearrange("(m p) -> p m", p=P))
    load(b1_1[:, :], I["L1_attn_b1"].rearrange("(m p) -> p m", p=P))
    load(b2_0[:, :], I["L0_ffn_b2"].partition_broadcast(P))
    load(b2_1[:, :], I["L1_attn_b2"].partition_broadcast(P))
    for k, name in enumerate(("ln1_scale", "ln1_bias", "ln2_scale", "ln2_bias")):
        load(ln_cols[:, k, :], I["L1_attn_" + name].rearrange("(c p) -> p c", p=P))
    slots = I["L1_ffn_bias"].rearrange("e s f -> (e s) f").rearrange("(q two) f -> two f q", two=2)
    for k in range(2):
        load(fbias[k * EF:(k + 1) * EF, :], slots[k])
    load(tie[:, :], I["tie"].partition_broadcast(P))
    for c in range(C):
        load(f1[:, c, :, :], I["L1_ffn_f1"].rearrange("(c p) e s f -> c p (e s) f", p=P)[c])
    cond_loads = [(cond[:, l, c, :], I[f"L{l}_c"].rearrange("b (c p) -> c p b", p=P)[c]) for l in range(2) for c in range(C)]
    cond_loads += [(wmod[l], rows(I[f"L{l}_wmod"])) for l in range(2)]

    s_act, s_dve, s_pe, s_pool = setup["act"], setup["dve"], setup["pe"], setup["pool"]
    silu_done = s_act.do(lambda e: nc.scalar.activation(silu, cond, ACT.Silu), (loaded["cond"], 16 * len(cond_loads)))
    mod_copied = []
    for l in range(2):
        for n in range(3):
            ps = all_banks[3 * l + n][0:NB, :]

            def mod_matmul(e, ps=ps, l=l, n=n):
                for c in range(C):
                    last = nc.tensor.matmul(ps, silu[:, l, c, :], wmod[l][:, c, n * 512:(n + 1) * 512],
                                            start=c == 0, stop=c == C - 1)
                return last

            done = s_pe.do(mod_matmul, silu_done)
            mod_copied.append(s_dve.do(
                lambda e, ps=ps, l=l, n=n: nc.vector.tensor_copy(
                    mod_sb[0:NB, l, 2 * n:2 * n + 2, :].rearrange("b s n -> b (s n)"), ps), done))
    last = mod_copied[-1]
    mod_done = []
    for l in range(2):
        scales = mod_sb[0:NB, l, 1:6:3, :]
        gates = mod_sb[0:NB, l, 2:6:3, :]
        ga_, gs_ = gate_a[0:NB], gate_s[0:NB]
        mod_done.append(s_dve.do(lambda e, a=scales: nc.vector.tensor_scalar(a, a, 1.0, None, op0=ALU.add), last))
        size = s_dve.do(lambda e, a=gates, o=ga_: nc.vector.scalar_tensor_tensor(
            o, a, -1.0, a, op0=ALU.mult, op1=ALU.max), last, mod_done[-1])
        size = s_dve.do(lambda e, o=ga_: nc.vector.tensor_scalar(o, o, 0.25, None, op0=ALU.max), size)
        sign = s_dve.do(lambda e, a=gates, o=gs_: nc.vector.tensor_scalar(o, a, 0.0, 2.0, op0=ALU.is_ge, op1=ALU.mult),
                        size)
        last = s_dve.do(lambda e, a=gates, s=gs_, g=ga_: nc.vector.scalar_tensor_tensor(
            a, s, -1.0, g, op0=ALU.add, op1=ALU.mult), sign)
        mod_done.append(last)

    def fill(ap, value):
        return s_pool.do(lambda e: nc.gpsimd.memset(ap, value))

    def select(ap, pattern, base, mult, op, value, *after):
        return s_pool.do(lambda e: nc.gpsimd.affine_select(
            out=ap, in_=ap, compare_op=op, fill=value, base=base, pattern=pattern, channel_multiplier=mult), *after)

    ident_done = select(ident[:, :], [[-1, P]], 0, 1, ALU.not_equal, 1.0, fill(ident[:, :], 0.0))
    s_dve.do(lambda e: nc.vector.tensor_copy(ident_b[:, :], ident[:, :]), ident_done)
    select(neg_b[:, :], [[-1, P]], 0, 1, ALU.is_ge, NEG, fill(neg_b[:, :], 0.0))
    select(tril[:, :], [[1, P]], 0, -1, ALU.is_ge, 0.0, fill(tril[:, :], 1.0))
    for ap, extra in ((head_mask[:, :], []), (kv_mask[:, :, :], [[0, VW]])):
        first = select(ap, [[-HD1, HC]] + extra, 0, 1, ALU.is_ge, 0.0, fill(ap, 1.0))
        select(ap, [[HD1, HC]] + extra, HD1 - 1, -1, ALU.is_ge, 0.0, first)
    first = select(half_mask[:, :], [[-ES, 2]], 0, 1, ALU.is_ge, 0.0, fill(half_mask[:, :], 1.0))
    select(half_mask[:, :], [[ES, 2]], ES - 1, -1, ALU.is_ge, 0.0, first)
    fill(minus_half[:, :], -0.5)

    def setup_sp(e):
        for dst, src in cond_loads:
            e.dma_start(dst, src).then_inc(loaded["cond"], 16)
        for dst, src in weight_loads:
            e.dma_start(dst, src).then_inc(loaded["weights"], 16)
        for m in mod_done:
            e.wait_ge(m.lane.sem, m.value)
        e.dma_start(mod_dram.rearrange("b l s n -> b l (s n)"),
                    mod_sb[0:NB, :, :, :].rearrange("b l s n -> b l (s n)")).then_inc(stored_mod, 16)
        e.wait_ge(stored_mod, 16)
        e.wait_ge(loaded["weights"], 16 * len(weight_loads))

    for m in mod_done:
        m.needed = True
    for s in setup.values():
        s.number()
    with nc.Block() as block:
        block.sync(setup_sp)
        block.scalar(setup["act"].emit)
        block.vector(setup["dve"].emit)
        block.tensor(setup["pe"].emit)
        block.gpsimd(setup["pool"].emit)

    banks = Banks(all_banks)
    x_in = I["L0_attn_x"].rearrange("b (t p) d -> b p t d", p=P)
    x_out = out.rearrange("b (t p) d -> b p t d", p=P)
    b_reg = {}

    def load_batch(e):
        b = b_reg["b"]
        for half in range(NH):
            ts = slice(half * TH, (half + 1) * TH)
            e.dma_start(x[:, ts, :], x_in[b][:, ts, :]).then_inc(loaded["x"], 16)
        for k, s in enumerate((0, 1, 3, 4)):
            e.dma_start(mod_cols[:, k, :], mod_dram[b, 0, s].rearrange("(c p) -> p c", p=P)).then_inc(loaded["rows"], 16)
        for k, s in enumerate((2, 5)):
            e.dma_start(mod_rows[:, k, :], mod_dram[b, 0, s].partition_broadcast(P)).then_inc(loaded["rows"], 16)
        return e.dma_start(mod_rows[:, 2:8, :].rearrange("p s n -> p (s n)"),
                           mod_dram[b, 1].rearrange("s n -> (s n)").partition_broadcast(P)).then_inc(loaded["rows"], 16)

    X_HALF = [(loaded["x"], 32), (loaded["x"], 32)]
    ROWS = (loaded["rows"], 16 * 7)

    def normalise(src, ready, eps):
        normed = []
        for half in range(NH):
            last = None
            for t in range(half * TH, (half + 1) * TH):
                s = dve.do(lambda e, t=t: nc.vector.bn_stats(stats[:, t, :], src[:, t, :]), ready[t])
                last = dve.do(lambda e, t=t: nc.vector.bn_aggr(mv[:, t, :], stats[:, t, :]), s)
            ts = slice(half * TH, (half + 1) * TH)
            var = pool.do(lambda e, ts=ts: nc.gpsimd.tensor_scalar(rstd[:, ts], mv[:, ts, 1], eps, None, op0=ALU.add), last)
            inv = pool.do(lambda e, ts=ts: nc.gpsimd.tensor_tensor(rstd[:, ts], rstd[:, ts], minus_half[:, ts], op=ALU.pow), var)
            for t in range(half * TH, (half + 1) * TH):
                normed.append(dve.do(lambda e, t=t: nc.vector.tensor_scalar(
                    xn[:, t, :], src[:, t, :], mv[:, t, 0:1], rstd[:, t:t + 1], op0=ALU.subtract, op1=ALU.mult), inv))
        return normed

    def turn(src, ready, dst, scale=None, bias=None, engine="act", after=None):
        wrote = []
        for half in range(NH):
            for c in range(C):
                i, ps, reader = banks.take()

                def transposes(e, half=half, c=c, ps=ps):
                    for t in range(TH):
                        last = nc.tensor.transpose(ps[:, t * P:(t + 1) * P], src[:, half * TH + t, c * P:(c + 1) * P],
                                                   ident[:, :])
                    return last

                done = pe.do(transposes, *ready[half * TH:(half + 1) * TH], reader)
                o = dst[:, c, half * HW:(half + 1) * HW]
                if scale is None:
                    copy = act.do(lambda e, o=o, ps=ps: nc.scalar.copy(o, ps), done, after)
                else:
                    copy = act.do(lambda e, o=o, ps=ps, c=c: nc.scalar.activation(
                        o, ps, ACT.Identity, bias=bias[:, c:c + 1], scale=scale[:, c:c + 1]), done, after)
                banks.read_by(i, copy)
            wrote.append(copy)
        return wrote

    def product(ps, pieces):
        def emit(e):
            for n, (w, m) in enumerate(pieces):
                last = nc.tensor.matmul(ps, w, m, start=n == 0, stop=n == len(pieces) - 1)
            return last
        return emit

    sp.do(lambda e: load_batch(e))
    places()
    hT = part(C * S, "p (c s) -> p c s", c=C)
    latT = part(S)
    q_t = [part(S) for _ in range(2)]
    k_t = [part(S) for _ in range(2)]
    v_t = [part(T * P, "p (t n) -> p t n", t=T) for _ in range(2)]
    prob = [part(S) for _ in range(2)]
    probT = [part(S) for _ in range(2)]
    y_t = part(T * P, "p (t n) -> p t n", t=T)
    w_ring = [part(4 * P) for _ in range(2)]
    yT = overlay[:, :].rearrange("p (j s) -> p j s", j=PAIRS)

    wq_dram = I["L0_attn_w_q"].rearrange("(c p) n -> p c n", p=P)
    wkv_dram = I["L0_attn_w_kv_up"]

    def load_pair(e, buf, col, sem):
        dst = w_ring[buf]
        e.dma_start(dst[:, 0:2 * P].rearrange("p (c n) -> p c n", c=C), wq_dram[:, :, bass.ds(col, P)]).then_inc(sem, 16)
        e.dma_start(dst[:, 2 * P:3 * P], wkv_dram[:, bass.ds(col, P)]).then_inc(sem, 16)
        return e.dma_start(dst[:, 3 * P:4 * P], wkv_dram[:, bass.ds(col + HEADS0 * HD0, P)]).then_inc(sem, 16)

    PAIR_DMA = 3 * 16
    JOBS = 8
    FIRST_JOBS = 6
    BODY = 2 * U
    TURNS = PAIRS // 2
    HIGH = T // 2

    normed = normalise(x, [X_HALF[t // TH] for t in range(T)], EPS)
    hT_done = turn(xn, normed, hT, scale=mod_cols[:, 1, :], bias=mod_cols[:, 0, :], after=ROWS)
    lat_done = []
    for half in range(NH):
        i, ps, reader = banks.take()
        cols = slice(half * HW, (half + 1) * HW)
        done = pe.do(product(ps, [(wdown[:, c, :], hT[:, c, cols]) for c in range(C)]), hT_done[half], reader)
        copy = act.do(lambda e, ps=ps, cols=cols: nc.scalar.copy(latT[:, cols], ps), done)
        banks.read_by(i, copy)
        lat_done.append(copy)
    before_pairs = [r for r in banks.readers if r is not None]

    turned_bank = [bank[0], bank[1]]
    value_bank, job_bank = bank[2], bank[3]

    def unit(u):
        return (u // U) % 2, (u % U) // 2, u % 2, u % 2

    def high_before(u):
        return (u // U) * 2 * HIGH + max(0, u % U - 2 * HIGH)

    def pe_job(e, n, kind, buf):
        half = int(kind[1])
        cols = slice(half * HW, (half + 1) * HW)
        e.wait_ge(flow["job_read"], n)
        wq, wk, wv = (w_ring[buf][:, k * P:(k + 1) * P] for k in (0, 2, 3))
        if kind[0] == "q":
            for c in range(C):
                last = nc.tensor.matmul(job_bank[:, :], w_ring[buf][:, c * P:(c + 1) * P], hT[:, c, cols],
                                        start=c == 0, stop=c == C - 1)
        elif kind[0] == "k":
            last = nc.tensor.matmul(job_bank[:, :], wk, latT[:, cols], start=True, stop=True)
        elif kind[0] == "v":
            for t in range(TH):
                tile = half * TH + t
                last = nc.tensor.matmul(job_bank[:, t * P:(t + 1) * P], latT[:, tile * P:(tile + 1) * P], wv,
                                        start=True, stop=True)
        else:
            for t in range(TH):
                last = nc.tensor.transpose(job_bank[:, t * P:(t + 1) * P], y_t[:, half * TH + t, :], ident[:, :])
        last.then_inc(flow["job_done"], 1)

    def act_job(e, n, kind, buf, pair):
        half = int(kind[1])
        cols = slice(half * HW, (half + 1) * HW)
        e.wait_ge(flow["job_done"], n + 1)
        if kind[0] == "q":
            last = nc.scalar.mul(q_t[buf][:, cols], job_bank[:, :], HD0 ** -0.5)
        elif kind[0] == "k":
            last = nc.scalar.copy(k_t[buf][:, cols], job_bank[:, :])
        elif kind[0] == "v":
            last = nc.scalar.copy(v_t[buf][:, half * TH:(half + 1) * TH, :],
                                  job_bank[:, :].rearrange("p (t n) -> p t n", t=TH))
        else:
            last = nc.scalar.copy(yT[:, bass.ds(pair, 1), cols],
                                  job_bank[:, :].rearrange("p (o n) -> p o n", o=1))
        last.then_inc(flow["job_read"], 1)

    SCHEDULE = {1: "q0", 3: "q1", 5: "k0", 7: "k1", 10: "Y0", 11: "v0", 13: "v1"}

    def jobs_at(u, tail):
        w, k = u // U, u % U
        if k not in SCHEDULE:
            return None
        kind = SCHEDULE[k]
        if tail and w == 1 and kind != "Y0":
            return None
        order = sorted(SCHEDULE)
        n = w * JOBS + order.index(k)
        if tail and w == 1:
            n = w * JOBS
        return n, kind, (w if kind[0] == "Y" else 1 - w)

    def y1_number(w, tail):
        return w * JOBS + (1 if tail and w == 1 else JOBS - 1)

    def pe_pairs(e):
        def scores(u, g):
            buf, i, head, par = unit(u)
            rows_ = slice(head * HD0, (head + 1) * HD0)
            width = (i + 1) * P
            flat = score_tiles[par][:, :, :].rearrange("p a n -> p (a n)")
            qs = q_t[buf][rows_, i * P:(i + 1) * P]
            for seg in range(0, width, 512):
                end = min(width, seg + 512)
                nc.tensor.matmul(flat[:, seg:end], qs, k_t[buf][rows_, seg:end], start=True, stop=end < width)
            nc.tensor.matmul(flat[:, i * P:width], ident_b[:, :], neg_b[:, :], start=False, stop=True
                             ).then_inc(flow["scores_done"], 1)

        def turn_probs(u, g, high):
            _, i, _, par = unit(u)
            e.wait_ge(flow["exp_done"], g + 1)
            e.wait_ge(flow["copied_low"], g)
            for j in range(min(4, i + 1)):
                last = nc.tensor.transpose(turned_bank[0][:, j * P:(j + 1) * P], prob[par][:, j * P:(j + 1) * P],
                                           ident[:, :])
            last.then_inc(flow["turned_low"], 1)
            if i >= 4:
                e.wait_ge(flow["copied_high"], high)
                for j in range(4, i + 1):
                    last = nc.tensor.transpose(turned_bank[1][:, (j - 4) * P:(j - 3) * P],
                                               prob[par][:, j * P:(j + 1) * P], ident[:, :])
                last.then_inc(flow["turned_high"], 1)

        def values(u, g, high, tiles_normed):
            buf, i, head, par = unit(u)
            e.wait_ge(flow["copied_low"], g + 1)
            if i >= 4:
                e.wait_ge(flow["copied_high"], high + 1)
            if head == 0:
                e.wait_ge(flow["normed"], tiles_normed)
            o = value_bank[:, head * HD0:(head + 1) * HD0]
            for j in range(i + 1):
                last = nc.tensor.matmul(o, probT[par][:, j * P:(j + 1) * P],
                                        v_t[buf][:, j, head * HD0:(head + 1) * HD0], start=j == 0, stop=j == i)
            last.then_inc(flow["values_done"], 1)

        def body(n, tail):
            g0 = e.snap(n * BODY) if not isinstance(n, int) else n * BODY
            hi0 = n * (4 * HIGH)
            j0 = n * (2 * JOBS) + FIRST_JOBS
            for u in range(BODY):
                turn_probs(u, g0 + u, hi0 + high_before(u))
                if u + 2 < BODY or not tail:
                    if u + 2 == U:
                        e.wait_ge(flow["job_read"], j0 + 4)
                    if u + 2 == BODY:
                        e.wait_ge(flow["job_read"], j0 + JOBS + 4)
                    scores((u + 2) % BODY, None)
                if u % U == 1:
                    e.wait_ge(flow["job_read"], j0 if u == 1 else j0 + JOBS - 1)
                if u > 0:
                    values(u - 1, g0 + u - 1, hi0 + high_before(u - 1), n * (BODY // 2) + (u - 1) // 2)
                if u == U:
                    e.wait_ge(flow["normed"], n * (BODY // 2) + T)
                    pe_job(e, j0 + y1_number(0, tail), "Y1", 0)
                job = jobs_at(u, tail)
                if job:
                    k, kind, buf = job
                    if kind == "Y0":
                        e.wait_ge(flow["normed"], n * (BODY // 2) + (u // U) * T + TH)
                    if kind == "q0":
                        if u // U == 0:
                            e.wait_ge(loaded["w1"], n * PAIR_DMA + PAIR_DMA)
                        else:
                            e.wait_ge(loaded["w0"], n * PAIR_DMA + 2 * PAIR_DMA)
                    pe_job(e, j0 + k, kind, buf)
            values(BODY - 1, g0 + BODY - 1, hi0 + high_before(BODY - 1), n * (BODY // 2) + T * 2 - 1)
            e.wait_ge(flow["normed"], n * (BODY // 2) + 2 * T)
            pe_job(e, j0 + y1_number(1, tail), "Y1", 1)

        e.wait_ge(loaded["w0"], PAIR_DMA)
        for n, kind in enumerate(("q0", "q1", "k0", "k1", "v0", "v1")):
            pe_job(e, n, kind, 0)
        e.wait_ge(flow["job_read"], 4)
        scores(0, 0)
        scores(1, 1)
        with e.Fori(0, TURNS - 1) as n:
            body(n, False)
        body(TURNS - 1, True)

    def dve_pairs(e):
        def maximum(u, g):
            _, i, _, par = unit(u)
            flat = score_tiles[par][:, :, :].rearrange("p a n -> p (a n)")
            e.wait_ge(flow["scores_done"], g + 1)
            nc.vector.tensor_reduce(neg_max[:, u % 4:u % 4 + 1], flat[:, 0:(i + 1) * P], axis=AX_X, op=ALU.max,
                                    negate=True).then_inc(flow["max_done"], 1)

        def copy_low(u, g):
            _, i, _, par = unit(u)
            w = min(4, i + 1) * P
            e.wait_ge(flow["turned_low"], g + 1)
            nc.vector.tensor_copy(probT[par][:, 0:w], turned_bank[0][:, 0:w]).then_inc(flow["copied_low"], 1)

        def norm(u, g, tiles):
            _, i, _, _ = unit(u)
            k = (u - 1) % 8
            e.wait_ge(flow["exp_done"], g + 1)
            nc.vector.reciprocal(rec[:, k:k + 2], row_sum[:, k:k + 2]).then_inc(flow["inverted"], 1)
            e.wait_ge(flow["values_done"], g + 1)
            e.wait_ge(flow["inverted"], tiles)
            nc.vector.tensor_tensor(y_t[:, i, :].rearrange("p (a n) -> p a n", a=2),
                                    value_bank[:, 0:P].rearrange("p (a n) -> p a n", a=2),
                                    rec[:, k:k + 2].unsqueeze(2).to_broadcast([P, 2, HD0]),
                                    op=ALU.mult).then_inc(flow["normed"], 1)

        def body(n, tail):
            g0 = e.snap(n * BODY) if not isinstance(n, int) else n * BODY
            for u in range(BODY):
                copy_low(u, g0 + u)
                if u + 2 < BODY or not tail:
                    maximum((u + 2) % BODY, g0 + u + 2)
                if u % 2 == 0 and u > 0:
                    norm(u - 1, g0 + u - 1, n * (BODY // 2) + u // 2)
            norm(BODY - 1, g0 + BODY - 1, n * (BODY // 2) + BODY // 2)

        maximum(0, 0)
        maximum(1, 1)
        with e.Fori(0, TURNS - 1) as n:
            body(n, False)
        body(TURNS - 1, True)


    def act_pairs(e):
        def exponential(u, g):
            _, i, _, par = unit(u)
            w = (i + 1) * P
            flat = score_tiles[par][:, :, :].rearrange("p a n -> p (a n)")
            e.wait_ge(flow["max_done"], g + 1)
            nc.scalar.activation(prob[par][:, 0:w], flat[:, 0:w], ACT.Exp, bias=neg_max[:, u % 4:u % 4 + 1],
                                 accum_out=row_sum[:, u % 8:u % 8 + 1]).then_inc(flow["exp_done"], 1)

        def copy_high(u, high):
            _, i, _, par = unit(u)
            w = (i - 3) * P
            e.wait_ge(flow["turned_high"], high + 1)
            nc.scalar.copy(probT[par][:, 4 * P:4 * P + w], turned_bank[1][:, 0:w]).then_inc(flow["copied_high"], 1)

        def body(n, tail):
            g0 = e.snap(n * BODY) if not isinstance(n, int) else n * BODY
            hi0 = n * (4 * HIGH)
            j0 = n * (2 * JOBS) + FIRST_JOBS
            for u in range(BODY):
                if unit(u)[1] >= 4:
                    copy_high(u, hi0 + high_before(u))
                if u + 2 < BODY or not tail:
                    exponential((u + 2) % BODY, g0 + u + 2)
                if u == U:
                    act_job(e, j0 + y1_number(0, tail), "Y1", 0, n * 2)
                job = jobs_at(u, tail)
                if job:
                    k, kind, buf = job
                    act_job(e, j0 + k, kind, buf, n * 2 + u // U)
            act_job(e, j0 + y1_number(1, tail), "Y1", 1, n * 2 + 1)

        for n, kind in enumerate(("q0", "q1", "k0", "k1", "v0", "v1")):
            act_job(e, n, kind, 0, 0)
        exponential(0, 0)
        exponential(1, 1)
        with e.Fori(0, TURNS - 1) as n:
            body(n, False)
        body(TURNS - 1, True)

    def sp_pairs(e):
        load_pair(e, 0, 0, loaded["w0"])
        load_pair(e, 1, P, loaded["w1"])
        with e.Fori(0, TURNS - 1) as n:
            even, odd = e.snap(n * 2 * P + 2 * P), e.snap(n * 2 * P + 3 * P)
            e.wait_ge(flow["job_done"], n * (2 * JOBS) + FIRST_JOBS)
            load_pair(e, 0, even, loaded["w0"])
            e.wait_ge(flow["job_done"], n * (2 * JOBS) + FIRST_JOBS + JOBS - 1)
            load_pair(e, 1, odd, loaded["w1"])

    JOBS_ALL = FIRST_JOBS + (TURNS - 1) * 2 * JOBS + JOBS + 2
    UNITS_ALL = TURNS * BODY
    PAIRS_DONE = [(flow["job_read"], JOBS_ALL), (flow["normed"], UNITS_ALL // 2), (flow["copied_low"], UNITS_ALL),
                  (flow["exp_done"], UNITS_ALL), (flow["copied_high"], TURNS * 4 * HIGH)]

    sp.do(sp_pairs)
    pe.do(pe_pairs, *before_pairs, *lat_done)
    dve.do(dve_pairs)
    act.do(act_pairs)

    banks = Banks(all_banks)

    def residual(t, ps, done, gate, bias=None, extra=None):
        a = tmp[:, t % 4, :]
        if bias is None:
            read = prod = dve.do(lambda e: nc.vector.tensor_tensor(a, ps, gate, op=ALU.mult), done, prior_x[t % 4])
        else:
            read = dve.do(lambda e: nc.vector.tensor_tensor(a, ps, bias, op=ALU.add), done, prior_x[t % 4])
            last = read
            if extra is not None:
                last = dve.do(lambda e: nc.vector.tensor_tensor(a, a, extra, op=ALU.add), last)
            prod = pool.do(lambda e: nc.gpsimd.tensor_tensor(a, a, gate, op=ALU.mult), last)
        wrote = dve.do(lambda e: nc.vector.tensor_tensor(x[:, t, :], x[:, t, :], a, op=ALU.add), prod)
        prior_x[t % 4] = wrote
        return read, wrote

    prior_x = [None] * 4
    ready = []
    for t in range(T):
        i, ps, reader = banks.take()
        done = pe.do(product(ps[:, 0:D], [(yT[:, j, t * P:(t + 1) * P], wout[:, j, :]) for j in range(PAIRS)]),
                     reader, *PAIRS_DONE)
        read, wrote = residual(t, ps[:, 0:D], done, mod_rows[:, 0, :])
        banks.read_by(i, read)
        ready.append(wrote)

    places()
    hT2 = part(C * S, "p (c s) -> p c s", c=C)
    rankT = part(S)
    hid = part(FM * S, "p (m s) -> p m s", m=FM)
    rank2T = part(S)
    normed = normalise(x, ready, EPS)
    hT_done = turn(xn, normed, hT2, scale=mod_cols[:, 3, :], bias=mod_cols[:, 2, :])

    def halves(m_count, stationary, moving, rows_, evacuate, deps):
        res = []
        for half in range(NH):
            cols = slice(half * HW, (half + 1) * HW)
            res.append([])
            for m in range(m_count):
                i, ps, reader = banks.take()
                done = pe.do(product(ps[0:rows_, :], [(w, mv_) for w, mv_ in zip(stationary(m), moving(cols))]),
                             reader, *deps[half])
                step = evacuate(m, half, cols, ps[0:rows_, :], done)
                banks.read_by(i, step)
                res[-1].append(step)
        return res

    low = halves(1, lambda m: [u1[:, c, :] for c in range(C)], lambda cols: [hT2[:, c, cols] for c in range(C)], RF,
                 lambda m, half, cols, ps, done: act.do(lambda e: nc.scalar.copy(rankT[0:RF, cols], ps), done),
                 [[d] for d in hT_done])
    gelu = halves(FM, lambda m: [v1[:, m * P:(m + 1) * P]], lambda cols: [rankT[0:RF, cols]], P,
                  lambda m, half, cols, ps, done: act.do(lambda e: nc.scalar.activation(
                      hid[:, m, cols], ps, ACT.Gelu_apprx_tanh, bias=b1_0[:, m:m + 1]), done),
                  low)
    low2 = halves(1, lambda m: [u2[:, j, :] for j in range(FM)], lambda cols: [hid[:, j, cols] for j in range(FM)], RF,
                  lambda m, half, cols, ps, done: act.do(lambda e: nc.scalar.copy(rank2T[0:RF, cols], ps), done),
                  gelu)
    ready = []
    for t in range(T):
        i, ps, reader = banks.take()
        done = pe.do(product(ps[:, 0:D], [(rank2T[0:RF, t * P:(t + 1) * P], v2[:, :])]), reader, low2[t // TH][0])
        read, wrote = residual(t, ps[:, 0:D], done, mod_rows[:, 1, :], b2_0[:, :])
        banks.read_by(i, read)
        ready.append(wrote)

    places()
    nT = part(C * S, "p (c s) -> p c s", c=C)
    qT = part(C * S, "p (c s) -> p c s", c=C)
    k_tok = part(T * D, "p (t n) -> p t n", t=T)
    v_tok = part(T * HEADS1 * VW, "p (t h v) -> p t h v", t=T, h=HEADS1)
    kT = part(C * S, "p (c s) -> p c s", c=C)
    am = [part(HEADS1 * P, "p (h n) -> p h n", h=HEADS1) for _ in range(2)]
    yT2 = nT
    q_spread = [overlay[:, k * 4096:(k + 1) * 4096].rearrange("p (h n) -> p h n", h=HC) for k in range(2)]

    def affine_rows(normed, scale, shift):
        res = []
        for t in range(T):
            m = pool.do(lambda e, t=t: nc.gpsimd.tensor_tensor(h[:, t, :], xn[:, t, :], scale, op=ALU.mult), normed[t])
            res.append(dve.do(lambda e, t=t: nc.vector.tensor_tensor(h[:, t, :], h[:, t, :], shift, op=ALU.add), m))
        return res

    h_done = affine_rows(normalise(x, ready, EPS), mod_rows[:, 3, :], mod_rows[:, 2, :])
    normed = normalise(h, h_done, EPS_LN)
    nT_done = turn(xn, normed, nT, scale=ln_cols[:, 0, :], bias=ln_cols[:, 1, :])
    ones_set = dve.do(lambda e: nc.vector.memset(v_tok[:, :, :, HD1:VW], 1.0), nT_done[0])
    state_clear = dve.do(lambda e: nc.vector.memset(kv_state[:, :, :], 0.0), nT_done[0])

    def phi(dst, src):
        return lambda e: nc.vector.tensor_scalar(dst, src, 0.0, EPS_PHI, op0=ALU.max, op1=ALU.add)

    k_done, v_done = [], []
    for t in range(T):
        i, ps, reader = banks.take()
        done = pe.do(product(ps, [(nT[:, c, t * P:(t + 1) * P], wkv1[:, c, :]) for c in range(C)]), reader, nT_done[t // TH])
        k_done.append(dve.do(phi(k_tok[:, t, :], ps[:, 0:D]), done))
        v_done.append(act.do(lambda e, t=t, ps=ps: nc.scalar.copy(
            v_tok[:, t, :, 0:HD1], ps[:, D:2 * D].rearrange("p (h n) -> p h n", h=HEADS1)), k_done[-1], ones_set))
        banks.read_by(i, v_done[-1])
    q_done = [[None] * NH for _ in range(C)]
    for half in range(NH):
        cols = slice(half * HW, (half + 1) * HW)
        for m in range(C):
            i, ps, reader = banks.take()
            done = pe.do(product(ps, [(wq1[:, c, m * P:(m + 1) * P], nT[:, c, cols]) for c in range(C)]), reader, nT_done[half])
            q_done[m][half] = dve.do(phi(qT[:, m, cols], ps), done)
            banks.read_by(i, q_done[m][half])
    kT_done = turn(k_tok, k_done, kT)

    state_bank = banks.tiles[7]
    banks7 = Banks(all_banks[0:7])
    banks7.readers = banks.readers[0:7]
    banks7.at = banks.at % 7
    state_reader = banks.readers[7]
    state_done, state_read = None, state_clear
    spread_used = [[None, None] for _ in range(2)]
    am_used = [None, None]
    y_rows, y_done = xn, []
    spread_done = {}
    for t in range(T):
        half, local = t // TH, t % TH
        tok = slice(t * P, (t + 1) * P)
        masked = []
        for c in range(C):
            if local == 0:
                steps = None
                for hh in range(HC):
                    steps = dve.do(lambda e, c=c, hh=hh, half=half: nc.vector.tensor_scalar(
                        q_spread[c][:, hh, :], qT[:, c, half * HW:(half + 1) * HW], head_mask[:, hh:hh + 1], None,
                        op0=ALU.mult), q_done[c][half], spread_used[c][0])
                spread_done[c] = steps
            for quad in range(2):
                i, ps, reader = banks7.take()
                done = pe.do(lambda e, ps=ps, c=c, quad=quad, tok=tok, local=local: nc.tensor.matmul(
                    ps, kT[:, c, tok], q_spread[c][:, quad * 4:quad * 4 + 4, local * P:(local + 1) * P],
                    start=True, stop=True), reader, spread_done[c], kT_done[half])
                spread_used[c][0] = done
                dst = am[t % 2][:, c * HC + quad * 4:c * HC + quad * 4 + 4, :]
                step = dve.do(lambda e, dst=dst, ps=ps: nc.vector.tensor_tensor(
                    dst, ps.rearrange("p (h n) -> p h n", h=4), tril[:, :].unsqueeze(1).to_broadcast([P, 4, P]),
                    op=ALU.mult), done, am_used[t % 2])
                banks7.read_by(i, step)
                masked.append(step)
        i, ps, reader = banks7.take()

        def numerators(e, t=t, tok=tok, ps=ps):
            for c in range(C):
                nc.tensor.matmul(ps[:, c * HC * VW:(c + 1) * HC * VW], qT[:, c, tok], kv_state[:, c, :],
                                 start=c == 0, stop=False, skip_group_check=True)
            for hd in range(HEADS1):
                last = nc.tensor.matmul(ps[:, hd * VW:(hd + 1) * VW], am[t % 2][:, hd, :], v_tok[:, t, hd, :],
                                        start=False, stop=hd == HEADS1 - 1, skip_group_check=True)
            return last

        done = pe.do(numerators, reader, state_read, *masked, v_done[t], q_done[0][half], q_done[1][half])
        am_used[t % 2] = done
        if t < T - 1:
            def update(e, t=t):
                for c in range(C):
                    last = nc.tensor.matmul(state_bank[:, c * HC * VW:(c + 1) * HC * VW],
                                            k_tok[:, t, c * P:(c + 1) * P],
                                            v_tok[:, t, c * HC:(c + 1) * HC, :].rearrange("p h v -> p (h v)"),
                                            start=t == 0 and c == 0, stop=t == T - 2 and c == C - 1,
                                            skip_group_check=True)
                return last

            state_done = pe.do(update, state_reader, state_read)
        view = ps[:, 0:HEADS1 * VW].rearrange("p (h v) -> p h v", h=HEADS1)
        inverse = dve.do(lambda e, view=view: nc.vector.reciprocal(rec[:, :], view[:, :, HD1]), done,
                         y_done[-1] if y_done else None)
        y_done.append(dve.do(lambda e, t=t, view=view: nc.vector.tensor_tensor(
            y_rows[:, t, :].rearrange("p (h n) -> p h n", h=HEADS1), view[:, :, 0:HD1],
            rec[:, :].unsqueeze(2).to_broadcast([P, HEADS1, HD1]), op=ALU.mult), inverse))
        banks7.read_by(i, y_done[-1])
        if t < T - 1:
            state_read = dve.do(lambda e: nc.vector.tensor_tensor(
                kv_state[:, :, :], state_bank[:, 0:HEADS1 * VW].rearrange("p (c n) -> p c n", c=C),
                kv_mask[:, :, :].rearrange("p h v -> p (h v)").unsqueeze(1).to_broadcast([P, C, HC * VW]),
                op=ALU.mult), state_done)
    banks = Banks(all_banks)
    banks.readers = banks7.readers + [state_read]
    attn_read = am_used[(T - 1) % 2]

    f2 = overlay[:, :].rearrange("p (q n) -> p q n", q=EP)
    f2_dram = I["L1_ffn_f2"].rearrange("e s f d -> (e s) f d").rearrange("(q two) f d -> two f q d", two=2)

    def load_f2(e):
        for k in range(2):
            last = e.dma_start(f2[k * EF:(k + 1) * EF, :, :], f2_dram[k]).then_inc(loaded["f2"], 16)
        return last

    sp.do(load_f2, attn_read)

    yT2_done = turn(y_rows, y_done, yT2)
    ready = []
    for t in range(T):
        i, ps, reader = banks.take()
        done = pe.do(product(ps[:, 0:D], [(yT2[:, c, t * P:(t + 1) * P], wo1[:, c, :]) for c in range(C)]), reader,
                     yT2_done[t // TH])
        ready.append(dve.do(lambda e, t=t, ps=ps: nc.vector.tensor_tensor(h[:, t, :], ps[:, 0:D], h[:, t, :], op=ALU.add),
                            done))
        banks.read_by(i, ready[-1])

    places()
    mT = part(C * S, "p (c s) -> p c s", c=C)
    hid1 = part(FM * S, "p (m s) -> p m s", m=FM)
    normed = normalise(h, ready, EPS_LN)
    mT_done = turn(xn, normed, mT, scale=ln_cols[:, 2, :], bias=ln_cols[:, 3, :])
    gelu = halves(FM, lambda m: [w1[:, c, m * P:(m + 1) * P] for c in range(C)],
                  lambda cols: [mT[:, c, cols] for c in range(C)], P,
                  lambda m, half, cols, ps, done: act.do(lambda e: nc.scalar.activation(
                      hid1[:, m, cols], ps, ACT.Gelu_apprx_tanh, bias=b1_1[:, m:m + 1]), done),
                  [[d] for d in mT_done])
    ready = []
    for t in range(T):
        i, ps, reader = banks.take()
        done = pe.do(product(ps[:, 0:D], [(hid1[:, m, t * P:(t + 1) * P], w2[:, m, :]) for m in range(FM)]), reader,
                     *gelu[t // TH])
        read, wrote = residual(t, ps[:, 0:D], done, mod_rows[:, 4, :], b2_1[:, :], h[:, t, :])
        banks.read_by(i, read)
        ready.append(wrote)

    places()
    sel = part(C * ES * G, "p (c s g) -> p c s g", c=C, s=ES)
    inter_t = sel.rearrange("p c s g -> p (c s g)").rearrange("p (c g s) -> p c g s", c=C, g=G)
    hT3 = part(C * S, "p (c s) -> p c s", c=C)
    permT = part(S)
    blockT = part(S)
    perm = [part(GT * ES, "p (g s) -> p g s", g=GT) for _ in range(2)]
    inter = [part(4 * D, "p (k n) -> p k n", k=4) for _ in range(2)]
    logits = inter[0].rearrange("p k n -> p (k n)")
    inner = xn[:, :, :].rearrange("p t n -> p (t n)").rearrange("p (q g) -> p q g", q=EP)

    h_done = affine_rows(normalise(x, ready, EPS), mod_rows[:, 6, :], mod_rows[:, 5, :])
    hT_done = turn(h, h_done, hT3)
    lg = halves(1, lambda m: [ctrl[:, c, :] for c in range(C)], lambda cols: [hT3[:, c, cols] for c in range(C)], P,
                lambda m, half, cols, ps, done: dve.do(lambda e: nc.vector.tensor_tensor(
                    logits[:, cols].rearrange("p (g t) -> p g t", t=NE), ps.rearrange("p (g t) -> p g t", t=NE),
                    tie[:, :].unsqueeze(1).to_broadcast([P, G // NH, NE]), op=ALU.add), done),
                [[d] for d in hT_done])
    perm_done, block_done = [], []
    for half in range(NH):
        cols = slice(half * HW, (half + 1) * HW)
        gs = slice(half * G // NH, (half + 1) * G // NH)
        v3 = logits[:, cols].rearrange("p (g t) -> p g t", t=NE)
        top = dve.do(lambda e, v3=v3, gs=gs: nc.vector.tensor_reduce(logit_max[:, gs], v3, axis=AX_X, op=ALU.max), lg[half][0])
        perm_done.append(dve.do(lambda e, v3=v3, gs=gs, cols=cols: nc.vector.tensor_tensor(
            permT[:, cols].rearrange("p (g t) -> p g t", t=NE), v3,
            logit_max[:, gs].unsqueeze(2).to_broadcast([P, G // NH, NE]), op=ALU.is_equal), top))
        for k in range(2):
            view = [a[:, cols].rearrange("p (q two t) -> p q two t", two=2, t=NE)[:, :, k, :] for a in (blockT, permT)]
            step = dve.do(lambda e, view=view, k=k: nc.vector.tensor_scalar(
                view[0], view[1], half_mask[:, k:k + 1], None, op0=ALU.mult), perm_done[-1])
        block_done.append(step)

    spread_reader = [None, None]
    sel_done = []
    for t in range(T):
        i, ps, reader = banks.take()
        done = pe.do(lambda e, t=t, ps=ps: nc.tensor.transpose(ps[:, 0:ES], permT[0:ES, t * P:(t + 1) * P],
                                                              ident[0:ES, 0:ES]), reader, perm_done[t // TH])
        step = dve.do(lambda e, t=t, ps=ps: nc.vector.tensor_tensor(
            perm[t % 2], ps[:, 0:ES].unsqueeze(1).to_broadcast([P, GT, ES]),
            head_mask[:, :].unsqueeze(2).to_broadcast([P, GT, ES]), op=ALU.mult), done, spread_reader[t % 2])
        banks.read_by(i, step)
        for c in range(C):
            i, ps, reader = banks.take()
            done = pe.do(product(ps, [(h[:, t, c * P:(c + 1) * P], perm[t % 2].rearrange("p g s -> p (g s)"))]), reader, step)
            spread_reader[t % 2] = done
            o = sel[:, c, :, t * GT:(t + 1) * GT].rearrange("p s g -> p g s")
            src = ps.rearrange("p (g s) -> p g s", g=GT)
            if c == 0:
                copy = act.do(lambda e, o=o, src=src: nc.scalar.copy(o, src), done)
            else:
                copy = dve.do(lambda e, o=o, src=src: nc.vector.tensor_copy(o, src), done)
            banks.read_by(i, copy)
            sel_done.append(copy)

    inner_done = []
    for blk in range(4):
        i, ps, reader = banks.take()

        def first_product(e, blk=blk, ps=ps):
            for s in range(blk * 16, blk * 16 + 16):
                o = ps[(s % 2) * EF:(s % 2 + 1) * EF, (s // 2 - blk * 8) * G:(s // 2 - blk * 8 + 1) * G]
                for c in range(C):
                    last = nc.tensor.matmul(o, f1[:, c, s, :], sel[:, c, s, :], start=c == 0, stop=c == C - 1)
            return last

        done = pe.do(first_product, reader, *(sel_done if blk == 0 else []))
        dst = inner[:, blk * 8:blk * 8 + 8, :]
        biased = dve.do(lambda e, ps=ps, dst=dst, blk=blk: nc.vector.tensor_tensor(
            dst, ps.rearrange("p (q g) -> p q g", q=8),
            fbias[:, blk * 8:blk * 8 + 8].unsqueeze(2).to_broadcast([P, 8, G]), op=ALU.add), done)
        banks.read_by(i, biased)
        inner_done.append(act.do(lambda e, dst=dst: nc.scalar.activation(dst, dst, ACT.Relu), biased))

    inter_t_done = []
    for c in range(C):
        for blk in range(4):
            (ie, pe_even, even_reader), (io, pe_odd, odd_reader) = banks.take(), banks.take()

            def second_product(e, blk=blk, ps=(pe_even, pe_odd), c=c):
                for s in range(blk * 16, blk * 16 + 16):
                    half_p = slice((s % 2) * EF, (s % 2 + 1) * EF)
                    k = s // 2 - blk * 8
                    last = nc.tensor.matmul(ps[s % 2][:, k * G:(k + 1) * G], f2[half_p, s // 2, c * P:(c + 1) * P],
                                            inner[half_p, s // 2, :], start=True, stop=True)
                return last

            done = pe.do(second_product, even_reader, odd_reader, inner_done[blk], (loaded["f2"], 32))
            for odd, i, ps in ((0, ie, pe_even), (1, io, pe_odd)):
                o = inter_t[:, c, :, blk * 16 + odd:(blk + 1) * 16:2].rearrange("p g s -> p s g")
                src = ps.rearrange("p (s g) -> p s g", s=8)
                if odd:
                    copy = act.do(lambda e, o=o, src=src: nc.scalar.copy(o, src), done, inner_done[3])
                else:
                    copy = dve.do(lambda e, o=o, src=src: nc.vector.tensor_copy(o, src), done, inner_done[3])
                banks.read_by(i, copy)
                inter_t_done.append(copy)

    inter_reader = [None, None]
    finals = []
    for t in range(T):
        copies = []
        for two in range(2):
            i, ps, reader = banks.take()

            def turn_back(e, t=t, two=two, ps=ps):
                for kk in range(2):
                    g = t * GT + (two * 2 + kk) * 2
                    for c in range(C):
                        last = nc.tensor.transpose(ps[:, kk * D + c * P:kk * D + (c + 1) * P],
                                                   inter_t[:, c, g:g + 2, :].rearrange("p g s -> p (g s)"), ident[:, :])
                return last

            done = pe.do(turn_back, reader, *(inter_t_done if t == 0 and two == 0 else []))
            dst = inter[t % 2][:, two * 2:two * 2 + 2, :]
            src = ps.rearrange("p (k n) -> p k n", k=2)
            if two:
                copies.append(act.do(lambda e, dst=dst, src=src: nc.scalar.copy(dst, src), done, inter_reader[t % 2]))
            else:
                copies.append(dve.do(lambda e, dst=dst, src=src: nc.vector.tensor_copy(dst, src), done, inter_reader[t % 2]))
            banks.read_by(i, copies[-1])
        i, ps, reader = banks.take()

        def combine(e, t=t, ps=ps):
            for kk in range(4):
                lo = t * P + kk * 32
                last = nc.tensor.matmul(ps[kk * 32:(kk + 1) * 32, 0:D], blockT[:, lo:lo + 32], inter[t % 2][:, kk, :],
                                        start=True, stop=True)
            return last

        done = pe.do(combine, reader, *copies, block_done[t // TH])
        inter_reader[t % 2] = done
        read, wrote = residual(t, ps[:, 0:D], done, mod_rows[:, 7, :])
        banks.read_by(i, read)
        finals.append(wrote)

    def store(e):
        return e.dma_start(x_out[b_reg["b"]], x[:, :, :]).then_inc(stored, 16)

    sp.do(store, finals[-1])

    def wait_stored(e):
        return e.wait_ge(stored, 16)

    sp.do(wait_stored)
    for ln in lane.values():
        ln.number()

    cleared = [ln.sem for ln in lane.values()] + list(flow.values())
    cleared += [loaded[k] for k in ("x", "rows", "f2", "w0", "w1")] + [stored]
    with nc.Fori(0, NB) as b:
        b_reg["b"] = b
        with nc.Block() as block:
            block.sync(sp.emit)
            block.scalar(act.emit)
            block.vector(dve.emit)
            block.tensor(pe.emit)
            block.gpsimd(pool.emit)
        for s in cleared:
            nc.sync.sem_clear(s)
        nc.all_engine_barrier()
    ctx.close()


_INS = ["L0_attn_x", "L0_attn_w_kv_down", "L0_attn_w_kv_up", "L0_attn_w_q", "L0_attn_w_out", "L0_ffn_U1", "L0_ffn_V1",
        "L0_ffn_b1", "L0_ffn_U2", "L0_ffn_V2", "L0_ffn_b2", "L0_c", "L0_wmod", "L1_attn_ln1_scale", "L1_attn_ln1_bias",
        "L1_attn_wq", "L1_attn_wk", "L1_attn_wv", "L1_attn_wo", "L1_attn_ln2_scale", "L1_attn_ln2_bias", "L1_attn_w1",
        "L1_attn_b1", "L1_attn_w2", "L1_attn_b2", "L1_ffn_controller", "L1_ffn_f1", "L1_ffn_f2", "L1_ffn_bias", "L1_c",
        "L1_wmod"]


def kernel(**inputs):
    import concourse.bacc as bacc
    from concourse.bass_utils import run_bass_kernel_spmd

    nc = bacc.Bacc("TRN2", target_bir_lowering=False, num_devices=1)
    arrays, args = {}, {}
    for name in _INS:
        arrays[name] = np.ascontiguousarray(inputs[name])
    arrays["tie"] = np.linspace(0.0, 1e-6, NE, dtype=np.float32)
    for name, a in arrays.items():
        args[name] = nc.dram_tensor("in_" + name, a.shape, mybir.dt.from_np(a.dtype), kind="ExternalInput").ap()
    out = nc.dram_tensor("out", (NB, S, D), F32, kind="ExternalOutput").ap()
    build(nc, args, out)
    r = run_bass_kernel_spmd(nc, [{"in_" + name: a for name, a in arrays.items()}], core_ids=[0])
    return r.results[0]["out"]
```

```python
import numpy as np
import concourse.bass as bass
from concourse import mybir
from contextlib import ExitStack

F32 = mybir.dt.float32
F32R = mybir.dt.float32r
BF16 = mybir.dt.bfloat16
ACT = mybir.ActivationFunctionType
ALU = mybir.AluOpType
AX_X = mybir.AxisListType.X

P = 128
NB = 4
S = 1024
D = 256
C = D // P
T = S // P
NH = 2
HW = S // NH
TH = T // NH
HD0 = 64
HEADS0 = 16
PAIRS = HEADS0 // 2
RK = 128
FF = 1024
FM = FF // P
RF = 64
U = 2 * T
EPS = 1e-5
HEADS1 = 16
HD1 = 16
HC = HEADS1 // C
VW = HD1 + 1
EPS_LN = 1e-6
EPS_PHI = 1e-3
NE = 16
ES = 64
EF = 64
G = S // NE
GT = P // NE
EP = ES // 2
NEG = -1e30


class Lane:

    def __init__(self, sem):
        self.sem, self.steps = sem, []

    def do(self, emit, *after):
        step = Step(self, emit, [a for a in after if a is not None])
        self.steps.append(step)
        return step

    def number(self):
        n = 0
        for s in self.steps:
            if s.needed:
                n += 1
                s.value = n

    def emit(self, engine):
        seen = {}
        for s in self.steps:
            for a in s.after:
                sem, value = (a.lane.sem, a.value) if isinstance(a, Step) else a
                if seen.get(sem.name, 0) < value:
                    engine.wait_ge(sem, value)
                    seen[sem.name] = value
            last = s.emit(engine)
            if s.needed:
                last.then_inc(self.sem, 1)


class Step:
    def __init__(self, lane, emit, after):
        self.lane, self.emit, self.after = lane, emit, after
        self.needed, self.value = False, 0
        for a in after:
            if isinstance(a, Step):
                a.needed = True


class Banks:

    def __init__(self, tiles):
        self.tiles, self.readers, self.at = tiles, [None] * len(tiles), -1

    def take(self):
        self.at = (self.at + 1) % len(self.tiles)
        return self.at, self.tiles[self.at], self.readers[self.at]

    def read_by(self, index, step):
        self.readers[index] = step


def build(nc, I, out):
    ctx = ExitStack()
    ctx.enter_context(nc.allow_non_contiguous_dma(reason="bias columns and broadcast rows"))

    def sb(name, shape, dt=F32):
        return ctx.enter_context(nc.sbuf_tensor(name, shape, dt))

    def semaphore(name):
        return ctx.enter_context(nc.semaphore(name))

    bank = [ctx.enter_context(nc.psum_tensor(f"bank{i}", [P, 512], F32)) for i in range(4)]
    score_tiles = [ctx.enter_context(nc.psum_tensor(f"scores{i}", [P, 2, 512], F32)) for i in range(2)]
    all_banks = [b[:, :] for b in bank] + [s[:, i, :] for s in score_tiles for i in range(2)]

    wout = sb("wout", [P, PAIRS, D])
    u1, v1 = sb("u1", [P, C, RF]), sb("v1", [RF, FF])
    u2, v2 = sb("u2", [P, FM, RF]), sb("v2", [RF, D])
    wdown = sb("wdown", [P, C, RK])
    wq1, wkv1, wo1 = sb("wq1", [P, C, D]), sb("wkv1", [P, C, 2 * D]), sb("wo1", [P, C, D])
    w1, w2 = sb("w1", [P, C, FF]), sb("w2", [P, FM, D])
    ctrl = sb("ctrl", [P, C, 2 * ES])
    b1_0, b1_1 = sb("b1_0", [P, FM]), sb("b1_1", [P, FM])
    b2_0, b2_1 = sb("b2_0", [P, D]), sb("b2_1", [P, D])
    ln_cols = sb("ln_cols", [P, 4, C])
    fbias = sb("fbias", [P, EP])
    tie = sb("tie", [P, NE])
    ident = sb("ident", [P, P])
    ident_b = sb("ident_b", [P, P], BF16)
    neg_b = sb("neg_b", [P, P], BF16)
    tril = sb("tril", [P, P])
    head_mask = sb("head_mask", [P, HC])
    kv_mask = sb("kv_mask", [P, HC, VW])
    half_mask = sb("half_mask", [P, 2])
    minus_half = sb("minus_half", [P, T])
    x = sb("x", [P, T, D])
    h = sb("h", [P, T, D])
    xn = sb("xn", [P, T, D])
    mod_rows = sb("mod_rows", [P, 8, D])
    mod_cols = sb("mod_cols", [P, 4, C])
    tmp = sb("tmp", [P, 4, D])
    stats = sb("stats", [P, T, 6])
    mv = sb("mv", [P, T, 2])
    rstd = sb("rstd", [P, T])
    neg_max = sb("neg_max", [P, 4])
    row_sum = sb("row_sum", [P, 8])
    rec = sb("rec", [P, HEADS1])
    logit_max = sb("logit_max", [P, G])
    kv_state = sb("kv_state", [P, C, HC * VW])

    STORES = T // 2 * 16

    SPLIT = 3 * 4 * S
    ROOM = 15 * S
    OVER = 8 * S
    slab_start = nc.sbuf_base
    sb("slab", [P, OVER + 8 * S + ROOM])
    at = [0]

    def begin(where):
        at[0] = where

    def part(name, shape, dt=F32):
        words = int(np.prod(shape[1:]))
        a = nc.alloc_sbuf_tensor_at(name, shape, dt, offset=slab_start + 4 * at[0])
        at[0] += words
        if at[0] > OVER + 8 * S + ROOM:
            raise ValueError("the slab is too small for " + name)
        return a

    OVERLAY, FIRST, WORK = 0, OVER, OVER + 8 * S

    lane = {k: Lane(semaphore(f"{k}_steps")) for k in ("pe", "act", "dve", "pool", "sp")}
    pe, act, dve, pool, sp = (lane[k] for k in ("pe", "act", "dve", "pool", "sp"))
    setup = {k: Lane(semaphore(f"{k}_setup")) for k in ("pe", "act", "dve", "pool", "sp")}
    loaded = {k: semaphore(f"loaded_{k}") for k in (
        "weights", "cond", "x", "next_x", "columns", "rows", "f1", "f2", "w0", "w1", "keys0", "keys1")}
    stored = semaphore("stored")
    flow = {k: semaphore(k) for k in (
        "scores_done", "max_done", "exp_done", "turned_low", "turned_high", "copied_low", "copied_high",
        "rounded", "values_done", "inverted", "normed", "job_done", "job_read")}
    names = ("pe", "act", "dve", "pool", "sp")

    mod_dram = nc.dram_tensor("mod_scratch", [NB, 2, 6, D], F32, kind="Internal").ap()

    begin(WORK)
    cond = part("cond", [P, 2, C, NB])
    silu = part("silu", [P, 2, C, NB])
    wmod = [part(f"wmod{k}", [P, C, 6 * D]) for k in range(2)]
    mod_sb = part("mod_sb", [P, 2, 6, D])
    gate_a, gate_s = h[:, 0:2, :], h[:, 2:4, :]

    weight_loads = []

    def load(dst, src):
        weight_loads.append((dst, src))

    def rows(w, p=P):
        return w.rearrange("(c p) n -> p c n", p=p)

    load(wdown[:, :, :], rows(I["L0_attn_w_kv_down"]))
    load(wout[:, :, :], rows(I["L0_attn_w_out"]))
    load(u1[:, :, :], rows(I["L0_ffn_U1"]))
    load(v1[:, :], I["L0_ffn_V1"])
    load(u2[:, :, :], rows(I["L0_ffn_U2"]))
    load(v2[:, :], I["L0_ffn_V2"])
    load(wq1[:, :, :], rows(I["L1_attn_wq"].rearrange("d h m -> d (h m)")))
    load(wkv1[:, :, 0:D], rows(I["L1_attn_wk"].rearrange("d h m -> d (h m)")))
    load(wkv1[:, :, D:2 * D], rows(I["L1_attn_wv"].rearrange("d h m -> d (h m)")))
    load(wo1[:, :, :], rows(I["L1_attn_wo"].rearrange("h m d -> (h m) d")))
    load(w1[:, :, :], rows(I["L1_attn_w1"]))
    load(w2[:, :, :], rows(I["L1_attn_w2"]))
    for k in range(2):
        load(ctrl[:, :, k * ES:(k + 1) * ES], rows(I["L1_ffn_controller"].rearrange("d e s -> d (e s)")))
    load(b1_0[:, :], I["L0_ffn_b1"].rearrange("(m p) -> p m", p=P))
    load(b1_1[:, :], I["L1_attn_b1"].rearrange("(m p) -> p m", p=P))
    load(b2_0[:, :], I["L0_ffn_b2"].partition_broadcast(P))
    load(b2_1[:, :], I["L1_attn_b2"].partition_broadcast(P))
    for k, name in enumerate(("ln1_scale", "ln1_bias", "ln2_scale", "ln2_bias")):
        load(ln_cols[:, k, :], I["L1_attn_" + name].rearrange("(c p) -> p c", p=P))
    slots = I["L1_ffn_bias"].rearrange("e s f -> (e s) f").rearrange("(q two) f -> two f q", two=2)
    for k in range(2):
        load(fbias[k * EF:(k + 1) * EF, :], slots[k])
    load(tie[:, :], I["tie"].partition_broadcast(P))
    cond_loads = [(cond[:, l, c, :], I[f"L{l}_c"].rearrange("b (c p) -> c p b", p=P)[c]) for l in range(2) for c in range(C)]
    cond_loads += [(wmod[l][:, :, :], rows(I[f"L{l}_wmod"])) for l in range(2)]

    s_act, s_dve, s_pe, s_pool = setup["act"], setup["dve"], setup["pe"], setup["pool"]

    x_in = I["L0_attn_x"].rearrange("b (t p) d -> b p t d", p=P)
    x_out = out.rearrange("b (t p) d -> b p t d", p=P)
    b_reg = {}

    def load_x(e, dst, b, sem="next_x"):
        for half in range(NH):
            ts = slice(half * TH, (half + 1) * TH)
            last = e.dma_start(dst[:, ts, :], x_in[b][:, ts, :]).then_inc(loaded[sem], 16)
        return last

    def load_columns(e, b):
        for k, s in enumerate((0, 1, 3, 4)):
            last = e.dma_start(mod_cols[:, k, :], mod_dram[b, 0, s].rearrange("(c p) -> p c", p=P)
                               ).then_inc(loaded["columns"], 16)
        return last

    def load_rows(e):
        b = b_reg["b"]
        for k, s in enumerate((2, 5)):
            e.dma_start(mod_rows[:, k, :], mod_dram[b, 0, s].partition_broadcast(P)).then_inc(loaded["rows"], 16)
        return e.dma_start(mod_rows[:, 2:8, :].rearrange("p s n -> p (s n)"),
                           mod_dram[b, 1].rearrange("s n -> (s n)").partition_broadcast(P)).then_inc(loaded["rows"], 16)

    COLUMN_DMA = 4 * 16
    X_LOADED, NEXT_X = (loaded["x"], NH * 16), (loaded["next_x"], NH * 16)
    ROWS = (loaded["rows"], 16 * 3)

    def tiles_of(half):
        return range(half * TH, (half + 1) * TH)

    def norm_stats(src, half, ready, eps, lanes=(dve, pool)):
        dve, pool = lanes
        last = None
        for t, r in zip(tiles_of(half), ready):
            s = dve.do(lambda e, t=t: nc.vector.bn_stats(stats[:, t, :], src[:, t, :]), r)
            last = dve.do(lambda e, t=t: nc.vector.bn_aggr(mv[:, t, :], stats[:, t, :]), s)
        ts = slice(half * TH, (half + 1) * TH)
        var = pool.do(lambda e: nc.gpsimd.tensor_scalar(rstd[:, ts], mv[:, ts, 1], eps, None, op0=ALU.add), last)
        return pool.do(lambda e: nc.gpsimd.tensor_tensor(rstd[:, ts], rstd[:, ts], minus_half[:, ts], op=ALU.pow), var)

    def norm_apply(src, half, inv, dve=dve):
        return [dve.do(lambda e, t=t: nc.vector.tensor_scalar(
            xn[:, t, :], src[:, t, :], mv[:, t, 0:1], rstd[:, t:t + 1], op0=ALU.subtract, op1=ALU.mult), inv)
            for t in tiles_of(half)]

    def normalise(src, half, ready, eps, lanes=(dve, pool)):
        return norm_apply(src, half, norm_stats(src, half, ready, eps, lanes), lanes[0])

    def fill(ap, value):
        return s_pool.do(lambda e: nc.gpsimd.memset(ap, value))

    def select(ap, pattern, base, mult, op, value, *after):
        return s_pool.do(lambda e: nc.gpsimd.affine_select(
            out=ap, in_=ap, compare_op=op, fill=value, base=base, pattern=pattern, channel_multiplier=mult), *after)

    ident_done = select(ident[:, :], [[-1, P]], 0, 1, ALU.not_equal, 1.0, fill(ident[:, :], 0.0))
    s_dve.do(lambda e: nc.vector.tensor_copy(ident_b[:, :], ident[:, :]), ident_done)
    select(neg_b[:, :], [[-1, P]], 0, 1, ALU.is_ge, NEG, fill(neg_b[:, :], 0.0))
    select(tril[:, :], [[1, P]], 0, -1, ALU.is_ge, 0.0, fill(tril[:, :], 1.0))
    for ap, extra in ((head_mask[:, :], []), (kv_mask[:, :, :], [[0, VW]])):
        first = select(ap, [[-HD1, HC]] + extra, 0, 1, ALU.is_ge, 0.0, fill(ap, 1.0))
        select(ap, [[HD1, HC]] + extra, HD1 - 1, -1, ALU.is_ge, 0.0, first)
    first = select(half_mask[:, :], [[-ES, 2]], 0, 1, ALU.is_ge, 0.0, fill(half_mask[:, :], 1.0))
    select(half_mask[:, :], [[ES, 2]], ES - 1, -1, ALU.is_ge, 0.0, first)
    fill(minus_half[:, :], -0.5)
    for half in range(NH):
        normalise(x, half, [NEXT_X] * TH, EPS, (s_dve, s_pool))

    silu_done = s_act.do(lambda e: nc.scalar.activation(silu[:, :, :, :], cond[:, :, :, :], ACT.Silu), (loaded["cond"], 16 * len(cond_loads)))
    mod_copied = []
    for l in range(2):
        for n in range(3):
            ps = all_banks[3 * l + n][0:NB, :]

            def mod_matmul(e, ps=ps, l=l, n=n):
                for c in range(C):
                    last = nc.tensor.matmul(ps, silu[:, l, c, :], wmod[l][:, c, n * 512:(n + 1) * 512],
                                            start=c == 0, stop=c == C - 1)
                return last

            done = s_pe.do(mod_matmul, silu_done)
            mod_copied.append(s_dve.do(
                lambda e, ps=ps, l=l, n=n: nc.vector.tensor_copy(
                    mod_sb[0:NB, l, 2 * n:2 * n + 2, :].rearrange("b s n -> b (s n)"), ps), done))
    last = mod_copied[-1]
    mod_done = []
    for l in range(2):
        scales = mod_sb[0:NB, l, 1:6:3, :]
        gates = mod_sb[0:NB, l, 2:6:3, :]
        ga_, gs_ = gate_a[0:NB], gate_s[0:NB]
        mod_done.append(s_dve.do(lambda e, a=scales: nc.vector.tensor_scalar(a, a, 1.0, None, op0=ALU.add), last))
        size = s_dve.do(lambda e, a=gates, o=ga_: nc.vector.scalar_tensor_tensor(
            o, a, -1.0, a, op0=ALU.mult, op1=ALU.max), last, mod_done[-1])
        size = s_dve.do(lambda e, o=ga_: nc.vector.tensor_scalar(o, o, 0.25, None, op0=ALU.max), size)
        sign = s_dve.do(lambda e, a=gates, o=gs_: nc.vector.tensor_scalar(o, a, 0.0, 2.0, op0=ALU.is_ge, op1=ALU.mult),
                        size)
        last = s_dve.do(lambda e, a=gates, s=gs_, g=ga_: nc.vector.scalar_tensor_tensor(
            a, s, -1.0, g, op0=ALU.add, op1=ALU.mult), sign)
        mod_done.append(last)

    def setup_sp(e):
        for dst, src in cond_loads:
            e.dma_start(dst, src).then_inc(loaded["cond"], 16)
        load_x(e, x, 0)
        for dst, src in weight_loads:
            e.dma_start(dst, src).then_inc(loaded["weights"], 16)
        for m in mod_done:
            e.wait_ge(m.lane.sem, m.value)
        e.dma_start(mod_dram.rearrange("b l s n -> b l (s n)"),
                    mod_sb[0:NB, :, :, :].rearrange("b l s n -> b l (s n)")).then_inc(stored, 16)
        e.wait_ge(stored, 16)
        load_columns(e, 0)
        e.wait_ge(loaded["columns"], COLUMN_DMA)

    for m in mod_done:
        m.needed = True
    for s in setup.values():
        s.number()
    with nc.Block() as block:
        block.sync(setup_sp)
        block.scalar(setup["act"].emit)
        block.vector(setup["dve"].emit)
        block.tensor(setup["pe"].emit)
        block.gpsimd(setup["pool"].emit)
    nc.sync.sem_clear(loaded["next_x"])
    nc.sync.sem_clear(loaded["columns"])
    nc.all_engine_barrier()

    WEIGHTS = (loaded["weights"], 16 * len(weight_loads))

    banks = Banks(all_banks)
    def turn(src, half, ready, dst, scale=None, bias=None, after=None):
        for c in range(C):
            i, ps, reader = banks.take()

            def transposes(e, c=c, ps=ps):
                for t in range(TH):
                    last = nc.tensor.transpose(ps[:, t * P:(t + 1) * P], src[:, half * TH + t, c * P:(c + 1) * P],
                                               ident[:, :])
                return last

            done = pe.do(transposes, *ready, reader)
            o = dst[:, c, half * HW:(half + 1) * HW]
            if scale is None:
                copy = act.do(lambda e, o=o, ps=ps: nc.scalar.copy(o, ps), done, after)
            else:
                copy = act.do(lambda e, o=o, ps=ps, c=c: nc.scalar.activation(
                    o, ps, ACT.Identity, bias=bias[:, c:c + 1], scale=scale[:, c:c + 1]), done, after)
            banks.read_by(i, copy)
        return copy

    def product(ps, pieces):
        def emit(e):
            for n, (w, m) in enumerate(pieces):
                last = nc.tensor.matmul(ps, w, m, start=n == 0, stop=n == len(pieces) - 1)
            return last
        return emit

    def load_batch(e):
        e.wait_ge(stored, b_reg["b"] * STORES + 16)
        load_x(e, x, b_reg["b"], "x")
        return load_rows(e)

    sp.do(load_batch)
    begin(OVERLAY)
    yT = part("yT", [P, PAIRS, S])
    begin(FIRST)
    q_split = part("q_split", [P, 2, 2, S], F32R)
    k_high = part("k_high", [P, 2, 2, S], F32R)
    k_low = part("k_low", [P, 2, 2, S], F32R)
    begin(WORK + SPLIT - 8 * S)
    hT = part("hT", [P, C, S])
    latT = part("latT", [P, S])
    v_t = [part(f"v_t{k}", [P, T, P]) for k in range(2)]
    prob = [part(f"prob{k}", [P, S]) for k in range(2)]
    probT = [part(f"probT{k}", [P, S]) for k in range(2)]
    y_t = part("y_t", [P, T, P])
    w_ring = [part(f"w_ring{k}", [P, 4 * P]) for k in range(2)]

    wq_dram = I["L0_attn_w_q"].rearrange("(c p) n -> p c n", p=P)
    wkv_dram = I["L0_attn_w_kv_up"]

    def load_pair(e, buf, col, sem):
        dst = w_ring[buf]
        e.dma_start(dst[:, 0:2 * P].rearrange("p (c n) -> p c n", c=C), wq_dram[:, :, bass.ds(col, P)]).then_inc(sem, 16)
        e.dma_start(dst[:, 2 * P:3 * P], wkv_dram[:, bass.ds(col, P)]).then_inc(sem, 16)
        return e.dma_start(dst[:, 3 * P:4 * P], wkv_dram[:, bass.ds(col + HEADS0 * HD0, P)]).then_inc(sem, 16)

    PAIR_DMA = 3 * 16
    KEY_DMA = 4 * 16

    def double_keys(e, buf):
        for dst in (k_high, k_low):
            for head, (a, b) in enumerate(((TOP, BOTTOM), (BOTTOM, TOP))):
                e.dma_start(dst[b, buf, head, :].bitcast(F32), dst[a, buf, head, :].bitcast(F32)
                            ).then_inc(loaded[f"keys{buf}"], 16)

    JOBS = 8
    FIRST_JOBS = 6
    BODY = 2 * U
    TURNS = PAIRS // 2
    HIGH = T // 2

    lat_done = []
    for half in range(NH):
        cols = slice(half * HW, (half + 1) * HW)
        turned = turn(xn, half, [], hT, scale=mod_cols[:, 1, :], bias=mod_cols[:, 0, :])
        i, ps, reader = banks.take()
        done = pe.do(product(ps, [(wdown[:, c, :], hT[:, c, cols]) for c in range(C)]), turned, reader, WEIGHTS)
        copy = act.do(lambda e, ps=ps, cols=cols: nc.scalar.copy(latT[:, cols], ps), done)
        banks.read_by(i, copy)
        lat_done.append(copy)
    before_pairs = [r for r in banks.readers if r is not None]

    turned_bank = [bank[0], bank[1]]
    value_bank, job_bank = bank[2], bank[3]

    def unit(u):
        return (u // U) % 2, (u % U) // 2, u % 2, u % 2

    def high_before(u):
        return (u // U) * 2 * HIGH + max(0, u % U - 2 * HIGH)

    first_jobs = list(zip(("k0", "k1", "q0", "q1", "v0", "v1"), bank + [t[:, i, :] for t in score_tiles[:1] for i in range(2)]))

    def pe_job(e, n, kind, buf, ps=None):
        half = int(kind[1])
        cols = slice(half * HW, (half + 1) * HW)
        if ps is None:
            ps = job_bank
            e.wait_ge(flow["job_read"], n)
        wq, wk, wv = (w_ring[buf][:, k * P:(k + 1) * P] for k in (0, 2, 3))
        if kind[0] == "q":
            for c in range(C):
                last = nc.tensor.matmul(ps[:, :], w_ring[buf][:, c * P:(c + 1) * P], hT[:, c, cols],
                                        start=c == 0, stop=c == C - 1)
        elif kind[0] == "k":
            last = nc.tensor.matmul(ps[:, :], wk, latT[:, cols], start=True, stop=True)
        elif kind[0] == "v":
            for t in range(TH):
                tile = half * TH + t
                last = nc.tensor.matmul(ps[:, t * P:(t + 1) * P], latT[:, tile * P:(tile + 1) * P], wv,
                                        start=True, stop=True)
        else:
            for t in range(TH):
                last = nc.tensor.transpose(ps[:, t * P:(t + 1) * P], y_t[:, half * TH + t, :], ident[:, :])
        last.then_inc(flow["job_done"], 1)

    TOP, BOTTOM = slice(0, HD0), slice(HD0, P)

    def act_job(e, n, kind, buf, pair, ps=job_bank):
        half = int(kind[1])
        cols = slice(half * HW, (half + 1) * HW)
        e.wait_ge(flow["job_done"], n + 1)
        if kind[0] in "qk":
            dst = q_split if kind[0] == "q" else k_high
            for head, rows_ in enumerate((TOP, BOTTOM)):
                last = nc.scalar.mul(dst[rows_, buf, head, cols], ps[rows_, :],
                                     HD0 ** -0.5 if kind[0] == "q" else 1.0)
            last.then_inc(flow["rounded"], 1)
            return
        if kind[0] == "v":
            last = nc.scalar.copy(v_t[buf][:, half * TH:(half + 1) * TH, :],
                                  ps[:, :].rearrange("p (t n) -> p t n", t=TH))
        else:
            last = nc.scalar.copy(yT[:, bass.ds(pair, 1), cols],
                                  ps[:, :].rearrange("p (o n) -> p o n", o=1))
        last.then_inc(flow["job_read"], 1)

    def dve_job(e, kind, buf, splits, ps=job_bank):
        if kind[0] not in "qk":
            return
        half = int(kind[1])
        cols = slice(half * HW, (half + 1) * HW)
        e.wait_ge(flow["rounded"], splits)
        for head, rows_, other in ((0, TOP, BOTTOM), (1, BOTTOM, TOP)):
            if kind[0] == "q":
                last = nc.vector.scalar_tensor_tensor(
                    q_split[other, buf, head, cols], ps[rows_, :], HD0 ** -0.5,
                    q_split[rows_, buf, head, cols].bitcast(F32), op0=ALU.mult, op1=ALU.subtract)
            else:
                last = nc.vector.tensor_tensor(k_low[rows_, buf, head, cols], ps[rows_, :],
                                               k_high[rows_, buf, head, cols].bitcast(F32), op=ALU.subtract)
        last.then_inc(flow["job_read"], 1)

    SCHEDULE = {2: "v0", 4: "v1", 6: "k0", 8: "k1", 10: "q0", 12: "q1", 14: "Y0"}

    QK_READ = 6

    def jobs_at(u, tail):
        w, k = u // U, u % U
        if w > 1 or k not in SCHEDULE:
            return None
        kind = SCHEDULE[k]
        if tail and w == 1 and kind != "Y0":
            return None
        order = sorted(SCHEDULE)
        n = w * JOBS + order.index(k)
        if tail and w == 1:
            n = w * JOBS
        splits = w * 4 + sum(SCHEDULE[j][0] in "qk" for j in order if j <= k)
        return n, kind, (w if kind[0] == "Y" else 1 - w), splits

    def y1_number(w, tail):
        return w * JOBS + (1 if tail and w == 1 else JOBS - 1)

    def pe_pairs(e):
        def scores(u):
            buf, i, head, par = unit(u)
            width = (i + 1) * P
            flat = score_tiles[par][:, :, :].rearrange("p a n -> p (a n)")
            qs = q_split[:, buf, head, i * P:(i + 1) * P]
            for seg in range(0, width, 512):
                end = min(width, seg + 512)
                nc.tensor.matmul(flat[:, seg:end], qs, k_high[:, buf, head, seg:end], start=True, stop=False)
                nc.tensor.matmul(flat[:, seg:end], qs, k_low[:, buf, head, seg:end], start=False, stop=end < width)
            nc.tensor.matmul(flat[:, i * P:width], ident_b[:, :], neg_b[:, :], start=False, stop=True
                             ).then_inc(flow["scores_done"], 1)

        def turn_probs(u, g, high):
            _, i, _, par = unit(u)
            e.wait_ge(flow["exp_done"], g + 1)
            e.wait_ge(flow["copied_low"], g)
            for j in range(min(4, i + 1)):
                last = nc.tensor.transpose(turned_bank[0][:, j * P:(j + 1) * P], prob[par][:, j * P:(j + 1) * P],
                                           ident[:, :])
            last.then_inc(flow["turned_low"], 1)
            if i >= 4:
                if u % U > 2 * HIGH:
                    e.wait_ge(flow["copied_high"], high)
                for j in range(4, i + 1):
                    last = nc.tensor.transpose(turned_bank[1][:, (j - 4) * P:(j - 3) * P],
                                               prob[par][:, j * P:(j + 1) * P], ident[:, :])
                last.then_inc(flow["turned_high"], 1)

        def values(u, g, high, tile, first):
            buf, i, head, par = unit(u)
            e.wait_ge(flow["copied_low"], g + 1)
            if i >= 4:
                e.wait_ge(flow["copied_high"], high + 1)
            if head == 0 and first > 0:
                e.wait_ge(flow["normed"], tile)
            o = value_bank[:, head * HD0:(head + 1) * HD0]
            for j in range(i + 1):
                last = nc.tensor.matmul(o, probT[par][:, j * P:(j + 1) * P],
                                        v_t[buf][:, j, head * HD0:(head + 1) * HD0], start=j == 0, stop=j == i)
            last.then_inc(flow["values_done"], 1)

        def steps(n, first, end, tail):
            g0 = e.snap(n * BODY) if not isinstance(n, int) else n * BODY
            hi0 = n * (4 * HIGH)
            j0 = n * (2 * JOBS) + FIRST_JOBS
            for u in range(first, end):
                turn_probs(u, g0 + u, hi0 + high_before(u))
                if u + 2 < BODY or not tail:
                    if u + 2 == U:
                        e.wait_ge(loaded["keys1"], n * KEY_DMA + KEY_DMA)
                        e.wait_ge(flow["job_read"], j0 + QK_READ)
                    if u + 2 == BODY:
                        e.wait_ge(loaded["keys0"], n * KEY_DMA + 2 * KEY_DMA)
                        e.wait_ge(flow["job_read"], j0 + JOBS + QK_READ)
                    scores(u + 2)
                if u > 0:
                    values(u - 1, g0 + u - 1, hi0 + high_before(u - 1), n * (BODY // 2) + (u - 1) // 2, (u - 1) // 2)
                if u > 1 and u % U == 1:
                    e.wait_ge(flow["normed"], n * (BODY // 2) + (u // U) * T)
                    pe_job(e, j0 + y1_number(u // U - 1, tail), "Y1", u // U - 1)
                job = jobs_at(u, tail)
                if job:
                    k, kind, buf, _ = job
                    if kind == "Y0":
                        e.wait_ge(flow["normed"], n * (BODY // 2) + (u // U) * T + TH)
                    if kind == "v0":
                        if u // U == 0:
                            e.wait_ge(loaded["w1"], n * PAIR_DMA + PAIR_DMA)
                        else:
                            e.wait_ge(loaded["w0"], n * PAIR_DMA + 2 * PAIR_DMA)
                    pe_job(e, j0 + k, kind, buf)
            if tail:
                values(BODY - 1, g0 + BODY - 1, hi0 + high_before(BODY - 1), n * (BODY // 2) + T * 2 - 1, T * 2 - 1)
                e.wait_ge(flow["normed"], n * (BODY // 2) + 2 * T)
                pe_job(e, j0 + y1_number(1, tail), "Y1", 1)

        e.wait_ge(loaded["w0"], PAIR_DMA)
        for n, (kind, ps) in enumerate(first_jobs):
            pe_job(e, n, kind, 0, ps)
        e.wait_ge(flow["job_read"], FIRST_JOBS)
        e.wait_ge(loaded["keys0"], KEY_DMA)
        scores(0)
        scores(1)
        steps(0, 0, 2, False)
        with e.Fori(0, TURNS - 1) as n:
            steps(n, 2, BODY + 2, False)
        steps(TURNS - 1, 2, BODY, True)

    def dve_pairs(e):
        def maximum(u, g):
            _, i, _, par = unit(u)
            flat = score_tiles[par][:, :, :].rearrange("p a n -> p (a n)")
            e.wait_ge(flow["scores_done"], g + 1)
            nc.vector.tensor_reduce(neg_max[:, u % 4:u % 4 + 1], flat[:, 0:(i + 1) * P], axis=AX_X, op=ALU.max,
                                    negate=True).then_inc(flow["max_done"], 1)

        def copy_low(u, g):
            _, i, _, par = unit(u)
            w = min(4, i + 1) * P
            e.wait_ge(flow["turned_low"], g + 1)
            nc.vector.tensor_copy(probT[par][:, 0:w], turned_bank[0][:, 0:w]).then_inc(flow["copied_low"], 1)

        def norm(u, g, tiles):
            _, i, _, _ = unit(u)
            k = (u - 1) % 8
            e.wait_ge(flow["exp_done"], g + 1)
            nc.vector.reciprocal(rec[:, k:k + 2], row_sum[:, k:k + 2]).then_inc(flow["inverted"], 1)
            e.wait_ge(flow["values_done"], g + 1)
            e.wait_ge(flow["inverted"], tiles)
            nc.vector.tensor_tensor(y_t[:, i, :].rearrange("p (a n) -> p a n", a=2),
                                    value_bank[:, 0:P].rearrange("p (a n) -> p a n", a=2),
                                    rec[:, k:k + 2].unsqueeze(2).to_broadcast([P, 2, HD0]),
                                    op=ALU.mult).then_inc(flow["normed"], 1)

        def steps(n, first, end, tail):
            g0 = e.snap(n * BODY) if not isinstance(n, int) else n * BODY
            for u in range(first, end):
                copy_low(u, g0 + u)
                if u + 2 < BODY or not tail:
                    maximum(u + 2, g0 + u + 2)
                if u % 2 == 0 and u > 0:
                    norm(u - 1, g0 + u - 1, n * (BODY // 2) + u // 2)
                job = jobs_at(u - 1, tail) if u else None
                if job:
                    dve_job(e, job[1], job[2], n * 8 + 4 + job[3])
            if tail:
                norm(BODY - 1, g0 + BODY - 1, n * (BODY // 2) + BODY // 2)

        for n, (kind, ps) in enumerate(first_jobs):
            dve_job(e, kind, 0, n + 1, ps)
        maximum(0, 0)
        maximum(1, 1)
        steps(0, 0, 2, False)
        with e.Fori(0, TURNS - 1) as n:
            steps(n, 2, BODY + 2, False)
        steps(TURNS - 1, 2, BODY, True)


    def act_pairs(e):
        def exponential(u, g):
            _, i, _, par = unit(u)
            w = (i + 1) * P
            flat = score_tiles[par][:, :, :].rearrange("p a n -> p (a n)")
            e.wait_ge(flow["max_done"], g + 1)
            nc.scalar.activation(prob[par][:, 0:w], flat[:, 0:w], ACT.Exp, bias=neg_max[:, u % 4:u % 4 + 1],
                                 accum_out=row_sum[:, u % 8:u % 8 + 1]).then_inc(flow["exp_done"], 1)

        def copy_high(u, high):
            _, i, _, par = unit(u)
            w = (i - 3) * P
            e.wait_ge(flow["turned_high"], high + 1)
            nc.scalar.copy(probT[par][:, 4 * P:4 * P + w], turned_bank[1][:, 0:w]).then_inc(flow["copied_high"], 1)

        def steps(n, first, end, tail):
            g0 = e.snap(n * BODY) if not isinstance(n, int) else n * BODY
            hi0 = n * (4 * HIGH)
            j0 = n * (2 * JOBS) + FIRST_JOBS
            for u in range(first, end):
                if unit(u)[1] >= 4:
                    copy_high(u, hi0 + high_before(u))
                if u + 2 < BODY or not tail:
                    exponential(u + 2, g0 + u + 2)
                if u > 1 and u % U == 1:
                    act_job(e, j0 + y1_number(u // U - 1, tail), "Y1", u // U - 1, n * 2 + u // U - 1)
                job = jobs_at(u, tail)
                if job:
                    k, kind, buf, splits = job
                    act_job(e, j0 + k, kind, buf, n * 2 + u // U)
            if tail:
                act_job(e, j0 + y1_number(1, tail), "Y1", 1, n * 2 + 1)

        for n, (kind, ps) in enumerate(first_jobs):
            if kind == "v0":
                e.wait_ge(flow["job_read"], n)
            act_job(e, n, kind, 0, 0, ps)
        exponential(0, 0)
        exponential(1, 1)
        steps(0, 0, 2, False)
        with e.Fori(0, TURNS - 1) as n:
            steps(n, 2, BODY + 2, False)
        steps(TURNS - 1, 2, BODY, True)

    def sp_pairs(e):
        load_pair(e, 0, 0, loaded["w0"])
        load_pair(e, 1, P, loaded["w1"])
        e.wait_ge(flow["job_read"], 2)
        double_keys(e, 0)
        with e.Fori(0, TURNS - 1) as n:
            j0 = n * (2 * JOBS) + FIRST_JOBS
            even, odd = e.snap(n * 2 * P + 2 * P), e.snap(n * 2 * P + 3 * P)
            e.wait_ge(flow["job_done"], j0)
            load_pair(e, 0, even, loaded["w0"])
            e.wait_ge(flow["job_read"], j0 + 4)
            double_keys(e, 1)
            e.wait_ge(flow["job_done"], j0 + JOBS - 1)
            load_pair(e, 1, odd, loaded["w1"])
            e.wait_ge(flow["job_read"], j0 + JOBS + 4)
            double_keys(e, 0)
        e.wait_ge(flow["job_read"], (TURNS - 1) * 2 * JOBS + FIRST_JOBS + 4)
        double_keys(e, 1)

    JOBS_ALL = FIRST_JOBS + (TURNS - 1) * 2 * JOBS + JOBS + 2
    UNITS_ALL = TURNS * BODY
    PAIRS_DONE = [(flow["job_read"], JOBS_ALL), (flow["normed"], UNITS_ALL // 2), (flow["copied_low"], UNITS_ALL),
                  (flow["exp_done"], UNITS_ALL), (flow["copied_high"], TURNS * 4 * HIGH)]

    sp.do(sp_pairs)
    pe.do(pe_pairs, *before_pairs, *lat_done)
    dve.do(dve_pairs)
    act.do(act_pairs)

    banks = Banks(all_banks)
    prior_x = [None] * 4

    def residual(t, ps, done, gate, bias=None, extra=None):
        a = tmp[:, t % 4, :]
        if bias is None:
            read = last = dve.do(lambda e: nc.vector.tensor_tensor(a, ps, gate, op=ALU.mult), done, prior_x[t % 4],
                                 ROWS, X_LOADED)
        else:
            read = last = dve.do(lambda e: nc.vector.tensor_tensor(a, ps, bias, op=ALU.add), done, prior_x[t % 4])
            if extra is not None:
                last = dve.do(lambda e: nc.vector.tensor_tensor(a, a, extra, op=ALU.add), last)
            last = dve.do(lambda e: nc.vector.tensor_tensor(a, a, gate, op=ALU.mult), last)
        wrote = dve.do(lambda e: nc.vector.tensor_tensor(x[:, t, :], x[:, t, :], a, op=ALU.add), last)
        prior_x[t % 4] = wrote
        return read, wrote

    def to_residual(half, pieces, gate, *deps, bias=None, extra=None):
        wrote = []
        for t in tiles_of(half):
            i, ps, reader = banks.take()
            done = pe.do(product(ps[:, 0:D], pieces(slice(t * P, (t + 1) * P))), reader, *deps)
            read, w = residual(t, ps[:, 0:D], done, gate, bias, extra and extra(t))
            banks.read_by(i, read)
            wrote.append(w)
        return wrote

    def blocks(m_count, pieces, half, rows_, evacuate, *deps):
        cols, res = slice(half * HW, (half + 1) * HW), []
        for m in range(m_count):
            i, ps, reader = banks.take()
            done = pe.do(product(ps[0:rows_, :], pieces(m, cols)), reader, *deps)
            step = evacuate(m, cols, ps[0:rows_, :], done)
            banks.read_by(i, step)
            res.append(step)
        return res

    def gelu_into(dst, bias):
        return lambda m, cols, ps, done: act.do(lambda e: nc.scalar.activation(
            dst[:, m, cols], ps, ACT.Gelu_apprx_tanh, bias=bias[:, m:m + 1]), done)

    def affine_rows(half, normed, scale, shift):
        ts = list(tiles_of(half))
        scaled = [dve.do(lambda e, t=t: nc.vector.tensor_tensor(h[:, t, :], xn[:, t, :], scale, op=ALU.mult), n)
                  for t, n in zip(ts, normed)]
        return [dve.do(lambda e, t=t: nc.vector.tensor_tensor(h[:, t, :], h[:, t, :], shift, op=ALU.add), s_)
                for t, s_ in zip(ts, scaled)]

    def head_outputs(half):
        wrote = to_residual(half, lambda tok: [(yT[:, j, tok], wout[:, j, :]) for j in range(PAIRS)], mod_rows[:, 0, :],
                            *PAIRS_DONE, WEIGHTS)
        return normalise(x, half, wrote, EPS)

    begin(WORK)
    hT2 = part("hT2", [P, C, S])
    rankT = part("rankT", [P, S])
    hid = part("hid", [P, FM, S])
    rank2T = part("rank2T", [P, S])

    def feed_low(half, normed):
        turned = turn(xn, half, normed, hT2, scale=mod_cols[:, 3, :], bias=mod_cols[:, 2, :])
        low = blocks(1, lambda m, cols: [(u1[:, c, :], hT2[:, c, cols]) for c in range(C)], half, RF,
                     lambda m, cols, ps, done: act.do(lambda e: nc.scalar.copy(rankT[0:RF, cols], ps), done), turned)
        wide = blocks(FM, lambda m, cols: [(v1[:, m * P:(m + 1) * P], rankT[0:RF, cols])], half, P,
                      gelu_into(hid, b1_0), *low)
        low2 = blocks(1, lambda m, cols: [(u2[:, j, :], hid[:, j, cols]) for j in range(FM)], half, RF,
                      lambda m, cols, ps, done: act.do(lambda e: nc.scalar.copy(rank2T[0:RF, cols], ps), done), *wide)
        return to_residual(half, lambda tok: [(rank2T[0:RF, tok], v2[:, :])], mod_rows[:, 1, :], *low2, bias=b2_0[:, :])

    begin(OVERLAY)
    q_spread = [part(f"q_spread{k}", [P, C, HC, P]) for k in range(2)]
    begin(WORK)
    nT = part("nT", [P, C, S])
    qT = part("qT", [P, C, S])
    k_tok = part("k_tok", [P, T, D])
    v_tok = part("v_tok", [P, T, HEADS1, VW])
    kT = part("kT", [P, C, S])
    am = [part(f"am{k}", [P, HEADS1, P]) for k in range(2)]
    yT2, y_rows = nT, xn

    def attention_norms(half, ready):
        h_done = affine_rows(half, normalise(x, half, ready, EPS), mod_rows[:, 3, :], mod_rows[:, 2, :])
        return normalise(h, half, h_done, EPS_LN)

    def phi(dst, src):
        return lambda e: nc.vector.tensor_scalar(dst, src, 0.0, EPS_PHI, op0=ALU.max, op1=ALU.add)

    ones_set = []
    q_done, v_done, kT_done = {}, {}, {}

    def attention_inputs(half, normed):
        turned = turn(xn, half, normed, nT, scale=ln_cols[:, 0, :], bias=ln_cols[:, 1, :])
        if half == 0:
            ones_set.append(dve.do(lambda e: nc.vector.memset(v_tok[:, :, :, HD1:VW], 1.0), turned))
        k_done = []
        for t in tiles_of(half):
            i, ps, reader = banks.take()
            done = pe.do(product(ps[:, :], [(nT[:, c, t * P:(t + 1) * P], wkv1[:, c, :]) for c in range(C)]), reader, turned)
            k_done.append(dve.do(phi(k_tok[:, t, :], ps[:, 0:D]), done))
            v_done[t] = act.do(lambda e, t=t, ps=ps: nc.scalar.copy(
                v_tok[:, t, :, 0:HD1], ps[:, D:2 * D].rearrange("p (h n) -> p h n", h=HEADS1)), k_done[-1], *ones_set)
            banks.read_by(i, v_done[t])
        q_done[half] = blocks(C, lambda m, cols: [(wq1[:, c, m * P:(m + 1) * P], nT[:, c, cols]) for c in range(C)],
                              half, P, lambda m, cols, ps, done: dve.do(phi(qT[:, m, cols], ps), done), turned)
        kT_done[half] = turn(k_tok, half, k_done, kT)

    def spread_queries(t, used):
        half, tok, spread = t // TH, slice(t * P, (t + 1) * P), q_spread[t % 2]
        ready = [None, None]
        ready[0] = dve.do(lambda e: nc.vector.tensor_tensor(
            spread[:, 0, :, :], qT[:, 0, tok].unsqueeze(1).to_broadcast([P, HC, P]),
            head_mask[:, :].unsqueeze(2).to_broadcast([P, HC, P]), op=ALU.mult), q_done[half][0], used[t % 2])
        for hh in range(HC):
            ready[1] = act.do(lambda e, hh=hh: nc.scalar.mul(spread[:, 1, hh, :], qT[:, 1, tok], head_mask[:, hh:hh + 1]),
                              q_done[half][1], used[t % 2])
        return ready

    def tile_scores(t, ready, used):
        half, tok, spread = t // TH, slice(t * P, (t + 1) * P), q_spread[t % 2]
        masked = []
        for c in range(C):
            for quad in range(2):
                i, ps, reader = banks.take()
                done = pe.do(lambda e, ps=ps, c=c, quad=quad: nc.tensor.matmul(
                    ps, kT[:, c, tok], spread[:, c, quad * 4:quad * 4 + 4, :], start=True, stop=True),
                    reader, ready[c], kT_done[half])
                dst = am[t % 2][:, c * HC + quad * 4:c * HC + quad * 4 + 4, :]
                step = dve.do(lambda e, dst=dst, ps=ps: nc.vector.tensor_tensor(
                    dst, ps.rearrange("p (h n) -> p h n", h=4), tril[:, :].unsqueeze(1).to_broadcast([P, 4, P]),
                    op=ALU.mult), done, am_used[t % 2])
                banks.read_by(i, step)
                masked.append(step)
        used[t % 2] = done
        return masked

    am_used, y_done = [None, None], []

    def tile_outputs(t, masked, state_read):
        half, tok = t // TH, slice(t * P, (t + 1) * P)
        i, ps, reader = banks.take()

        def numerators(e):
            for c in range(C):
                nc.tensor.matmul(ps[:, c * HC * VW:(c + 1) * HC * VW], qT[:, c, tok], kv_state[:, c, :],
                                 start=c == 0, stop=False, skip_group_check=True)
            for hd in range(HEADS1):
                last = nc.tensor.matmul(ps[:, hd * VW:(hd + 1) * VW], am[t % 2][:, hd, :], v_tok[:, t, hd, :],
                                        start=False, stop=hd == HEADS1 - 1, skip_group_check=True)
            return last

        done = pe.do(numerators, reader, state_read, *masked, v_done[t])
        am_used[t % 2] = done
        if t < T - 1:
            def update(e):
                for c in range(C):
                    last = nc.tensor.matmul(state_bank[:, c * HC * VW:(c + 1) * HC * VW],
                                            k_tok[:, t, c * P:(c + 1) * P],
                                            v_tok[:, t, c * HC:(c + 1) * HC, :].rearrange("p h v -> p (h v)"),
                                            start=t == 0 and c == 0, stop=t == T - 2 and c == C - 1,
                                            skip_group_check=True)
                return last

            updated = pe.do(update, state_reader, state_read)
        view = ps[:, 0:HEADS1 * VW].rearrange("p (h v) -> p h v", h=HEADS1)
        inverse = dve.do(lambda e: nc.vector.reciprocal(rec[:, :], view[:, :, HD1]), done,
                         y_done[-1] if y_done else None)
        y_done.append(dve.do(lambda e: nc.vector.tensor_tensor(
            y_rows[:, t, :].rearrange("p (h n) -> p h n", h=HEADS1), view[:, :, 0:HD1],
            rec[:, :].unsqueeze(2).to_broadcast([P, HEADS1, HD1]), op=ALU.mult), inverse))
        banks.read_by(i, y_done[-1])
        if t < T - 1:
            return dve.do(lambda e: nc.vector.tensor_tensor(
                kv_state[:, :, :], state_bank[:, 0:HEADS1 * VW].rearrange("p (c n) -> p c n", c=C),
                kv_mask[:, :, :].rearrange("p h v -> p (h v)").unsqueeze(1).to_broadcast([P, C, HC * VW]),
                op=ALU.mult), updated)
        return state_read

    def attention_output(half):
        turned = turn(y_rows, half, y_done[half * TH:(half + 1) * TH], yT2)
        wrote = []
        for t in tiles_of(half):
            i, ps, reader = banks.take()
            done = pe.do(product(ps[:, 0:D], [(yT2[:, c, t * P:(t + 1) * P], wo1[:, c, :]) for c in range(C)]), reader, turned)
            wrote.append(dve.do(lambda e, t=t, ps=ps: nc.vector.tensor_tensor(h[:, t, :], ps[:, 0:D], h[:, t, :],
                                                                              op=ALU.add), done))
            banks.read_by(i, wrote[-1])
        return normalise(h, half, wrote, EPS_LN)

    begin(WORK)
    mT = part("mT", [P, C, S])
    hid1 = part("hid1", [P, FM, S])

    def mlp(half, normed):
        turned = turn(xn, half, normed, mT, scale=ln_cols[:, 2, :], bias=ln_cols[:, 3, :])
        wide = blocks(FM, lambda m, cols: [(w1[:, c, m * P:(m + 1) * P], mT[:, c, cols]) for c in range(C)], half, P,
                      gelu_into(hid1, b1_1), turned)
        return to_residual(half, lambda tok: [(hid1[:, m, tok], w2[:, m, :]) for m in range(FM)], mod_rows[:, 4, :],
                           *wide, bias=b2_1[:, :], extra=lambda t: h[:, t, :])

    begin(OVERLAY)
    f2 = part("f2", [P, EP, D])
    f1 = part("f1", [P, C, ES, EF])
    begin(WORK)
    sel = part("sel", [P, C, ES, G])
    begin(WORK)
    inter_t = part("inter_t", [P, C, G, ES])
    hT3 = part("hT3", [P, C, S])
    begin(WORK + 8 * S)
    next_x = part("next_x", [P, T, D])
    permT = part("permT", [P, S])
    blockT = part("blockT", [P, S])
    perm = [part(f"perm{k}", [P, GT, ES]) for k in range(2)]
    inter = [part(f"inter{k}", [P, 4, D]) for k in range(2)]
    logits = inter[0][:, :, :].rearrange("p k n -> p (k n)")
    before_relu = xn[:, :, :].rearrange("p t n -> p (t n)").rearrange("p (q g) -> p q g", q=EP)
    begin(FIRST)
    inner = part("inner", [P, EP, 2, G])
    f1_dram = I["L1_ffn_f1"].rearrange("(c p) e s f -> c p (e s) f", p=P)
    f2_dram = I["L1_ffn_f2"].rearrange("e s f d -> (e s) f d").rearrange("(q two) f d -> two f q d", two=2)

    def load_f1(e):
        for c in range(C):
            last = e.dma_start(f1[:, c, :, :], f1_dram[c]).then_inc(loaded["f1"], 16)
        return last

    def load_f2(e):
        for k in range(2):
            last = e.dma_start(f2[k * EF:(k + 1) * EF, :, :], f2_dram[k]).then_inc(loaded["f2"], 16)
        return last

    def slot_norms(half, ready):
        return affine_rows(half, normalise(x, half, ready, EPS), mod_rows[:, 6, :], mod_rows[:, 5, :])

    perm_done, block_done = [], []

    def choices(half, h_done):
        turned = turn(h, half, h_done, hT3)
        gs = slice(half * G // NH, (half + 1) * G // NH)
        cols = slice(half * HW, (half + 1) * HW)
        v3 = logits[:, cols].rearrange("p (g t) -> p g t", t=NE)
        lg = blocks(1, lambda m, cols: [(ctrl[:, c, :], hT3[:, c, cols]) for c in range(C)], half, P,
                    lambda m, cols, ps, done: dve.do(lambda e: nc.vector.tensor_tensor(
                        v3, ps.rearrange("p (g t) -> p g t", t=NE),
                        tie[:, :].unsqueeze(1).to_broadcast([P, G // NH, NE]), op=ALU.add), done), turned)
        top = dve.do(lambda e: nc.vector.tensor_reduce(logit_max[:, gs], v3, axis=AX_X, op=ALU.max), *lg)
        perm_done.append(dve.do(lambda e: nc.vector.tensor_tensor(
            permT[:, cols].rearrange("p (g t) -> p g t", t=NE), v3,
            logit_max[:, gs].unsqueeze(2).to_broadcast([P, G // NH, NE]), op=ALU.is_equal), top))
        for k in range(2):
            view = [a[:, cols].rearrange("p (q two t) -> p q two t", two=2, t=NE)[:, :, k, :] for a in (blockT, permT)]
            step = dve.do(lambda e, view=view, k=k: nc.vector.tensor_scalar(
                view[0], view[1], half_mask[:, k:k + 1], None, op0=ALU.mult), perm_done[-1])
        block_done.append(step)
        return lg[-1]

    sp.do(load_f1, *PAIRS_DONE)
    low_norms = [head_outputs(0), head_outputs(1)]
    ready = feed_low(0, low_norms[0])
    attn_norms = [attention_norms(0, ready)]
    ready = feed_low(1, low_norms[1])
    attn_norms.append(attention_norms(1, ready))
    state_bank, state_reader = banks.tiles[7], banks.readers[7]
    banks7 = Banks(all_banks[0:7])
    banks7.readers, banks7.at = banks.readers[0:7], (banks.at if banks.at < 7 else 6)
    banks = banks7
    attention_inputs(0, attn_norms[0])
    state = dve.do(lambda e: nc.vector.memset(kv_state[:, :, :], 0.0), *ones_set)
    spread_used = [None, None]
    spread = {0: spread_queries(0, spread_used), 1: spread_queries(1, spread_used)}
    masked = tile_scores(0, spread[0], spread_used)
    mlp_norms = []
    for t in range(T):
        if t + 2 == TH:
            attention_inputs(1, attn_norms[1])
        if t + 2 < T:
            spread[t + 2] = spread_queries(t + 2, spread_used)
        ahead = tile_scores(t + 1, spread[t + 1], spread_used) if t + 1 < T else None
        state = tile_outputs(t, masked, state)
        masked = ahead
        if t == TH:
            mlp_norms.append(attention_output(0))
    sp.do(load_f2, spread_used[(T - 1) % 2])
    mlp_norms.append(attention_output(1))
    readers = banks.readers + [state]
    banks = Banks(all_banks)
    banks.readers = readers
    ready = mlp(0, mlp_norms[0])
    h_done = [slot_norms(0, ready)]
    ready = mlp(1, mlp_norms[1])
    h_done.append(slot_norms(1, ready))
    choices(0, h_done[0])
    turned_read = choices(1, h_done[1])

    def load_next(e):
        nxt = e.snap((b_reg["b"] + 1) % NB)
        load_x(e, next_x, nxt)
        return load_columns(e, nxt)

    sp.do(load_next, turned_read)

    spread_reader = [None, None]
    sel_done = []

    def spread_choices(t):
        i, ps, reader = banks.take()
        done = pe.do(lambda e: nc.tensor.transpose(ps[:, 0:ES], permT[0:ES, t * P:(t + 1) * P], ident[0:ES, 0:ES]),
                     reader, perm_done[t // TH])
        step = dve.do(lambda e: nc.vector.tensor_tensor(
            perm[t % 2][:, :, :], ps[:, 0:ES].unsqueeze(1).to_broadcast([P, GT, ES]),
            head_mask[:, :].unsqueeze(2).to_broadcast([P, GT, ES]), op=ALU.mult), done, spread_reader[t % 2])
        banks.read_by(i, step)
        return step

    spread_ready = spread_choices(0)
    for t in range(T):
        step = spread_ready
        if t + 1 < T:
            spread_ready = spread_choices(t + 1)
        for c in range(C):
            i, ps, reader = banks.take()
            done = pe.do(product(ps, [(h[:, t, c * P:(c + 1) * P], perm[t % 2][:, :, :].rearrange("p g s -> p (g s)"))]), reader, step)
            spread_reader[t % 2] = done
            o = sel[:, c, :, t * GT:(t + 1) * GT].rearrange("p s g -> p g s")
            src = ps.rearrange("p (g s) -> p g s", g=GT)
            if c == 0:
                copy = act.do(lambda e, o=o, src=src: nc.scalar.copy(o, src), done)
            else:
                copy = dve.do(lambda e, o=o, src=src: nc.vector.tensor_copy(o, src), done)
            banks.read_by(i, copy)
            sel_done.append(copy)

    inner_done = []
    for blk in range(4):
        i, ps, reader = banks.take()

        def first_product(e, blk=blk, ps=ps):
            for s in range(blk * 16, blk * 16 + 16):
                o = ps[(s % 2) * EF:(s % 2 + 1) * EF, (s // 2 - blk * 8) * G:(s // 2 - blk * 8 + 1) * G]
                for c in range(C):
                    last = nc.tensor.matmul(o, f1[:, c, s, :], sel[:, c, s, :], start=c == 0, stop=c == C - 1)
            return last

        done = pe.do(first_product, reader, *(sel_done + [(loaded["f1"], 32)] if blk == 0 else []))
        dst = before_relu[:, blk * 8:blk * 8 + 8, :]
        biased = dve.do(lambda e, ps=ps, dst=dst, blk=blk: nc.vector.tensor_tensor(
            dst, ps.rearrange("p (q g) -> p q g", q=8),
            fbias[:, blk * 8:blk * 8 + 8].unsqueeze(2).to_broadcast([P, 8, G]), op=ALU.add), done)
        banks.read_by(i, biased)
        for k in range(2):
            relu = act.do(lambda e, dst=dst, blk=blk, k=k: nc.scalar.activation(
                inner[:, blk * 8:blk * 8 + 8, k, :], dst, ACT.Relu, scale=half_mask[:, k:k + 1]), biased)
        inner_done.append(relu)

    inter_t_done = []
    for blk in range(4):
        for c in range(C):
            for quad in range(2):
                i, ps, reader = banks.take()
                pairs = [blk * 8 + quad * 4 + k for k in range(4)]

                def second_product(e, ps=ps, c=c, pairs=pairs):
                    for k, q in enumerate(pairs):
                        last = nc.tensor.matmul(ps[:, k * P:(k + 1) * P], f2[:, q, c * P:(c + 1) * P],
                                                inner[:, q, :, :].rearrange("p two g -> p (two g)"), start=True, stop=True)
                    return last

                done = pe.do(second_product, reader, inner_done[blk], (loaded["f2"], 32))
                o = inter_t[:, c, :, 2 * pairs[0]:2 * pairs[0] + 8].rearrange("p g s -> p s g")
                src = ps.rearrange("p (s g) -> p s g", s=8)
                if quad:
                    copy = act.do(lambda e, o=o, src=src: nc.scalar.copy(o, src), done, inner_done[3])
                else:
                    copy = dve.do(lambda e, o=o, src=src: nc.vector.tensor_copy(o, src), done, inner_done[3])
                banks.read_by(i, copy)
                inter_t_done.append(copy)
        if blk in (1, 2):
            norm_apply(next_x, blk - 1, next_norm)
        if blk < 2:
            next_norm = norm_stats(next_x, blk, [NEXT_X] * TH, EPS)

    inter_reader = [None, None]
    finals = []

    def slot_rows(t):
        copies = []
        for two in range(2):
            i, ps, reader = banks.take()

            def turn_back(e, two=two, ps=ps):
                for kk in range(2):
                    g = t * GT + (two * 2 + kk) * 2
                    for c in range(C):
                        last = nc.tensor.transpose(ps[:, kk * D + c * P:kk * D + (c + 1) * P],
                                                   inter_t[:, c, g:g + 2, :].rearrange("p g s -> p (g s)"), ident[:, :])
                return last

            done = pe.do(turn_back, reader, *(inter_t_done if t == 0 and two == 0 else []))
            dst = inter[t % 2][:, two * 2:two * 2 + 2, :]
            src = ps.rearrange("p (k n) -> p k n", k=2)
            if two:
                copies.append(act.do(lambda e, dst=dst, src=src: nc.scalar.copy(dst, src), done, inter_reader[t % 2]))
            else:
                copies.append(dve.do(lambda e, dst=dst, src=src: nc.vector.tensor_copy(dst, src), done, inter_reader[t % 2]))
            banks.read_by(i, copies[-1])
        return copies

    rows_ready = slot_rows(0)
    for t in range(T):
        copies = rows_ready
        if t + 1 < T:
            rows_ready = slot_rows(t + 1)
        i, ps, reader = banks.take()

        def combine(e, t=t, ps=ps):
            for kk in range(4):
                lo = t * P + kk * 32
                last = nc.tensor.matmul(ps[kk * 32:(kk + 1) * 32, 0:D], blockT[:, lo:lo + 32], inter[t % 2][:, kk, :],
                                        start=True, stop=True)
            return last

        done = pe.do(combine, reader, *copies, block_done[t // TH])
        inter_reader[t % 2] = done
        read, wrote = residual(t, ps[:, 0:D], done, mod_rows[:, 7, :])
        banks.read_by(i, read)
        finals.append(wrote)
        if t % 2:
            sp.do(lambda e, t=t: e.dma_start(x_out[b_reg["b"]][:, t - 1:t + 1, :], x[:, t - 1:t + 1, :]
                                             ).then_inc(stored, 16), wrote)

    sp.do(lambda e: e.wait_ge(loaded["columns"], COLUMN_DMA))
    for ln in lane.values():
        ln.number()

    cleared = [ln.sem for ln in lane.values()] + list(flow.values())
    cleared += [loaded[k] for k in ("x", "next_x", "columns", "rows", "f1", "f2", "w0", "w1", "keys0", "keys1")]
    with nc.Fori(0, NB) as b:
        b_reg["b"] = b
        with nc.Block() as block:
            block.sync(sp.emit)
            block.scalar(act.emit)
            block.vector(dve.emit)
            block.tensor(pe.emit)
            block.gpsimd(pool.emit)
        for s in cleared:
            nc.sync.sem_clear(s)
        nc.all_engine_barrier()
    nc.sync.wait_ge(stored, NB * STORES + 16)
    ctx.close()


_INS = ["L0_attn_x", "L0_attn_w_kv_down", "L0_attn_w_kv_up", "L0_attn_w_q", "L0_attn_w_out", "L0_ffn_U1", "L0_ffn_V1",
        "L0_ffn_b1", "L0_ffn_U2", "L0_ffn_V2", "L0_ffn_b2", "L0_c", "L0_wmod", "L1_attn_ln1_scale", "L1_attn_ln1_bias",
        "L1_attn_wq", "L1_attn_wk", "L1_attn_wv", "L1_attn_wo", "L1_attn_ln2_scale", "L1_attn_ln2_bias", "L1_attn_w1",
        "L1_attn_b1", "L1_attn_w2", "L1_attn_b2", "L1_ffn_controller", "L1_ffn_f1", "L1_ffn_f2", "L1_ffn_bias", "L1_c",
        "L1_wmod"]


def kernel(**inputs):
    import concourse.bacc as bacc
    from concourse.bass_utils import run_bass_kernel_spmd

    nc = bacc.Bacc("TRN2", target_bir_lowering=False, num_devices=1)
    arrays, args = {}, {}
    for name in _INS:
        arrays[name] = np.ascontiguousarray(inputs[name])
    arrays["tie"] = np.linspace(0.0, 1e-6, NE, dtype=np.float32)
    for name, a in arrays.items():
        args[name] = nc.dram_tensor("in_" + name, a.shape, mybir.dt.from_np(a.dtype), kind="ExternalInput").ap()
    out = nc.dram_tensor("out", (NB, S, D), F32, kind="ExternalOutput").ap()
    build(nc, args, out)
    r = run_bass_kernel_spmd(nc, [{"in_" + name: a for name, a in arrays.items()}], core_ids=[0])
    return r.results[0]["out"]
```

```python
import numpy as np
import concourse.bass as bass
from concourse import mybir
from contextlib import ExitStack
from itertools import islice

F32 = mybir.dt.float32
F32R = mybir.dt.float32r
BF16 = mybir.dt.bfloat16
ACT = mybir.ActivationFunctionType
ALU = mybir.AluOpType
AX_X = mybir.AxisListType.X

P = 128
NB = 4
S = 1024
D = 256
C = D // P
T = S // P
NH = 2
HW = S // NH
TH = T // NH
HD0 = 64
HEADS0 = 16
PAIRS = HEADS0 // 2
RK = 128
FF = 1024
FM = FF // P
RF = 64
U = 2 * T
EPS = 1e-5
HEADS1 = 16
HD1 = 16
HC = HEADS1 // C
VW = HD1 + 1
EPS_LN = 1e-6
EPS_PHI = 1e-3
NE = 16
ES = 64
EF = 64
G = S // NE
GT = P // NE
EP = ES // 2
NEG = -1e30


class Lane:

    def __init__(self, sem):
        self.sem, self.steps = sem, []

    def do(self, emit, *after):
        step = Step(self, emit, [a for a in after if a is not None])
        self.steps.append(step)
        return step

    def number(self):
        n = 0
        for s in self.steps:
            if s.needed:
                n += 1
                s.value = n

    def emit(self, engine):
        seen = {}
        for s in self.steps:
            for a in s.after:
                sem, value = (a.lane.sem, a.value) if isinstance(a, Step) else a
                if seen.get(sem.name, 0) < value:
                    engine.wait_ge(sem, value)
                    seen[sem.name] = value
            last = s.emit(engine)
            if s.needed:
                last.then_inc(self.sem, 1)


class Step:
    def __init__(self, lane, emit, after):
        self.lane, self.emit, self.after = lane, emit, after
        self.needed, self.value = False, 0
        for a in after:
            if isinstance(a, Step):
                a.needed = True


class Banks:

    def __init__(self, tiles):
        self.tiles, self.readers, self.at = tiles, [None] * len(tiles), -1

    def take(self):
        self.at = (self.at + 1) % len(self.tiles)
        return self.at, self.tiles[self.at], self.readers[self.at]

    def read_by(self, index, step):
        self.readers[index] = step


def build(nc, I, out):
    ctx = ExitStack()
    ctx.enter_context(nc.allow_non_contiguous_dma(reason="bias columns and broadcast rows"))

    def sb(name, shape, dt=F32):
        return ctx.enter_context(nc.sbuf_tensor(name, shape, dt))

    def semaphore(name):
        return ctx.enter_context(nc.semaphore(name))

    bank = [ctx.enter_context(nc.psum_tensor(f"bank{i}", [P, 512], F32)) for i in range(4)]
    score_tiles = [ctx.enter_context(nc.psum_tensor(f"scores{i}", [P, 2, 512], F32)) for i in range(2)]
    all_banks = [b[:, :] for b in bank] + [s[:, i, :] for s in score_tiles for i in range(2)]

    wout = sb("wout", [P, PAIRS, D])
    u1 = sb("u1", [P, C, 2 * RF])
    v1_split = sb("v1_split", [P, FF], F32R)
    u2, v2 = sb("u2", [P, FM, RF]), sb("v2", [RF, D])
    wdown = sb("wdown", [P, C, RK])
    wq1, wkv1, wo1 = sb("wq1", [P, C, D]), sb("wkv1", [P, C, 2 * D]), sb("wo1", [P, C, D])
    w1, w2 = sb("w1", [P, C, FF]), sb("w2", [P, FM, D])
    ctrl = sb("ctrl", [P, C, 2 * ES])
    b1_0, b1_1 = sb("b1_0", [P, FM]), sb("b1_1", [P, FM])
    b2_0, b2_1 = sb("b2_0", [P, D]), sb("b2_1", [P, D])
    ln_cols = sb("ln_cols", [P, 4, C])
    fbias = sb("fbias", [P, EP])
    tie = sb("tie", [P, NE])
    ident = sb("ident", [P, P])
    ident_b = sb("ident_b", [P, P], BF16)
    neg_b = sb("neg_b", [P, P], BF16)
    tril = sb("tril", [P, P])
    head_mask = sb("head_mask", [P, HC])
    kv_mask = sb("kv_mask", [P, HC, VW])
    half_mask = sb("half_mask", [P, 2])
    minus_half = sb("minus_half", [P, T])
    x = sb("x", [P, T, D])
    h = sb("h", [P, T, D])
    xn = sb("xn", [P, T, D])
    mod_rows = sb("mod_rows", [P, 8, D])
    mod_cols = sb("mod_cols", [P, 4, C])
    tmp = sb("tmp", [P, 3, D])
    stats = sb("stats", [P, T, 6])
    mv = sb("mv", [P, T, 2])
    rstd = sb("rstd", [P, T])
    neg_max = sb("neg_max", [P, 4])
    row_sum = sb("row_sum", [P, 8])
    rec = sb("rec", [P, HEADS1])
    logit_max = sb("logit_max", [P, G])
    kv_state = sb("kv_state", [P, C, HC * VW])

    STORES = T // 2 * 16

    SPLIT = 3 * 4 * S
    ROOM = 15 * S
    OVER = 8 * S
    slab_start = nc.sbuf_base
    sb("slab", [P, OVER + 8 * S + ROOM])
    at = [0]

    def begin(where):
        at[0] = where

    def part(name, shape, dt=F32):
        words = int(np.prod(shape[1:]))
        a = nc.alloc_sbuf_tensor_at(name, shape, dt, offset=slab_start + 4 * at[0])
        at[0] += words
        if at[0] > OVER + 8 * S + ROOM:
            raise ValueError("the slab is too small for " + name)
        return a

    OVERLAY, FIRST, WORK = 0, OVER, OVER + 8 * S

    lane = {k: Lane(semaphore(f"{k}_steps")) for k in ("pe", "act", "dve", "pool", "sp")}
    pe, act, dve, pool, sp = (lane[k] for k in ("pe", "act", "dve", "pool", "sp"))
    setup = {k: Lane(semaphore(f"{k}_setup")) for k in ("pe", "act", "dve", "pool", "sp")}
    loaded = {k: semaphore(f"loaded_{k}") for k in (
        "weights", "cond0", "cond1", "v1", "x", "next_x", "columns", "rows", "f1", "f2", "w0", "w1", "first_keys", "keys0", "keys1")}
    stored = semaphore("stored")
    flow = {k: semaphore(k) for k in (
        "scores_done", "max_done", "exp_done", "turned_low", "turned_high", "copied_low", "copied_high",
        "rounded", "values_done", "inverted", "normed", "job_done", "job_read")}
    names = ("pe", "act", "dve", "pool", "sp")

    mod_dram = nc.dram_tensor("mod_scratch", [NB, 2, 6, D], F32, kind="Internal").ap()

    begin(WORK)
    cond = part("cond", [P, 2, C, NB])
    silu = part("silu", [P, 2, C, NB])
    wmod = [part(f"wmod{k}", [P, C, 6 * D]) for k in range(2)]
    mod_sb = part("mod_sb", [P, 2, 6, D])
    v1_raw, v1_high = part("v1_raw", [P, FF]), part("v1_high", [P, FF], F32R)
    gate_a, gate_s = h[:, 0:2, :], h[:, 2:4, :]

    weight_loads = []

    def load(dst, src):
        weight_loads.append((dst, src))

    def rows(w, p=P):
        return w.rearrange("(c p) n -> p c n", p=p)

    load(wdown[:, :, :], rows(I["L0_attn_w_kv_down"]))
    load(wout[:, :, :], rows(I["L0_attn_w_out"]))
    for k in range(2):
        load(u1[:, :, k * RF:(k + 1) * RF], rows(I["L0_ffn_U1"]))
    load(u2[:, :, :], rows(I["L0_ffn_U2"]))
    load(v2[:, :], I["L0_ffn_V2"])
    load(wq1[:, :, :], rows(I["L1_attn_wq"].rearrange("d h m -> d (h m)")))
    load(wkv1[:, :, 0:D], rows(I["L1_attn_wk"].rearrange("d h m -> d (h m)")))
    load(wkv1[:, :, D:2 * D], rows(I["L1_attn_wv"].rearrange("d h m -> d (h m)")))
    load(wo1[:, :, :], rows(I["L1_attn_wo"].rearrange("h m d -> (h m) d")))
    load(w1[:, :, :], rows(I["L1_attn_w1"]))
    load(w2[:, :, :], rows(I["L1_attn_w2"]))
    for k in range(2):
        load(ctrl[:, :, k * ES:(k + 1) * ES], rows(I["L1_ffn_controller"].rearrange("d e s -> d (e s)")))
    load(b1_0[:, :], I["L0_ffn_b1"].rearrange("(m p) -> p m", p=P))
    load(b1_1[:, :], I["L1_attn_b1"].rearrange("(m p) -> p m", p=P))
    load(b2_0[:, :], I["L0_ffn_b2"].partition_broadcast(P))
    load(b2_1[:, :], I["L1_attn_b2"].partition_broadcast(P))
    for k, name in enumerate(("ln1_scale", "ln1_bias", "ln2_scale", "ln2_bias")):
        load(ln_cols[:, k, :], I["L1_attn_" + name].rearrange("(c p) -> p c", p=P))
    slots = I["L1_ffn_bias"].rearrange("e s f -> (e s) f").rearrange("(q two) f -> two f q", two=2)
    for k in range(2):
        load(fbias[k * EF:(k + 1) * EF, :], slots[k])
    load(tie[:, :], I["tie"].partition_broadcast(P))
    cond_loads = [[(cond[:, l, c, :], I[f"L{l}_c"].rearrange("b (c p) -> c p b", p=P)[c]) for c in range(C)]
                  + [(wmod[l][:, :, :], rows(I[f"L{l}_wmod"]))] for l in range(2)]

    s_act, s_dve, s_pe, s_pool = setup["act"], setup["dve"], setup["pe"], setup["pool"]

    x_in = I["L0_attn_x"].rearrange("b (t p) d -> b p t d", p=P)
    x_out = out.rearrange("b (t p) d -> b p t d", p=P)
    b_reg = {}

    def load_x(e, dst, b, sem="next_x"):
        for half in range(NH):
            ts = slice(half * TH, (half + 1) * TH)
            last = e.dma_start(dst[:, ts, :], x_in[b][:, ts, :]).then_inc(loaded[sem], 16)
        return last

    def load_columns(e, b):
        for k, s in enumerate((0, 1, 3, 4)):
            last = e.dma_start(mod_cols[:, k, :], mod_dram[b, 0, s].rearrange("(c p) -> p c", p=P)
                               ).then_inc(loaded["columns"], 16)
        return last

    def load_rows(e):
        b = b_reg["b"]
        for k, s in enumerate((2, 5)):
            e.dma_start(mod_rows[:, k, :], mod_dram[b, 0, s].partition_broadcast(P)).then_inc(loaded["rows"], 16)
        return e.dma_start(mod_rows[:, 2:8, :].rearrange("p s n -> p (s n)"),
                           mod_dram[b, 1].rearrange("s n -> (s n)").partition_broadcast(P)).then_inc(loaded["rows"], 16)

    COLUMN_DMA = 4 * 16
    X_LOADED, NEXT_X = (loaded["x"], NH * 16), (loaded["next_x"], NH * 16)
    ROWS = (loaded["rows"], 16 * 3)

    def tiles_of(half):
        return range(half * TH, (half + 1) * TH)

    def norm_stats(src, half, ready, eps, lanes=(dve, pool), filled=None):
        dve, pool = lanes
        last = None
        for t, r in zip(tiles_of(half), ready):
            s = dve.do(lambda e, t=t: nc.vector.bn_stats(stats[:, t, :], src[:, t, :]), r)
            last = dve.do(lambda e, t=t: nc.vector.bn_aggr(mv[:, t, :], stats[:, t, :]), s)
        ts = slice(half * TH, (half + 1) * TH)
        var = dve.do(lambda e: nc.vector.tensor_scalar(rstd[:, ts], mv[:, ts, 1], eps, None, op0=ALU.add), last)
        return pool.do(lambda e: nc.gpsimd.tensor_tensor(rstd[:, ts], rstd[:, ts], minus_half[:, ts], op=ALU.pow),
                       var, filled)

    def norm_apply(src, half, inv, dve=dve):
        return [dve.do(lambda e, t=t: nc.vector.tensor_scalar(
            xn[:, t, :], src[:, t, :], mv[:, t, 0:1], rstd[:, t:t + 1], op0=ALU.subtract, op1=ALU.mult), inv)
            for t in tiles_of(half)]

    def normalise(src, half, ready, eps, lanes=(dve, pool), filled=None):
        return norm_apply(src, half, norm_stats(src, half, ready, eps, lanes, filled), lanes[0])

    def fill(ap, value):
        return s_pool.do(lambda e: nc.gpsimd.memset(ap, value))

    def select(ap, pattern, base, mult, op, value, *after):
        return s_pool.do(lambda e: nc.gpsimd.affine_select(
            out=ap, in_=ap, compare_op=op, fill=value, base=base, pattern=pattern, channel_multiplier=mult), *after)

    ident_done = select(ident[:, :], [[-1, P]], 0, 1, ALU.not_equal, 1.0, fill(ident[:, :], 0.0))
    s_dve.do(lambda e: nc.vector.tensor_copy(ident_b[:, :], ident[:, :]), ident_done)
    select(neg_b[:, :], [[-1, P]], 0, 1, ALU.is_ge, NEG, fill(neg_b[:, :], 0.0))
    select(tril[:, :], [[1, P]], 0, -1, ALU.is_ge, 0.0, fill(tril[:, :], 1.0))
    for ap, extra in ((head_mask[:, :], []), (kv_mask[:, :, :], [[0, VW]])):
        first = select(ap, [[-HD1, HC]] + extra, 0, 1, ALU.is_ge, 0.0, fill(ap, 1.0))
        select(ap, [[HD1, HC]] + extra, HD1 - 1, -1, ALU.is_ge, 0.0, first)
    first = select(half_mask[:, :], [[-ES, 2]], 0, 1, ALU.is_ge, 0.0, fill(half_mask[:, :], 1.0))
    select(half_mask[:, :], [[ES, 2]], ES - 1, -1, ALU.is_ge, 0.0, first)
    filled = fill(minus_half[:, :], -0.5)

    silu_done = [s_act.do(lambda e, l=l: nc.scalar.activation(silu[:, l, :, :], cond[:, l, :, :], ACT.Silu),
                          (loaded[f"cond{l}"], 16 * len(cond_loads[l]))) for l in range(2)]
    mod_done = []
    for l in range(2):
        for n in range(3):
            ps = all_banks[3 * l + n][0:NB, :]

            def mod_matmul(e, ps=ps, l=l, n=n):
                for c in range(C):
                    last = nc.tensor.matmul(ps, silu[:, l, c, :], wmod[l][:, c, n * 512:(n + 1) * 512],
                                            start=c == 0, stop=c == C - 1)
                return last

            done = s_pe.do(mod_matmul, silu_done[l])
            last = s_dve.do(
                lambda e, ps=ps, l=l, n=n: nc.vector.tensor_copy(
                    mod_sb[0:NB, l, 2 * n:2 * n + 2, :].rearrange("b s n -> b (s n)"), ps), done)
        scales = mod_sb[0:NB, l, 1:6:3, :]
        gates = mod_sb[0:NB, l, 2:6:3, :]
        ga_, gs_ = gate_a[0:NB], gate_s[0:NB]
        mod_done.append(s_dve.do(lambda e, a=scales: nc.vector.tensor_scalar(a, a, 1.0, None, op0=ALU.add), last))
        size = s_dve.do(lambda e, a=gates, o=ga_: nc.vector.scalar_tensor_tensor(
            o, a, -1.0, a, op0=ALU.mult, op1=ALU.max), last, mod_done[-1])
        size = s_dve.do(lambda e, o=ga_: nc.vector.tensor_scalar(o, o, 0.25, None, op0=ALU.max), size)
        sign = s_dve.do(lambda e, a=gates, o=gs_: nc.vector.tensor_scalar(o, a, 0.0, 2.0, op0=ALU.is_ge, op1=ALU.mult),
                        size)
        last = s_dve.do(lambda e, a=gates, s=gs_, g=ga_: nc.vector.scalar_tensor_tensor(
            a, s, -1.0, g, op0=ALU.add, op1=ALU.mult), sign)
        mod_done.append(last)
        normalise(x, l, [NEXT_X] * TH, EPS, (s_dve, s_pool), filled)

    def setup_sp(e):
        for l in range(2):
            for dst, src in cond_loads[l]:
                e.dma_start(dst, src).then_inc(loaded[f"cond{l}"], 16)
        load_x(e, x, 0)
        for k in range(2):
            e.dma_start(v1_raw[k * RF:(k + 1) * RF, :], I["L0_ffn_V1"]).then_inc(loaded["v1"], 16)
        for dst, src in weight_loads:
            e.dma_start(dst, src).then_inc(loaded["weights"], 16)
        for m in mod_done:
            e.wait_ge(m.lane.sem, m.value)
        e.dma_start(mod_dram.rearrange("b l s n -> b l (s n)"),
                    mod_sb[0:NB, :, :, :].rearrange("b l s n -> b l (s n)")).then_inc(stored, 16)
        e.wait_ge(stored, 16)
        load_columns(e, 0)
        e.wait_ge(loaded["columns"], COLUMN_DMA)

    V1_LOADED = (loaded["v1"], 32)
    high = s_act.do(lambda e: nc.scalar.copy(v1_high[:, :], v1_raw[:, :]), V1_LOADED)
    s_act.do(lambda e: nc.scalar.copy(v1_split[0:RF, :], v1_raw[0:RF, :]))
    s_dve.do(lambda e: nc.vector.tensor_tensor(v1_split[RF:P, :], v1_raw[RF:P, :], v1_high[RF:P, :].bitcast(F32),
                                               op=ALU.subtract), high, V1_LOADED)

    for m in mod_done:
        m.needed = True
    for s in setup.values():
        s.number()
    with nc.Block() as block:
        block.sync(setup_sp)
        block.scalar(setup["act"].emit)
        block.vector(setup["dve"].emit)
        block.tensor(setup["pe"].emit)
        block.gpsimd(setup["pool"].emit)
    nc.sync.sem_clear(loaded["next_x"])
    nc.sync.sem_clear(loaded["columns"])
    nc.all_engine_barrier()

    WEIGHTS = (loaded["weights"], 16 * len(weight_loads))

    banks = Banks(all_banks)
    def turn(src, half, ready, dst, scale=None, bias=None):
        copies = []
        for c in range(C):
            i, ps, reader = banks.take()

            def transposes(e, c=c, ps=ps):
                for t in range(TH):
                    last = nc.tensor.transpose(ps[:, t * P:(t + 1) * P], src[:, half * TH + t, c * P:(c + 1) * P],
                                               ident[:, :])
                return last

            done = pe.do(transposes, *ready, reader)
            o = dst[:, c, half * HW:(half + 1) * HW]
            if scale is None:
                copy = act.do(lambda e, o=o, ps=ps: nc.scalar.copy(o, ps), done)
            else:
                copy = act.do(lambda e, o=o, ps=ps, c=c: nc.scalar.activation(
                    o, ps, ACT.Identity, bias=bias[:, c:c + 1], scale=scale[:, c:c + 1]), done)
            banks.read_by(i, copy)
            copies.append(copy)
        return copies

    def product(ps, pieces):
        def emit(e):
            for n, (w, m) in enumerate(pieces):
                last = nc.tensor.matmul(ps, w, m, start=n == 0, stop=n == len(pieces) - 1)
            return last
        return emit

    def multiply(ps, pieces, *after, turned=None):
        if turned is None:
            return pe.do(product(ps, pieces), *after)
        for n, ((w, m), copy) in enumerate(zip(pieces, turned)):
            step = pe.do(lambda e, n=n, w=w, m=m: nc.tensor.matmul(ps, w, m, start=n == 0, stop=n == C - 1), copy, *after)
        return step

    def load_batch(e):
        e.wait_ge(stored, b_reg["b"] * STORES + 16)
        load_x(e, x, b_reg["b"], "x")
        return load_rows(e)

    sp.do(load_batch)
    begin(OVERLAY)
    yT = part("yT", [P, PAIRS, S])
    begin(FIRST)
    q_split = part("q_split", [P, 2, 2, S], F32R)
    k_high = part("k_high", [P, 2, 2, S], F32R)
    k_low = part("k_low", [P, 2, 2, S], F32R)
    begin(WORK + SPLIT - 8 * S)
    hT = part("hT", [P, C, S])
    latT = part("latT", [P, S])
    v_t = [part(f"v_t{k}", [P, T, P]) for k in range(2)]
    prob = [part(f"prob{k}", [P, S]) for k in range(2)]
    probT = [part(f"probT{k}", [P, S]) for k in range(2)]
    y_t = part("y_t", [P, T, P])
    w_ring = [part(f"w_ring{k}", [P, 4 * P]) for k in range(2)]

    wq_dram = I["L0_attn_w_q"].rearrange("(c p) n -> p c n", p=P)
    wkv_dram = I["L0_attn_w_kv_up"]

    def load_pair(e, buf, col, sem):
        dst = w_ring[buf]
        e.dma_start(dst[:, 0:2 * P].rearrange("p (c n) -> p c n", c=C), wq_dram[:, :, bass.ds(col, P)]).then_inc(sem, 16)
        e.dma_start(dst[:, 2 * P:3 * P], wkv_dram[:, bass.ds(col, P)]).then_inc(sem, 16)
        return e.dma_start(dst[:, 3 * P:4 * P], wkv_dram[:, bass.ds(col + HEADS0 * HD0, P)]).then_inc(sem, 16)

    PAIR_DMA = 3 * 16
    KEY_DMA = 4 * 16

    def double_keys(e, buf, cols=slice(0, S), sem=None):
        for dst in (k_high, k_low):
            for head, (a, b) in enumerate(((TOP, BOTTOM), (BOTTOM, TOP))):
                e.dma_start(dst[b, buf, head, cols].bitcast(F32), dst[a, buf, head, cols].bitcast(F32)
                            ).then_inc(sem or loaded[f"keys{buf}"], 16)

    JOBS = 8
    FIRST_JOBS = 6
    BODY = 2 * U
    TURNS = PAIRS // 2
    HIGH = T // 2

    lat_done = []
    for half in range(NH):
        cols = slice(half * HW, (half + 1) * HW)
        turned = turn(xn, half, [], hT, scale=mod_cols[:, 1, :], bias=mod_cols[:, 0, :])
        i, ps, reader = banks.take()
        done = multiply(ps, [(wdown[:, c, :], hT[:, c, cols]) for c in range(C)], reader, WEIGHTS, turned=turned)
        copy = act.do(lambda e, ps=ps, cols=cols: nc.scalar.copy(latT[:, cols], ps), done)
        banks.read_by(i, copy)
        lat_done.append(copy)
    before_pairs = [r for r in banks.readers if r is not None]

    turned_bank = [bank[0], bank[1]]
    value_bank, job_bank = bank[2], bank[3]

    def unit(u):
        return (u // U) % 2, (u % U) // 2, u % 2, u % 2

    def high_before(u):
        return (u // U) * 2 * HIGH + max(0, u % U - 2 * HIGH)

    first_jobs = list(zip(("k0", "k1", "q0", "q1", "v0", "v1"), bank + [t[:, i, :] for t in score_tiles[:1] for i in range(2)]))

    def pe_job(e, n, kind, buf, ps=None):
        half = int(kind[1])
        cols = slice(half * HW, (half + 1) * HW)
        if ps is None:
            ps = job_bank
            e.wait_ge(flow["job_read"], n)
        wk, wv = (w_ring[buf][:, k * P:(k + 1) * P] for k in (2, 3))
        if kind[0] == "q":
            for c in range(C):
                last = nc.tensor.matmul(ps[:, :], w_ring[buf][:, c * P:(c + 1) * P], hT[:, c, cols],
                                        start=c == 0, stop=c == C - 1)
        elif kind[0] == "k":
            last = nc.tensor.matmul(ps[:, :], wk, latT[:, cols], start=True, stop=True)
        elif kind[0] == "v":
            for t in range(TH):
                tile = half * TH + t
                last = nc.tensor.matmul(ps[:, t * P:(t + 1) * P], latT[:, tile * P:(tile + 1) * P], wv,
                                        start=True, stop=True)
        else:
            for t in range(TH):
                last = nc.tensor.transpose(ps[:, t * P:(t + 1) * P], y_t[:, half * TH + t, :], ident[:, :])
        last.then_inc(flow["job_done"], 1)

    TOP, BOTTOM = slice(0, HD0), slice(HD0, P)

    def act_job(e, n, kind, buf, pair, ps=job_bank):
        half = int(kind[1])
        cols = slice(half * HW, (half + 1) * HW)
        e.wait_ge(flow["job_done"], n + 1)
        if kind[0] in "qk":
            dst = q_split if kind[0] == "q" else k_high
            for head, rows_ in enumerate((TOP, BOTTOM)):
                last = nc.scalar.mul(dst[rows_, buf, head, cols], ps[rows_, :],
                                     HD0 ** -0.5 if kind[0] == "q" else 1.0)
            last.then_inc(flow["rounded"], 1)
            return
        if kind[0] == "v":
            last = nc.scalar.copy(v_t[buf][:, half * TH:(half + 1) * TH, :],
                                  ps[:, :].rearrange("p (t n) -> p t n", t=TH))
        else:
            last = nc.scalar.copy(yT[:, bass.ds(pair, 1), cols],
                                  ps[:, :].rearrange("p (o n) -> p o n", o=1))
        last.then_inc(flow["job_read"], 1)

    def dve_job(e, kind, buf, splits, ps=job_bank):
        if kind[0] not in "qk":
            return
        half = int(kind[1])
        cols = slice(half * HW, (half + 1) * HW)
        e.wait_ge(flow["rounded"], splits)
        for head, rows_, other in ((0, TOP, BOTTOM), (1, BOTTOM, TOP)):
            if kind[0] == "q":
                last = nc.vector.scalar_tensor_tensor(
                    q_split[other, buf, head, cols], ps[rows_, :], HD0 ** -0.5,
                    q_split[rows_, buf, head, cols].bitcast(F32), op0=ALU.mult, op1=ALU.subtract)
            else:
                last = nc.vector.tensor_tensor(k_low[rows_, buf, head, cols], ps[rows_, :],
                                               k_high[rows_, buf, head, cols].bitcast(F32), op=ALU.subtract)
        last.then_inc(flow["job_read"], 1)

    SCHEDULE = {2: "v0", 4: "v1", 6: "k0", 8: "k1", 10: "q0", 12: "q1", 14: "Y0"}

    QK_READ = 5

    def jobs_at(u, tail):
        w, k = u // U, u % U
        if w > 1 or k not in SCHEDULE:
            return None
        kind = SCHEDULE[k]
        if tail and w == 1 and kind != "Y0":
            return None
        order = sorted(SCHEDULE)
        n = w * JOBS + order.index(k)
        if tail and w == 1:
            n = w * JOBS
        splits = w * 4 + sum(SCHEDULE[j][0] in "qk" for j in order if j <= k)
        return n, kind, (w if kind[0] == "Y" else 1 - w), splits

    def y1_number(w, tail):
        return w * JOBS + (1 if tail and w == 1 else JOBS - 1)

    def pe_pairs(e):
        def scores(u):
            buf, i, head, par = unit(u)
            width = (i + 1) * P
            flat = score_tiles[par][:, :, :].rearrange("p a n -> p (a n)")
            qs = q_split[:, buf, head, i * P:(i + 1) * P]
            for seg in range(0, width, 512):
                end = min(width, seg + 512)
                nc.tensor.matmul(flat[:, seg:end], qs, k_high[:, buf, head, seg:end], start=True, stop=False)
                nc.tensor.matmul(flat[:, seg:end], qs, k_low[:, buf, head, seg:end], start=False, stop=end < width)
            nc.tensor.matmul(flat[:, i * P:width], ident_b[:, :], neg_b[:, :], start=False, stop=True
                             ).then_inc(flow["scores_done"], 1)

        def turn_probs(u, g, high):
            _, i, _, par = unit(u)
            e.wait_ge(flow["exp_done"], g + 1)
            e.wait_ge(flow["copied_low"], g)
            for j in range(min(4, i + 1)):
                last = nc.tensor.transpose(turned_bank[0][:, j * P:(j + 1) * P], prob[par][:, j * P:(j + 1) * P],
                                           ident[:, :])
            last.then_inc(flow["turned_low"], 1)
            if i >= 4:
                if u % U > 2 * HIGH:
                    e.wait_ge(flow["copied_high"], high)
                for j in range(4, i + 1):
                    last = nc.tensor.transpose(turned_bank[1][:, (j - 4) * P:(j - 3) * P],
                                               prob[par][:, j * P:(j + 1) * P], ident[:, :])
                last.then_inc(flow["turned_high"], 1)

        def values(u, g, high, tile, first):
            buf, i, head, par = unit(u)
            e.wait_ge(flow["copied_low"], g + 1)
            if i >= 4:
                e.wait_ge(flow["copied_high"], high + 1)
            if head == 0 and first > 0:
                e.wait_ge(flow["normed"], tile)
            o = value_bank[:, head * HD0:(head + 1) * HD0]
            for j in range(i + 1):
                last = nc.tensor.matmul(o, probT[par][:, j * P:(j + 1) * P],
                                        v_t[buf][:, j, head * HD0:(head + 1) * HD0], start=j == 0, stop=j == i)
            last.then_inc(flow["values_done"], 1)

        def steps(n, first, end, tail):
            g0 = e.snap(n * BODY) if not isinstance(n, int) else n * BODY
            hi0 = n * (4 * HIGH)
            j0 = n * (2 * JOBS) + FIRST_JOBS
            for u in range(first, end):
                turn_probs(u, g0 + u, hi0 + high_before(u))
                if u + 2 < BODY or not tail:
                    if u + 2 == U:
                        e.wait_ge(loaded["keys1"], n * KEY_DMA + KEY_DMA)
                        e.wait_ge(flow["job_read"], j0 + QK_READ)
                    if u + 2 == BODY:
                        e.wait_ge(loaded["keys0"], n * KEY_DMA + 2 * KEY_DMA)
                        e.wait_ge(flow["job_read"], j0 + JOBS + QK_READ)
                    scores(u + 2)
                if u > 0:
                    values(u - 1, g0 + u - 1, hi0 + high_before(u - 1), n * (BODY // 2) + (u - 1) // 2, (u - 1) // 2)
                if u > 1 and u % U == 1:
                    e.wait_ge(flow["normed"], n * (BODY // 2) + (u // U) * T)
                    pe_job(e, j0 + y1_number(u // U - 1, tail), "Y1", u // U - 1)
                job = jobs_at(u, tail)
                if job:
                    k, kind, buf, _ = job
                    if kind == "Y0":
                        e.wait_ge(flow["normed"], n * (BODY // 2) + (u // U) * T + TH)
                    if kind == "v0":
                        if u // U == 0:
                            e.wait_ge(loaded["w1"], n * PAIR_DMA + PAIR_DMA)
                        else:
                            e.wait_ge(loaded["w0"], n * PAIR_DMA + 2 * PAIR_DMA)
                    pe_job(e, j0 + k, kind, buf)
            if tail:
                values(BODY - 1, g0 + BODY - 1, hi0 + high_before(BODY - 1), n * (BODY // 2) + T * 2 - 1, T * 2 - 1)
                e.wait_ge(flow["normed"], n * (BODY // 2) + 2 * T)
                pe_job(e, j0 + y1_number(1, tail), "Y1", 1)

        e.wait_ge(loaded["w0"], PAIR_DMA)
        for n, (kind, ps) in enumerate(first_jobs):
            pe_job(e, n, kind, 0, ps)
        e.wait_ge(flow["job_read"], FIRST_JOBS)
        e.wait_ge(loaded["first_keys"], KEY_DMA)
        scores(0)
        scores(1)
        steps(0, 0, 2, False)
        e.wait_ge(loaded["keys0"], KEY_DMA)
        with e.Fori(0, TURNS - 1) as n:
            steps(n, 2, BODY + 2, False)
        steps(TURNS - 1, 2, BODY, True)

    def dve_pairs(e):
        def maximum(u, g):
            _, i, _, par = unit(u)
            flat = score_tiles[par][:, :, :].rearrange("p a n -> p (a n)")
            e.wait_ge(flow["scores_done"], g + 1)
            nc.vector.tensor_reduce(neg_max[:, u % 4:u % 4 + 1], flat[:, 0:(i + 1) * P], axis=AX_X, op=ALU.max,
                                    negate=True).then_inc(flow["max_done"], 1)

        def copy_low(u, g):
            _, i, _, par = unit(u)
            w = min(4, i + 1) * P
            e.wait_ge(flow["turned_low"], g + 1)
            nc.vector.tensor_copy(probT[par][:, 0:w], turned_bank[0][:, 0:w]).then_inc(flow["copied_low"], 1)

        def norm(u, g, tiles):
            _, i, _, _ = unit(u)
            k = (u - 1) % 8
            e.wait_ge(flow["exp_done"], g + 1)
            nc.vector.reciprocal(rec[:, k:k + 2], row_sum[:, k:k + 2]).then_inc(flow["inverted"], 1)
            e.wait_ge(flow["values_done"], g + 1)
            e.wait_ge(flow["inverted"], tiles)
            nc.vector.tensor_tensor(y_t[:, i, :].rearrange("p (a n) -> p a n", a=2),
                                    value_bank[:, 0:P].rearrange("p (a n) -> p a n", a=2),
                                    rec[:, k:k + 2].unsqueeze(2).to_broadcast([P, 2, HD0]),
                                    op=ALU.mult).then_inc(flow["normed"], 1)

        def steps(n, first, end, tail):
            g0 = e.snap(n * BODY) if not isinstance(n, int) else n * BODY
            for u in range(first, end):
                copy_low(u, g0 + u)
                if u + 2 < BODY or not tail:
                    maximum(u + 2, g0 + u + 2)
                if u % 2 == 0 and u > 0:
                    norm(u - 1, g0 + u - 1, n * (BODY // 2) + u // 2)
                job = jobs_at(u - 1, tail) if u else None
                if job:
                    dve_job(e, job[1], job[2], n * 8 + 4 + job[3])
            if tail:
                norm(BODY - 1, g0 + BODY - 1, n * (BODY // 2) + BODY // 2)

        for n, (kind, ps) in enumerate(first_jobs):
            dve_job(e, kind, 0, n + 1, ps)
        maximum(0, 0)
        maximum(1, 1)
        steps(0, 0, 2, False)
        with e.Fori(0, TURNS - 1) as n:
            steps(n, 2, BODY + 2, False)
        steps(TURNS - 1, 2, BODY, True)


    def act_pairs(e):
        def exponential(u, g):
            _, i, _, par = unit(u)
            w = (i + 1) * P
            flat = score_tiles[par][:, :, :].rearrange("p a n -> p (a n)")
            e.wait_ge(flow["max_done"], g + 1)
            nc.scalar.activation(prob[par][:, 0:w], flat[:, 0:w], ACT.Exp, bias=neg_max[:, u % 4:u % 4 + 1],
                                 accum_out=row_sum[:, u % 8:u % 8 + 1]).then_inc(flow["exp_done"], 1)

        def copy_high(u, high):
            _, i, _, par = unit(u)
            w = (i - 3) * P
            e.wait_ge(flow["turned_high"], high + 1)
            nc.scalar.copy(probT[par][:, 4 * P:4 * P + w], turned_bank[1][:, 0:w]).then_inc(flow["copied_high"], 1)

        def steps(n, first, end, tail):
            g0 = e.snap(n * BODY) if not isinstance(n, int) else n * BODY
            hi0 = n * (4 * HIGH)
            j0 = n * (2 * JOBS) + FIRST_JOBS
            for u in range(first, end):
                if unit(u)[1] >= 4:
                    copy_high(u, hi0 + high_before(u))
                if u + 2 < BODY or not tail:
                    exponential(u + 2, g0 + u + 2)
                if u > 1 and u % U == 1:
                    act_job(e, j0 + y1_number(u // U - 1, tail), "Y1", u // U - 1, n * 2 + u // U - 1)
                job = jobs_at(u, tail)
                if job:
                    k, kind, buf, splits = job
                    act_job(e, j0 + k, kind, buf, n * 2 + u // U)
            if tail:
                act_job(e, j0 + y1_number(1, tail), "Y1", 1, n * 2 + 1)

        for n, (kind, ps) in enumerate(first_jobs):
            if kind == "v0":
                e.wait_ge(flow["job_read"], n)
            act_job(e, n, kind, 0, 0, ps)
        exponential(0, 0)
        exponential(1, 1)
        steps(0, 0, 2, False)
        with e.Fori(0, TURNS - 1) as n:
            steps(n, 2, BODY + 2, False)
        steps(TURNS - 1, 2, BODY, True)

    def sp_pairs(e):
        load_pair(e, 0, 0, loaded["w0"])
        load_pair(e, 1, P, loaded["w1"])
        for half in range(NH):
            e.wait_ge(flow["job_read"], half + 1)
            double_keys(e, 0, slice(half * HW, (half + 1) * HW), loaded[("first_keys", "keys0")[half]])
        with e.Fori(0, TURNS - 1) as n:
            j0 = n * (2 * JOBS) + FIRST_JOBS
            even, odd = e.snap(n * 2 * P + 2 * P), e.snap(n * 2 * P + 3 * P)
            e.wait_ge(flow["job_done"], j0)
            load_pair(e, 0, even, loaded["w0"])
            e.wait_ge(flow["job_read"], j0 + 4)
            double_keys(e, 1)
            e.wait_ge(flow["job_done"], j0 + JOBS - 1)
            load_pair(e, 1, odd, loaded["w1"])
            e.wait_ge(flow["job_read"], j0 + JOBS + 4)
            double_keys(e, 0)
        e.wait_ge(flow["job_read"], (TURNS - 1) * 2 * JOBS + FIRST_JOBS + 4)
        double_keys(e, 1)

    JOBS_ALL = FIRST_JOBS + (TURNS - 1) * 2 * JOBS + JOBS + 2
    UNITS_ALL = TURNS * BODY
    PAIRS_DONE = [(flow["job_read"], JOBS_ALL), (flow["normed"], UNITS_ALL // 2), (flow["copied_low"], UNITS_ALL),
                  (flow["exp_done"], UNITS_ALL), (flow["copied_high"], TURNS * 4 * HIGH)]

    sp.do(sp_pairs)
    pe.do(pe_pairs, *before_pairs, *lat_done)
    dve.do(dve_pairs)
    act.do(act_pairs)

    banks = Banks(all_banks)
    prior_x = [None] * 3

    def residual(t, ps, done, gate, bias=None, extra=None):
        a = tmp[:, t % 3, :]
        if bias is None:
            read = last = dve.do(lambda e: nc.vector.tensor_tensor(a, ps, gate, op=ALU.mult), done, prior_x[t % 3],
                                 ROWS, X_LOADED)
        else:
            read = last = dve.do(lambda e: nc.vector.tensor_tensor(a, ps, bias, op=ALU.add), done, prior_x[t % 3])
            if extra is not None:
                last = dve.do(lambda e: nc.vector.tensor_tensor(a, a, extra, op=ALU.add), last)
            last = dve.do(lambda e: nc.vector.tensor_tensor(a, a, gate, op=ALU.mult), last)
        wrote = dve.do(lambda e: nc.vector.tensor_tensor(x[:, t, :], x[:, t, :], a, op=ALU.add), last)
        prior_x[t % 3] = wrote
        return read, wrote

    def to_residual(half, pieces, gate, *deps, bias=None, extra=None, between=None):
        wrote = []
        for t in tiles_of(half):
            if between and t == half * TH + 1:
                between()
            i, ps, reader = banks.take()
            done = pe.do(product(ps[:, 0:D], pieces(slice(t * P, (t + 1) * P))), reader, *deps)
            read, w = residual(t, ps[:, 0:D], done, gate, bias, extra and extra(t))
            banks.read_by(i, read)
            wrote.append(w)
        return wrote

    def blocks(m_count, pieces, half, rows_, evacuate, *deps, turned=None):
        cols, res = slice(half * HW, (half + 1) * HW), []
        for m in range(m_count):
            i, ps, reader = banks.take()
            done = multiply(ps[0:rows_, :], pieces(m, cols), reader, *deps, turned=turned)
            step = evacuate(m, cols, ps[0:rows_, :], done)
            banks.read_by(i, step)
            res.append(step)
        return res

    def gelu_into(dst, bias):
        return lambda m, cols, ps, done: act.do(lambda e: nc.scalar.activation(
            dst[:, m, cols], ps, ACT.Gelu_apprx_tanh, bias=bias[:, m:m + 1]), done)

    def affine_rows(half, normed, scale, shift, pool_adds=False):
        ts = list(tiles_of(half))
        scaled = [dve.do(lambda e, t=t: nc.vector.tensor_tensor(h[:, t, :], xn[:, t, :], scale, op=ALU.mult), n)
                  for t, n in zip(ts, normed)]
        if pool_adds:
            return [pool.do(lambda e, t=t: nc.gpsimd.tensor_tensor(h[:, t, :], h[:, t, :], shift, op=ALU.add), s_)
                    for t, s_ in zip(ts, scaled)]
        return [dve.do(lambda e, t=t: nc.vector.tensor_tensor(h[:, t, :], h[:, t, :], shift, op=ALU.add), s_)
                for t, s_ in zip(ts, scaled)]

    def head_outputs(half):
        wrote = to_residual(half, lambda tok: [(yT[:, j, tok], wout[:, j, :]) for j in range(PAIRS)], mod_rows[:, 0, :],
                            *PAIRS_DONE, WEIGHTS)
        return norm_stats(x, half, wrote, EPS)

    begin(WORK)
    hT2 = part("hT2", [P, C, S])
    rank_high, rank_low = part("rank_high", [P, S], F32R), part("rank_low", [P, S], F32R)
    hid = part("hid", [P, FM, S])
    rank2T = part("rank2T", [P, S])

    def feed_turn(half, normed):
        return turn(xn, half, normed, hT2, scale=mod_cols[:, 3, :], bias=mod_cols[:, 2, :])

    def feed_rank(half, turned):
        high = []

        def split(m, cols, ps, done):
            high.append(act.do(lambda e: nc.scalar.copy(rank_high[:, cols], ps), done))
            return dve.do(lambda e: nc.vector.tensor_tensor(rank_low[:, cols], ps, rank_high[:, cols].bitcast(F32),
                                                            op=ALU.subtract), high[0])

        low = blocks(1, lambda m, cols: [(u1[:, c, :], hT2[:, c, cols]) for c in range(C)], half, P, split, turned=turned)
        return high + low

    def feed_wide(half, split):
        return blocks(FM, lambda m, cols: [(v1_split[:, m * P:(m + 1) * P], r[:, cols]) for r in (rank_high, rank_low)],
                      half, P, gelu_into(hid, b1_0), turned=split)

    def feed_rank2(half, wide):
        return blocks(1, lambda m, cols: [(u2[:, j, :], hid[:, j, cols]) for j in range(FM)], half, RF,
                      lambda m, cols, ps, done: act.do(lambda e: nc.scalar.copy(rank2T[0:RF, cols], ps), done), *wide)

    def feed_output(half, low2):
        return to_residual(half, lambda tok: [(rank2T[0:RF, tok], v2[:, :])], mod_rows[:, 1, :], *low2, bias=b2_0[:, :])

    begin(OVERLAY)
    q_spread = [part(f"q_spread{k}", [P, C, HC, P]) for k in range(2)]
    begin(WORK)
    nT = part("nT", [P, C, S])
    qT = part("qT", [P, C, S])
    k_tok = part("k_tok", [P, T, D])
    v_tok = part("v_tok", [P, T, HEADS1, VW])
    kT = part("kT", [P, C, S])
    am = [part(f"am{k}", [P, HEADS1, P]) for k in range(2)]
    yT2, y_rows = nT, xn

    def attention_norms(half, ready):
        inv = norm_stats(x, half, ready, EPS)
        yield
        normed = norm_apply(x, half, inv)
        yield
        h_done = affine_rows(half, normed, mod_rows[:, 3, :], mod_rows[:, 2, :], pool_adds=half == 1)
        yield
        inv = norm_stats(h, half, h_done, EPS_LN)
        yield
        yield norm_apply(h, half, inv)

    def phi(dst, src):
        return lambda e: nc.vector.tensor_scalar(dst, src, 0.0, EPS_PHI, op0=ALU.max, op1=ALU.add)

    ones_set = []
    q_done, v_done, kT_done = {}, {}, {}

    def attention_turn(half, normed):
        return turn(xn, half, normed, nT, scale=ln_cols[:, 0, :], bias=ln_cols[:, 1, :])

    def attention_inputs(half, turned, between=iter(())):
        if half == 0:
            ones_set.append(dve.do(lambda e: nc.vector.memset(v_tok[:, :, :, HD1:VW], 1.0), turned[0]))
        k_done = []
        for t in tiles_of(half):
            i, ps, reader = banks.take()
            done = multiply(ps, [(nT[:, c, t * P:(t + 1) * P], wkv1[:, c, :]) for c in range(C)], reader, turned=turned)
            k_done.append(dve.do(phi(k_tok[:, t, :], ps[:, 0:D]), done))
            v_done[t] = act.do(lambda e, t=t, ps=ps: nc.scalar.copy(
                v_tok[:, t, :, 0:HD1], ps[:, D:2 * D].rearrange("p (h n) -> p h n", h=HEADS1)), k_done[-1], *ones_set)
            banks.read_by(i, v_done[t])
            next(between, None)
        q_done[half] = blocks(C, lambda m, cols: [(wq1[:, c, m * P:(m + 1) * P], nT[:, c, cols]) for c in range(C)],
                              half, P, lambda m, cols, ps, done: dve.do(phi(qT[:, m, cols], ps), done), turned=turned)
        kT_done[half] = turn(k_tok, half, k_done, kT)

    def spread_queries(t, used):
        half, tok, spread = t // TH, slice(t * P, (t + 1) * P), q_spread[t % 2]
        ready = [None, None]
        ready[0] = dve.do(lambda e: nc.vector.tensor_tensor(
            spread[:, 0, :, :], qT[:, 0, tok].unsqueeze(1).to_broadcast([P, HC, P]),
            head_mask[:, :].unsqueeze(2).to_broadcast([P, HC, P]), op=ALU.mult), q_done[half][0], used[t % 2])
        for hh in range(HC):
            ready[1] = act.do(lambda e, hh=hh: nc.scalar.mul(spread[:, 1, hh, :], qT[:, 1, tok], head_mask[:, hh:hh + 1]),
                              q_done[half][1], used[t % 2])
        return ready

    def tile_scores(t, ready, used, between=None):
        half, tok, spread = t // TH, slice(t * P, (t + 1) * P), q_spread[t % 2]
        masked = []
        for c in range(C):
            for quad in range(2):
                i, ps, reader = banks.take()
                done = pe.do(lambda e, ps=ps, c=c, quad=quad: nc.tensor.matmul(
                    ps, kT[:, c, tok], spread[:, c, quad * 4:quad * 4 + 4, :], start=True, stop=True),
                    reader, ready[c], kT_done[half][c])
                if between:
                    between(c * 2 + quad)
                dst = am[t % 2][:, c * HC + quad * 4:c * HC + quad * 4 + 4, :]
                step = dve.do(lambda e, dst=dst, ps=ps: nc.vector.tensor_tensor(
                    dst, ps.rearrange("p (h n) -> p h n", h=4), tril[:, :].unsqueeze(1).to_broadcast([P, 4, P]),
                    op=ALU.mult), done, am_used[t % 2])
                banks.read_by(i, step)
                masked.append(step)
        used[t % 2] = done
        return masked

    am_used, y_done = [None, None], []

    def tile_numerators(t, masked, state_read):
        tok = slice(t * P, (t + 1) * P)
        i, ps, reader = banks.take()
        steps = []

        def numerators(e, n):
            for hd in range(n * 4, n * 4 + 4):
                last = nc.tensor.matmul(ps[:, hd * VW:(hd + 1) * VW], am[t % 2][:, hd, :], v_tok[:, t, hd, :],
                                        start=hd == 0, stop=False, skip_group_check=True)
            if n == 3:
                for c in range(C):
                    last = nc.tensor.matmul(ps[:, c * HC * VW:(c + 1) * HC * VW], qT[:, c, tok], kv_state[:, c, :],
                                            start=False, stop=c == C - 1, skip_group_check=True)
            return last

        def put(n):
            steps.append(pe.do(lambda e: numerators(e, n), reader, masked[n], v_done[t], state_read if n == 3 else None))

        return i, ps, put, steps

    def tile_outputs(t, i, ps, done, state_read):

        am_used[t % 2] = done
        if t < T - 1:
            def update(e):
                for c in range(C):
                    last = nc.tensor.matmul(state_bank[:, c * HC * VW:(c + 1) * HC * VW],
                                            k_tok[:, t, c * P:(c + 1) * P],
                                            v_tok[:, t, c * HC:(c + 1) * HC, :].rearrange("p h v -> p (h v)"),
                                            start=t == 0 and c == 0, stop=t == T - 2 and c == C - 1,
                                            skip_group_check=True)
                return last

            updated = pe.do(update, state_reader, state_read)
        view = ps[:, 0:HEADS1 * VW].rearrange("p (h v) -> p h v", h=HEADS1)
        inverse = dve.do(lambda e: nc.vector.reciprocal(rec[:, :], view[:, :, HD1]), done,
                         y_done[-1] if y_done else None)
        y_done.append(dve.do(lambda e: nc.vector.tensor_tensor(
            y_rows[:, t, :].rearrange("p (h n) -> p h n", h=HEADS1), view[:, :, 0:HD1],
            rec[:, :].unsqueeze(2).to_broadcast([P, HEADS1, HD1]), op=ALU.mult), inverse))
        banks.read_by(i, y_done[-1])
        if t < T - 1:
            return dve.do(lambda e: nc.vector.tensor_tensor(
                kv_state[:, :, :], state_bank[:, 0:HEADS1 * VW].rearrange("p (c n) -> p c n", c=C),
                kv_mask[:, :, :].rearrange("p h v -> p (h v)").unsqueeze(1).to_broadcast([P, C, HC * VW]),
                op=ALU.mult), updated)
        return state_read

    def attention_output(half):
        turned = turn(y_rows, half, y_done[half * TH:(half + 1) * TH], yT2)
        wrote = []
        for t in tiles_of(half):
            i, ps, reader = banks.take()
            done = multiply(ps[:, 0:D], [(yT2[:, c, t * P:(t + 1) * P], wo1[:, c, :]) for c in range(C)], reader,
                            turned=turned)
            wrote.append(dve.do(lambda e, t=t, ps=ps: nc.vector.tensor_tensor(h[:, t, :], ps[:, 0:D], h[:, t, :],
                                                                              op=ALU.add), done))
            banks.read_by(i, wrote[-1])
        return normalise(h, half, wrote, EPS_LN)

    begin(WORK + 2 * S)
    hid1 = part("hid1", [P, FM, S])
    mT = part("mT", [P, C, S])

    def mlp_turn(half, normed):
        return turn(xn, half, normed, mT, scale=ln_cols[:, 2, :], bias=ln_cols[:, 3, :])

    def mlp_wide(half, turned):
        return blocks(FM, lambda m, cols: [(w1[:, c, m * P:(m + 1) * P], mT[:, c, cols]) for c in range(C)], half, P,
                      gelu_into(hid1, b1_1), turned=turned)

    def mlp_output(half, wide, between=None):
        return to_residual(half, lambda tok: [(hid1[:, m, tok], w2[:, m, :]) for m in range(FM)], mod_rows[:, 4, :],
                           *wide, bias=b2_1[:, :], extra=lambda t: h[:, t, :], between=between)

    begin(OVERLAY)
    f2 = part("f2", [P, EP, D])
    f1 = part("f1", [P, C, ES, EF])
    begin(WORK)
    permT = part("permT", [P, S])
    blockT = part("blockT", [P, S])
    sel = part("sel", [P, C, ES, G])
    begin(WORK + 2 * S)
    inter_t = part("inter_t", [P, C, G, ES])
    perm = [part(f"perm{k}", [P, GT, ES]) for k in range(2)]
    inter = [part(f"inter{k}", [P, 4, D]) for k in range(2)]
    hT3 = part("hT3", [P, C, S])
    begin(WORK + 13 * S)
    next_x = part("next_x", [P, T, D])
    logits = inter[0][:, :, :].rearrange("p k n -> p (k n)")
    before_relu = xn[:, :, :].rearrange("p t n -> p (t n)").rearrange("p (q g) -> p q g", q=EP)
    begin(FIRST)
    inner = part("inner", [P, EP, 2, G])
    f1_dram = I["L1_ffn_f1"].rearrange("(c p) e s f -> c p (e s) f", p=P)
    f2_dram = I["L1_ffn_f2"].rearrange("e s f d -> (e s) f d").rearrange("(q two) f d -> two f q d", two=2)

    def load_f1(e):
        for c in range(C):
            last = e.dma_start(f1[:, c, :, :], f1_dram[c]).then_inc(loaded["f1"], 16)
        return last

    def load_f2(e):
        for k in range(2):
            last = e.dma_start(f2[k * EF:(k + 1) * EF, :, :], f2_dram[k]).then_inc(loaded["f2"], 16)
        return last

    def slot_norms(half, inv):
        return affine_rows(half, norm_apply(x, half, inv), mod_rows[:, 6, :], mod_rows[:, 5, :])

    perm_done, block_done = [], []

    def choices(half, turned):
        gs = slice(half * G // NH, (half + 1) * G // NH)
        cols = slice(half * HW, (half + 1) * HW)
        v3 = logits[:, cols].rearrange("p (g t) -> p g t", t=NE)
        lg = blocks(1, lambda m, cols: [(ctrl[:, c, :], hT3[:, c, cols]) for c in range(C)], half, P,
                    lambda m, cols, ps, done: dve.do(lambda e: nc.vector.tensor_tensor(
                        v3, ps.rearrange("p (g t) -> p g t", t=NE),
                        tie[:, :].unsqueeze(1).to_broadcast([P, G // NH, NE]), op=ALU.add), done), turned=turned)
        top = dve.do(lambda e: nc.vector.tensor_reduce(logit_max[:, gs], v3, axis=AX_X, op=ALU.max), *lg)
        perm_done.append(dve.do(lambda e: nc.vector.tensor_tensor(
            permT[:, cols].rearrange("p (g t) -> p g t", t=NE), v3,
            logit_max[:, gs].unsqueeze(2).to_broadcast([P, G // NH, NE]), op=ALU.is_equal), top))
        for k in range(2):
            view = [a[:, cols].rearrange("p (q two t) -> p q two t", two=2, t=NE)[:, :, k, :] for a in (blockT, permT)]
            step = dve.do(lambda e, view=view, k=k: nc.vector.tensor_scalar(
                view[0], view[1], half_mask[:, k:k + 1], None, op0=ALU.mult), perm_done[-1])
        block_done.append(step)
        return lg[-1]

    sp.do(load_f1, *PAIRS_DONE)
    low_norm = norm_apply(x, 0, head_outputs(0))
    inv = head_outputs(1)
    rank0 = feed_rank(0, feed_turn(0, low_norm))
    wide0 = feed_wide(0, rank0)
    feed_turned = feed_turn(1, norm_apply(x, 1, inv))
    rank2_0 = feed_rank2(0, wide0)
    rank1 = feed_rank(1, feed_turned)
    *_, attn_norm = attention_norms(0, feed_output(0, rank2_0))
    wide1 = feed_wide(1, rank1)
    rank2_1 = feed_rank2(1, wide1)
    norms = attention_norms(1, feed_output(1, rank2_1))
    next(norms)
    state_bank, state_reader = banks.tiles[7], banks.readers[7]
    banks7 = Banks(all_banks[0:7])
    banks7.readers, banks7.at = banks.readers[0:7], (banks.at if banks.at < 7 else 6)
    banks = banks7
    attention_inputs(0, attention_turn(0, attn_norm), islice(norms, 3))
    state = dve.do(lambda e: nc.vector.memset(kv_state[:, :, :], 0.0), *ones_set)
    spread_used = [None, None]
    spread = {0: spread_queries(0, spread_used), 1: spread_queries(1, spread_used)}
    masked = tile_scores(0, spread[0], spread_used)
    attn_norm = next(norms)
    mlp_norms = []
    for t in range(T):
        if t + 3 == TH:
            attn_turned = attention_turn(1, attn_norm)
        if t + 2 == TH:
            attention_inputs(1, attn_turned)
        if t + 2 < T:
            spread[t + 2] = spread_queries(t + 2, spread_used)
        i, ps, put, parts = tile_numerators(t, masked, state)
        if t + 1 < T:
            ahead = tile_scores(t + 1, spread[t + 1], spread_used, put)
        else:
            mlp_turned = mlp_turn(0, mlp_norms[0])
            for n in range(4):
                put(n)
        state = tile_outputs(t, i, ps, parts[-1], state)
        masked = ahead
        if t == TH:
            mlp_norms.append(attention_output(0))
    sp.do(load_f2, spread_used[(T - 1) % 2])
    wide0 = mlp_wide(0, mlp_turned)
    mlp_norms.append(attention_output(1))
    readers = banks.readers + [state]
    banks = Banks(all_banks)
    banks.readers = readers
    slots_h = [slot_norms(0, norm_stats(x, 0, mlp_output(0, wide0), EPS))]
    wide1 = mlp_wide(1, mlp_turn(1, mlp_norms[1]))
    slots_turned = turn(h, 0, slots_h[0], hT3)
    choices(0, slots_turned)

    spread_reader = [None, None]
    sel_done = []

    def spread_choices(t):
        i, ps, reader = banks.take()
        done = pe.do(lambda e: nc.tensor.transpose(ps[:, 0:ES], permT[0:ES, t * P:(t + 1) * P], ident[0:ES, 0:ES]),
                     reader, perm_done[t // TH])
        step = dve.do(lambda e: nc.vector.tensor_tensor(
            perm[t % 2][:, :, :], ps[:, 0:ES].unsqueeze(1).to_broadcast([P, GT, ES]),
            head_mask[:, :].unsqueeze(2).to_broadcast([P, GT, ES]), op=ALU.mult), done, spread_reader[t % 2])
        banks.read_by(i, step)
        return step

    spread_ready = {}
    inv = norm_stats(x, 1, mlp_output(1, wide1, lambda: spread_ready.update({t: spread_choices(t) for t in range(2)})), EPS)
    for t in range(T):
        step = spread_ready[t]
        for c in range(C):
            i, ps, reader = banks.take()
            done = pe.do(product(ps, [(h[:, t, c * P:(c + 1) * P], perm[t % 2][:, :, :].rearrange("p g s -> p (g s)"))]), reader, step)
            spread_reader[t % 2] = done
            o = sel[:, c, :, t * GT:(t + 1) * GT].rearrange("p s g -> p g s")
            src = ps.rearrange("p (g s) -> p g s", g=GT)
            if c == 0 or t < TH:
                copy = act.do(lambda e, o=o, src=src: nc.scalar.copy(o, src), done)
            else:
                copy = dve.do(lambda e, o=o, src=src: nc.vector.tensor_copy(o, src), done)
            banks.read_by(i, copy)
            sel_done.append(copy)
        if t + 1 == TH:
            turned_read = choices(1, turn(h, 1, slots_h[1], hT3))
            spread_ready[TH] = spread_choices(TH)
        if t + 2 < T and t + 2 != TH:
            spread_ready[t + 2] = spread_choices(t + 2)
        if t == 0:
            inv = norm_apply(x, 1, inv)
        if t == 1:
            slots_h.append(affine_rows(1, inv, mod_rows[:, 6, :], mod_rows[:, 5, :], pool_adds=True))

    def load_next(e):
        nxt = e.snap((b_reg["b"] + 1) % NB)
        load_x(e, next_x, nxt)
        return load_columns(e, nxt)

    sp.do(load_next, turned_read)

    inner_done = []
    for blk in range(4):
        i, ps, reader = banks.take()

        def first_product(e, blk=blk, ps=ps):
            for s in range(blk * 16, blk * 16 + 16):
                o = ps[(s % 2) * EF:(s % 2 + 1) * EF, (s // 2 - blk * 8) * G:(s // 2 - blk * 8 + 1) * G]
                for c in range(C):
                    last = nc.tensor.matmul(o, f1[:, c, s, :], sel[:, c, s, :], start=c == 0, stop=c == C - 1)
            return last

        done = pe.do(first_product, reader, *(sel_done + [(loaded["f1"], 32)] if blk == 0 else []))
        dst = before_relu[:, blk * 8:blk * 8 + 8, :]
        biased = dve.do(lambda e, ps=ps, dst=dst, blk=blk: nc.vector.tensor_tensor(
            dst, ps.rearrange("p (q g) -> p q g", q=8),
            fbias[:, blk * 8:blk * 8 + 8].unsqueeze(2).to_broadcast([P, 8, G]), op=ALU.add), done)
        banks.read_by(i, biased)
        for k in range(2):
            relu = act.do(lambda e, dst=dst, blk=blk, k=k: nc.scalar.activation(
                inner[:, blk * 8:blk * 8 + 8, k, :], dst, ACT.Relu, scale=half_mask[:, k:k + 1]), biased)
        inner_done.append(relu)

    inter_t_done = []
    for blk in range(4):
        for c in range(C):
            for quad in range(2):
                i, ps, reader = banks.take()
                pairs = [blk * 8 + quad * 4 + k for k in range(4)]

                def second_product(e, ps=ps, c=c, pairs=pairs):
                    for k, q in enumerate(pairs):
                        last = nc.tensor.matmul(ps[:, k * P:(k + 1) * P], f2[:, q, c * P:(c + 1) * P],
                                                inner[:, q, :, :].rearrange("p two g -> p (two g)"), start=True, stop=True)
                    return last

                done = pe.do(second_product, reader, inner_done[blk], (loaded["f2"], 32))
                o = inter_t[:, c, :, 2 * pairs[0]:2 * pairs[0] + 8].rearrange("p g s -> p s g")
                src = ps.rearrange("p (s g) -> p s g", s=8)
                if quad:
                    copy = act.do(lambda e, o=o, src=src: nc.scalar.copy(o, src), done, inner_done[3])
                else:
                    copy = dve.do(lambda e, o=o, src=src: nc.vector.tensor_copy(o, src), done, inner_done[3])
                banks.read_by(i, copy)
                inter_t_done.append(copy)
        if blk in (1, 2):
            norm_apply(next_x, blk - 1, next_norm)
        if blk < 2:
            next_norm = norm_stats(next_x, blk, [NEXT_X] * TH, EPS)

    inter_reader = [None, None]
    finals = []

    def slot_rows(t):
        copies = []
        for two in range(2):
            i, ps, reader = banks.take()

            def turn_back(e, two=two, ps=ps):
                for kk in range(2):
                    g = t * GT + (two * 2 + kk) * 2
                    for c in range(C):
                        last = nc.tensor.transpose(ps[:, kk * D + c * P:kk * D + (c + 1) * P],
                                                   inter_t[:, c, g:g + 2, :].rearrange("p g s -> p (g s)"), ident[:, :])
                return last

            done = pe.do(turn_back, reader, *(inter_t_done if t == 0 and two == 0 else []))
            dst = inter[t % 2][:, two * 2:two * 2 + 2, :]
            src = ps.rearrange("p (k n) -> p k n", k=2)
            if two:
                copies.append(act.do(lambda e, dst=dst, src=src: nc.scalar.copy(dst, src), done, inter_reader[t % 2]))
            else:
                copies.append(dve.do(lambda e, dst=dst, src=src: nc.vector.tensor_copy(dst, src), done, inter_reader[t % 2]))
            banks.read_by(i, copies[-1])
        return copies

    rows_ready = slot_rows(0)
    for t in range(T):
        copies = rows_ready
        if t + 1 < T:
            rows_ready = slot_rows(t + 1)
        i, ps, reader = banks.take()

        def combine(e, t=t, ps=ps):
            for kk in range(4):
                lo = t * P + kk * 32
                last = nc.tensor.matmul(ps[kk * 32:(kk + 1) * 32, 0:D], blockT[:, lo:lo + 32], inter[t % 2][:, kk, :],
                                        start=True, stop=True)
            return last

        done = pe.do(combine, reader, *copies, block_done[t // TH])
        inter_reader[t % 2] = done
        read, wrote = residual(t, ps[:, 0:D], done, mod_rows[:, 7, :])
        banks.read_by(i, read)
        finals.append(wrote)
        if t % 2:
            sp.do(lambda e, t=t: e.dma_start(x_out[b_reg["b"]][:, t - 1:t + 1, :], x[:, t - 1:t + 1, :]
                                             ).then_inc(stored, 16), wrote)

    sp.do(lambda e: e.wait_ge(loaded["columns"], COLUMN_DMA))
    for ln in lane.values():
        ln.number()

    cleared = [ln.sem for ln in lane.values()] + list(flow.values())
    cleared += [loaded[k] for k in ("x", "next_x", "columns", "rows", "f1", "f2", "w0", "w1", "first_keys", "keys0", "keys1")]
    with nc.Fori(0, NB) as b:
        b_reg["b"] = b
        with nc.Block() as block:
            block.sync(sp.emit)
            block.scalar(act.emit)
            block.vector(dve.emit)
            block.tensor(pe.emit)
            block.gpsimd(pool.emit)
        for s in cleared:
            nc.sync.sem_clear(s)
        nc.all_engine_barrier()
    nc.sync.wait_ge(stored, NB * STORES + 16)
    ctx.close()


_INS = ["L0_attn_x", "L0_attn_w_kv_down", "L0_attn_w_kv_up", "L0_attn_w_q", "L0_attn_w_out", "L0_ffn_U1", "L0_ffn_V1",
        "L0_ffn_b1", "L0_ffn_U2", "L0_ffn_V2", "L0_ffn_b2", "L0_c", "L0_wmod", "L1_attn_ln1_scale", "L1_attn_ln1_bias",
        "L1_attn_wq", "L1_attn_wk", "L1_attn_wv", "L1_attn_wo", "L1_attn_ln2_scale", "L1_attn_ln2_bias", "L1_attn_w1",
        "L1_attn_b1", "L1_attn_w2", "L1_attn_b2", "L1_ffn_controller", "L1_ffn_f1", "L1_ffn_f2", "L1_ffn_bias", "L1_c",
        "L1_wmod"]


def kernel(**inputs):
    import concourse.bacc as bacc
    from concourse.bass_utils import run_bass_kernel_spmd

    nc = bacc.Bacc("TRN2", target_bir_lowering=False, num_devices=1)
    arrays, args = {}, {}
    for name in _INS:
        arrays[name] = np.ascontiguousarray(inputs[name])
    arrays["tie"] = np.linspace(0.0, 1e-6, NE, dtype=np.float32)
    for name, a in arrays.items():
        args[name] = nc.dram_tensor("in_" + name, a.shape, mybir.dt.from_np(a.dtype), kind="ExternalInput").ap()
    out = nc.dram_tensor("out", (NB, S, D), F32, kind="ExternalOutput").ap()
    build(nc, args, out)
    r = run_bass_kernel_spmd(nc, [{"in_" + name: a for name, a in arrays.items()}], core_ids=[0])
    return r.results[0]["out"]
```
